# Optimizing a Trainium2 kernel written in Bass

```python
import numpy as np
import jax
import jax.numpy as jnp

def _softmax(x, axis=-1):
    return jax.nn.softmax(x, axis=axis)

def _gelu(x):
    return jax.nn.gelu(x, approximate=True)

def _silu(x):
    return jax.nn.silu(x)

def _sigmoid(x):
    return jax.nn.sigmoid(x)

def _layernorm(x, axis=-1, eps=1e-05):
    m = jnp.mean(x, axis=axis, keepdims=True)
    v = jnp.var(x, axis=axis, keepdims=True)
    return (x - m) / jnp.sqrt(v + eps)

def _scatter_add(tgt, idx, src, axis=0):
    return tgt.at[idx].add(src)

def _segment_sum(src, seg, n):
    return jax.ops.segment_sum(src, seg, n)
kernel_name = 'mk_hybrid_d1_jaxref_r4_85708f'

def setup_inputs(seed: int=0):
    np.random.seed(seed)
    _w = jnp.asarray

    def _L0_attn_a_setup():
        import jax, jax.numpy as jnp
        import numpy as np
        import math
        B, S, D = (2, 1024, 256)
        key = jax.random.key(seed)
        ks = jax.random.split(key, 8)
        s = 1.0 / math.sqrt(D)
        return {'x': jax.random.normal(ks[0], (B, S, D), dtype=jnp.float32), 'Wq': jax.random.normal(ks[1], (D, D), dtype=jnp.float32) * s, 'bq': jax.random.normal(ks[2], (D,), dtype=jnp.float32) * s, 'Wk': jax.random.normal(ks[3], (D, D), dtype=jnp.float32) * s, 'bk': jax.random.normal(ks[4], (D,), dtype=jnp.float32) * s, 'Wv': jax.random.normal(ks[5], (D, D), dtype=jnp.float32) * s, 'bv': jax.random.normal(ks[6], (D,), dtype=jnp.float32) * s, 'phase_bias': jnp.zeros((D,), dtype=jnp.float32)}
    _L0_attn_a_in = _L0_attn_a_setup()

    def _L0_attn_b_setup():
        import jax, jax.numpy as jnp
        import numpy as np
        from jax import lax
        B_, L, DM = (2, 512, 256)
        DI, N, K, R = (512, 16, 4, 64)
        EPS = 1e-05

        def _rmsnorm(x, w, eps=EPS):
            var = jnp.mean(x * x, axis=-1, keepdims=True)
            return x * lax.rsqrt(var + eps) * w

        def _causal_depthwise_conv(u, conv_w, conv_b):
            lhs = jnp.transpose(u, (0, 2, 1))
            lhs = jnp.pad(lhs, ((0, 0), (0, 0), (K - 1, 0)))
            rhs = conv_w[:, None, :]
            out = lax.conv_general_dilated(lhs, rhs, window_strides=(1,), padding='VALID', dimension_numbers=('NCH', 'OIH', 'NCH'), feature_group_count=DI)
            return jnp.transpose(out, (0, 2, 1)) + conv_b

        def _mamba_mixer(h, in_proj_w, conv_w, conv_b, x_proj_w, dt_proj_w, dt_proj_b, A_log, D, out_proj_w):
            xz = h @ in_proj_w
            u, z = jnp.split(xz, 2, axis=-1)
            u = jax.nn.silu(_causal_depthwise_conv(u, conv_w, conv_b))
            xdbl = u @ x_proj_w
            dt_r = xdbl[..., :R]
            Bm = xdbl[..., R:R + N]
            Cm = xdbl[..., R + N:]
            dt = jax.nn.softplus(dt_r @ dt_proj_w + dt_proj_b)
            A = -jnp.exp(A_log)

            def step(hst, inp):
                dt_t, B_t, C_t, u_t = inp
                dA = jnp.exp(dt_t[..., None] * A)
                dBu = dt_t[..., None] * B_t[:, None, :] * u_t[..., None]
                hst = dA * hst + dBu
                y = jnp.einsum('bdn,bn->bd', hst, C_t)
                return (hst, y)
            xs = (jnp.swapaxes(dt, 0, 1), jnp.swapaxes(Bm, 0, 1), jnp.swapaxes(Cm, 0, 1), jnp.swapaxes(u, 0, 1))
            h0 = jnp.zeros((u.shape[0], DI, N), dtype=u.dtype)
            _, ys = lax.scan(step, h0, xs)
            y = jnp.swapaxes(ys, 0, 1) + u * D
            y = y * jax.nn.silu(z)
            return y @ out_proj_w
        key = jax.random.key(seed)
        ks = jax.random.split(key, 12)
        w = lambda k, s: jax.random.normal(k, s, dtype=jnp.float32) * 0.02
        inp = {'x': jax.random.normal(ks[0], (B_, L, DM), dtype=jnp.float32), 'hormone_vectors': jax.random.normal(ks[1], (B_, 64), dtype=jnp.float32), 'norm_w': jnp.ones((DM,), dtype=jnp.float32), 'in_proj_w': w(ks[2], (DM, 2 * DI)), 'conv_w': w(ks[3], (DI, K)), 'conv_b': jnp.zeros((DI,), dtype=jnp.float32), 'x_proj_w': w(ks[4], (DI, R + 2 * N)), 'dt_proj_w': w(ks[5], (R, DI)), 'dt_proj_b': jax.random.uniform(ks[6], (DI,), dtype=jnp.float32, minval=-4.0, maxval=-2.0), 'A_log': jnp.log(jnp.broadcast_to(jnp.arange(1, N + 1, dtype=jnp.float32), (DI, N))), 'D': jnp.ones((DI,), dtype=jnp.float32), 'out_proj_w': w(ks[7], (DI, DM))}
        return inp
    _L0_attn_b_in = _L0_attn_b_setup()

    def _L0_ffn_setup():
        import jax, jax.numpy as jnp
        import numpy as np
        SL, BS, HS = (512, 4, 256)
        FF = 1024
        E, RANK, TOPK = (8, 64, 2)
        key = jax.random.key(seed)
        ks = jax.random.split(key, 7)
        s = 0.02
        return {'x': jax.random.normal(ks[0], (SL, BS, HS), jnp.float32), 'expert_weights': jax.random.uniform(ks[1], (SL * BS, TOPK), jnp.float32), 'expert_indices': jax.random.randint(ks[2], (SL * BS, TOPK), 0, E).astype(jnp.int32), 'w1_A': jax.random.normal(ks[3], (E * RANK, HS), jnp.float32) * s, 'w1_B': jax.random.normal(ks[4], (E * RANK, FF), jnp.float32) * s, 'w2_A': jax.random.normal(ks[5], (E * RANK, FF), jnp.float32) * s, 'w2_B': jax.random.normal(ks[6], (E * RANK, HS), jnp.float32) * s}
    _L0_ffn_in = _L0_ffn_setup()
    _d = {'L0_attn_a_x': _L0_attn_a_in['x'], 'L0_attn_a_Wq': _L0_attn_a_in['Wq'], 'L0_attn_a_bq': _L0_attn_a_in['bq'], 'L0_attn_a_Wk': _L0_attn_a_in['Wk'], 'L0_attn_a_bk': _L0_attn_a_in['bk'], 'L0_attn_a_Wv': _L0_attn_a_in['Wv'], 'L0_attn_a_bv': _L0_attn_a_in['bv'], 'L0_attn_a_phase_bias': _L0_attn_a_in['phase_bias'], 'L0_attn_b_hormone_vectors': _L0_attn_b_in['hormone_vectors'], 'L0_attn_b_norm_w': _L0_attn_b_in['norm_w'], 'L0_attn_b_in_proj_w': _L0_attn_b_in['in_proj_w'], 'L0_attn_b_conv_w': _L0_attn_b_in['conv_w'], 'L0_attn_b_conv_b': _L0_attn_b_in['conv_b'], 'L0_attn_b_x_proj_w': _L0_attn_b_in['x_proj_w'], 'L0_attn_b_dt_proj_w': _L0_attn_b_in['dt_proj_w'], 'L0_attn_b_dt_proj_b': _L0_attn_b_in['dt_proj_b'], 'L0_attn_b_A_log': _L0_attn_b_in['A_log'], 'L0_attn_b_D': _L0_attn_b_in['D'], 'L0_attn_b_out_proj_w': _L0_attn_b_in['out_proj_w'], 'L0_ffn_expert_weights': _L0_ffn_in['expert_weights'], 'L0_ffn_expert_indices': _L0_ffn_in['expert_indices'], 'L0_ffn_w1_A': _L0_ffn_in['w1_A'], 'L0_ffn_w1_B': _L0_ffn_in['w1_B'], 'L0_ffn_w2_A': _L0_ffn_in['w2_A'], 'L0_ffn_w2_B': _L0_ffn_in['w2_B']}
    _x0 = _d['L0_attn_a_x']
    _d['L0_attn_a_x'] = jax.random.normal(jax.random.fold_in(jax.random.key(seed), 1), (16, 512, 256), dtype=_x0.dtype)
    del _x0
    return _d

def reference(L0_attn_a_x, L0_attn_a_Wq, L0_attn_a_bq, L0_attn_a_Wk, L0_attn_a_bk, L0_attn_a_Wv, L0_attn_a_bv, L0_attn_a_phase_bias, L0_attn_b_hormone_vectors, L0_attn_b_norm_w, L0_attn_b_in_proj_w, L0_attn_b_conv_w, L0_attn_b_conv_b, L0_attn_b_x_proj_w, L0_attn_b_dt_proj_w, L0_attn_b_dt_proj_b, L0_attn_b_A_log, L0_attn_b_D, L0_attn_b_out_proj_w, L0_ffn_expert_weights, L0_ffn_expert_indices, L0_ffn_w1_A, L0_ffn_w1_B, L0_ffn_w2_A, L0_ffn_w2_B):

    def _L0_attn_a_ref(x, Wq, bq, Wk, bk, Wv, bv, phase_bias):
        import jax, jax.numpy as jnp
        import numpy as np
        import math
        B, S, D = (2, 1024, 256)
        d = x.shape[-1]
        wavelengths = jnp.arange(1, d + 1, dtype=jnp.float32) * (2.0 * math.pi / d)
        inv_wl = 1.0 / (wavelengths + 1e-08)
        Q = jnp.einsum('bsd,ed->bse', x, Wq) + bq
        K = jnp.einsum('bsd,ed->bse', x, Wk) + bk
        V = jnp.einsum('bsd,ed->bse', x, Wv) + bv
        theta_q = Q * inv_wl + phase_bias
        theta_k = K * inv_wl + phase_bias
        sim = jnp.einsum('bsd,btd->bst', jnp.cos(theta_q), jnp.cos(theta_k)) + jnp.einsum('bsd,btd->bst', jnp.sin(theta_q), jnp.sin(theta_k))
        weights = jax.nn.softmax(sim / math.sqrt(d), axis=-1)
        return jnp.einsum('bst,btd->bsd', weights, V)

    def _L0_attn_b_ref(x, hormone_vectors, norm_w, in_proj_w, conv_w, conv_b, x_proj_w, dt_proj_w, dt_proj_b, A_log, D, out_proj_w):
        import jax, jax.numpy as jnp
        import numpy as np
        from jax import lax
        B_, L, DM = (2, 512, 256)
        DI, N, K, R = (512, 16, 4, 64)
        EPS = 1e-05

        def _rmsnorm(x, w, eps=EPS):
            var = jnp.mean(x * x, axis=-1, keepdims=True)
            return x * lax.rsqrt(var + eps) * w

        def _causal_depthwise_conv(u, conv_w, conv_b):
            lhs = jnp.transpose(u, (0, 2, 1))
            lhs = jnp.pad(lhs, ((0, 0), (0, 0), (K - 1, 0)))
            rhs = conv_w[:, None, :]
            out = lax.conv_general_dilated(lhs, rhs, window_strides=(1,), padding='VALID', dimension_numbers=('NCH', 'OIH', 'NCH'), feature_group_count=DI)
            return jnp.transpose(out, (0, 2, 1)) + conv_b

        def _mamba_mixer(h, in_proj_w, conv_w, conv_b, x_proj_w, dt_proj_w, dt_proj_b, A_log, D, out_proj_w):
            xz = h @ in_proj_w
            u, z = jnp.split(xz, 2, axis=-1)
            u = jax.nn.silu(_causal_depthwise_conv(u, conv_w, conv_b))
            xdbl = u @ x_proj_w
            dt_r = xdbl[..., :R]
            Bm = xdbl[..., R:R + N]
            Cm = xdbl[..., R + N:]
            dt = jax.nn.softplus(dt_r @ dt_proj_w + dt_proj_b)
            A = -jnp.exp(A_log)

            def step(hst, inp):
                dt_t, B_t, C_t, u_t = inp
                dA = jnp.exp(dt_t[..., None] * A)
                dBu = dt_t[..., None] * B_t[:, None, :] * u_t[..., None]
                hst = dA * hst + dBu
                y = jnp.einsum('bdn,bn->bd', hst, C_t)
                return (hst, y)
            xs = (jnp.swapaxes(dt, 0, 1), jnp.swapaxes(Bm, 0, 1), jnp.swapaxes(Cm, 0, 1), jnp.swapaxes(u, 0, 1))
            h0 = jnp.zeros((u.shape[0], DI, N), dtype=u.dtype)
            _, ys = lax.scan(step, h0, xs)
            y = jnp.swapaxes(ys, 0, 1) + u * D
            y = y * jax.nn.silu(z)
            return y @ out_proj_w
        del hormone_vectors
        h = _rmsnorm(x, norm_w)
        return x + _mamba_mixer(h, in_proj_w, conv_w, conv_b, x_proj_w, dt_proj_w, dt_proj_b, A_log, D, out_proj_w)

    def _L0_ffn_ref(x, expert_weights, expert_indices, w1_A, w1_B, w2_A, w2_B):
        import jax, jax.numpy as jnp
        import numpy as np
        SL, BS, HS = (512, 4, 256)
        FF = 1024
        E, RANK, TOPK = (8, 64, 2)
        sl, bs, hs = x.shape
        T = sl * bs
        top_k = expert_indices.shape[-1]
        flat_e = expert_indices.reshape(-1)
        flat_w = expert_weights.reshape(-1)
        order = jnp.argsort(flat_e, stable=True)
        bin_ids = flat_e[order]
        tok = order // top_k
        xr = x.reshape(T, hs)[tok]
        w1A = w1_A.reshape(E, RANK, hs)
        w1B = w1_B.reshape(E, RANK, FF)
        w2A = w2_A.reshape(E, RANK, FF)
        w2B = w2_B.reshape(E, RANK, hs)
        out = jnp.zeros_like(xr)
        for e in range(E):
            mask = (bin_ids == e).astype(xr.dtype)[:, None]
            h = jax.nn.gelu(xr @ w1A[e].T @ w1B[e], approximate=False)
            ye = h @ w2A[e].T @ w2B[e]
            out = out + mask * ye
        y = jnp.zeros((T, hs), xr.dtype).at[tok].add(flat_w[order][:, None] * out)
        return y.reshape(sl, bs, hs)
    x = L0_attn_a_x
    x = x + _L0_attn_a_ref(_layernorm(x, axis=-1), L0_attn_a_Wq, L0_attn_a_bq, L0_attn_a_Wk, L0_attn_a_bk, L0_attn_a_Wv, L0_attn_a_bv, L0_attn_a_phase_bias)
    x = x + _L0_ffn_ref(_layernorm(x, axis=-1), L0_ffn_expert_weights, L0_ffn_expert_indices, L0_ffn_w1_A, L0_ffn_w1_B, L0_ffn_w2_A, L0_ffn_w2_B)
    x = x + _L0_attn_b_ref(_layernorm(x, axis=-1), L0_attn_b_hormone_vectors, L0_attn_b_norm_w, L0_attn_b_in_proj_w, L0_attn_b_conv_w, L0_attn_b_conv_b, L0_attn_b_x_proj_w, L0_attn_b_dt_proj_w, L0_attn_b_dt_proj_b, L0_attn_b_A_log, L0_attn_b_D, L0_attn_b_out_proj_w)
    x = x + _L0_ffn_ref(_layernorm(x, axis=-1), L0_ffn_expert_weights, L0_ffn_expert_indices, L0_ffn_w1_A, L0_ffn_w1_B, L0_ffn_w2_A, L0_ffn_w2_B)
    return x

_drawn_inputs = setup_inputs


def setup_inputs(seed=0):
    import zlib

    import numpy as np

    out = dict(_drawn_inputs(seed))
    spreads = {'L0_attn_a_phase_bias': (0.0, 2.0),
     'L0_attn_b_norm_w': (1.0, 0.6),
     'L0_attn_b_conv_b': (0.0, 0.8),
     'L0_attn_b_D': (1.0, 0.6)}
    factors = {'L0_attn_a_Wq': 3.324,
     'L0_attn_a_bq': 31.794,
     'L0_attn_a_Wk': 3.159,
     'L0_attn_a_bk': 34.061,
     'L0_attn_b_in_proj_w': 8.0,
     'L0_attn_b_conv_w': 8.0,
     'L0_attn_b_x_proj_w': 8.0,
     'L0_attn_b_dt_proj_w': 8.0,
     'L0_attn_b_dt_proj_b': 8.0,
     'L0_attn_b_A_log': 8.0,
     'L0_attn_b_out_proj_w': 8.0,
     'L0_ffn_expert_weights': 8.0,
     'L0_ffn_w1_A': 8.0,
     'L0_ffn_w1_B': 8.0,
     'L0_ffn_w2_A': 8.0,
     'L0_ffn_w2_B': 8.0}
    for name, (base, spread) in spreads.items():
        noise = np.random.default_rng([zlib.crc32(name.encode()), seed]).standard_normal(out[name].shape)
        drawn = base * np.exp(spread * noise) if base else spread * noise
        out[name] = jnp.asarray(drawn.astype(out[name].dtype))
    for name, factor in factors.items():
        out[name] = (out[name] * factor).astype(out[name].dtype)
    return out
```

```python
import concourse.bass as bass
from concourse import mybir
from contextlib import ExitStack
import math
import numpy as np

F32 = mybir.dt.float32
I32 = mybir.dt.int32
ALU = mybir.AluOpType
ACT = mybir.ActivationFunctionType
P = 128
EPS = 1e-5


class Step:

    def __init__(self, base, j, items):
        self.base, self.j, self.items = base, j, items

    def has(self, o):
        return not isinstance(self.base, int) or 0 <= 2 * self.base + self.j + o < self.items

    def reuses(self, o):
        return not isinstance(self.base, int) or 2 * self.base + self.j + o >= 2

    def item(self, o):
        return 2 * self.base + (self.j + o)

    def half(self, o):
        return (self.j + o) % 2

    def turn(self, o):
        return self.base + (self.j + o) // 2


def run_steps(eng, emit, items, ahead, after=0):
    for s in range(-ahead, 2):
        emit(Step(s // 2, s % 2, items))
    pairs = (items - ahead) // 2
    with eng.Fori(1, pairs) as i:
        emit(Step(i, 0, items))
        emit(Step(i, 1, items))
    for s in range(2 * pairs, items + after):
        emit(Step(s // 2, s % 2, items))


def attention(nc, x, wqkT, wvT, bqk, bv, phase, inv_wl, ident, x1):
    NB, S, D = x.shape
    TT, KT = S // P, D // P
    NF = 2 * KT
    MAGIC = 1.5 * 2.0 ** 23
    C1 = 6.28125
    C2 = 2.0 * math.pi - C1
    PI_IN = 3.1415925
    with ExitStack() as ctx:
        def sb(name, shape, dt=F32):
            return ctx.enter_context(nc.sbuf_tensor("a_" + name, shape, dt))

        def sem(name):
            return ctx.enter_context(nc.semaphore("a_" + name))

        w_qk = sb("w_qk", [P, KT, 2 * D])
        w_v = sb("w_v", [P, KT, D])
        b_v = sb("b_v", [P, D])
        id_sb = sb("ident", [P, P])
        bqk_c = sb("bqk_c", [P, NF])
        wl_c = sb("wl_c", [P, NF])
        ph_c = sb("ph_c", [P, NF])
        shift = sb("shift", [P, NF])
        half_pi = sb("half_pi", [P, 1])
        neg_half = sb("neg_half", [P, TT])
        xin = [sb(f"xin{h}", [P, TT, D]) for h in range(2)]
        xn = [sb(f"xn{h}", [P, TT, D]) for h in range(2)]
        xT = [sb(f"xT{h}", [P, KT, S]) for h in range(2)]
        xres = [sb(f"xres{h}", [P, TT, D]) for h in range(2)]
        xout = [sb(f"xout{h}", [P, TT, D]) for h in range(2)]
        stats = sb("stats", [P, TT, 6])
        mv = [sb(f"mv{h}", [P, TT, 2]) for h in range(2)]
        var_eps = [sb(f"var_eps{h}", [P, TT]) for h in range(2)]
        rstd = [sb(f"rstd{h}", [P, TT]) for h in range(2)]
        theta = sb("theta", [P, NF, S])
        turns = sb("turns", [P, NF, S])
        rest = sb("rest", [P, NF, S])
        sin_in = sb("sin_in", [P, NF, S])
        cos_in = sb("cos_in", [P, NF, S])
        sin_f = [sb(f"sin_f{h}", [P, NF, S]) for h in range(2)]
        cos_f = [sb(f"cos_f{h}", [P, NF, S]) for h in range(2)]
        vals = [sb(f"vals{h}", [P, TT, D + 1]) for h in range(2)]
        probs = [sb(f"probs{h}", [P, TT, S]) for h in range(2)]
        rden = sb("rden", [P, TT])
        ps_t = [ctx.enter_context(nc.psum_tensor(f"a_ps_t{r}", [P, 512], F32)) for r in range(2)]
        ring = [ctx.enter_context(nc.psum_tensor(f"a_ring{r}", [P, 512], F32)) for r in range(2)]
        ps_s = [ctx.enter_context(nc.psum_tensor(f"a_ps_s{r}", [P, 512], F32)) for r in range(2)]
        ps_o = [ctx.enter_context(nc.psum_tensor(f"a_ps_o{r}", [P, 512], F32)) for r in range(2)]

        w_loaded = sem("w_loaded")
        consts_set = sem("consts_set")
        shift_set = sem("shift_set")
        xin_loaded = [sem(f"xin_loaded{h}") for h in range(2)]
        xres_loaded = [sem(f"xres_loaded{h}") for h in range(2)]
        mv_done = sem("mv_done")
        var_done = sem("var_done")
        rstd_done = sem("rstd_done")
        xn_ready = sem("xn_ready")
        xT_full = sem("xT_full")
        xT_copied = sem("xT_copied")
        ring_full = [sem(f"ring_full{r}") for r in range(2)]
        ring_free = [sem(f"ring_free{r}") for r in range(2)]
        reduced = sem("reduced")
        trig_in_used = sem("trig_in_used")
        sim_full = sem("sim_full")
        probs_ready = sem("probs_ready")
        out_full = [sem(f"out_full{r}") for r in range(2)]
        rden_done = sem("rden_done")
        out_free = [sem(f"out_free{r}") for r in range(2)]
        stored = [sem(f"stored{h}") for h in range(2)]

        def rows(t, b):
            return t[bass.ds(b, 1), :, :].rearrange("a (t p) d -> p (a t) d", p=P)

        block = ctx.enter_context(nc.Block())

        @block.sync
        def _(sp):
            sp.dma_start(id_sb[:, :], ident).then_inc(w_loaded, 16)
            sp.dma_start(w_qk[:, :, :], wqkT.rearrange("(k p) e -> p k e", p=P)).then_inc(w_loaded, 16)
            sp.dma_start(w_v[:, :, :], wvT.rearrange("(k p) e -> p k e", p=P)).then_inc(w_loaded, 16)
            sp.dma_start(b_v[:, :], bv.to_broadcast([P, D])).then_inc(w_loaded, 16)
            sp.dma_start(bqk_c[:, :], bqk).then_inc(w_loaded, 16)
            sp.dma_start(wl_c[:, :], inv_wl).then_inc(w_loaded, 16)
            sp.dma_start(ph_c[:, :], phase).then_inc(w_loaded, 16)

            def emit(st):
                if st.has(3):
                    h, n = st.half(3), st.turn(3)
                    if st.reuses(3):
                        sp.wait_ge(xn_ready, TT * (st.item(3) - 1))
                    sp.dma_start(xin[h][:, :, :], rows(x, st.item(3))).then_inc(xin_loaded[h], 16)
                if st.has(0):
                    h, n = st.half(0), st.turn(0)
                    if st.reuses(0):
                        sp.wait_ge(out_free[1], 2 * (st.item(0) - 1))
                    sp.dma_start(xres[h][:, :, :], rows(x, st.item(0))).then_inc(xres_loaded[h], 16)
                    for r in range(2):
                        sp.wait_ge(out_free[r], 2 * st.item(0) + 2)
                    sp.dma_start(rows(x1, st.item(0)), xout[h][:, :, :]).then_inc(stored[h], 16)

            run_steps(sp, emit, NB, 3)
            for h in range(2):
                sp.wait_ge(stored[h], 16 * (NB // 2))

        @block.gpsimd
        def _(pool):
            nc.gpsimd.memset(neg_half[:, :], -0.5).then_inc(consts_set, 1)
            pool.wait_ge(consts_set, 1)

            def emit(st):
                if st.has(3):
                    h = st.half(3)
                    pool.wait_ge(var_done, st.item(3) + 1)
                    nc.gpsimd.tensor_tensor(rstd[h][:, :], var_eps[h][:, :], neg_half[:, :],
                                            ALU.pow).then_inc(rstd_done, 1)

            run_steps(pool, emit, NB, 3)

        @block.vector
        def _(dve):
            nc.vector.memset(half_pi[:, :], math.pi / 2).then_inc(shift_set, 1)
            for h in range(2):
                nc.vector.memset(vals[h][:, :, D:D + 1], 1.0).then_inc(shift_set, 1)
            dve.wait_ge(w_loaded, 7 * 16)
            nc.vector.tensor_tensor(shift[:, :], bqk_c[:, :], wl_c[:, :], ALU.mult).then_inc(shift_set, 1)
            dve.wait_ge(shift_set, 4)
            nc.vector.tensor_tensor(shift[:, :], shift[:, :], ph_c[:, :], ALU.add).then_inc(shift_set, 1)

            def emit(st):
                if st.has(2):
                    h, n = st.half(2), st.turn(2)
                    b = st.item(2)
                    if st.reuses(2):
                        dve.wait_ge(ring_full[1], 3 * (b - 1))
                    for k in range(KT):
                        dve.wait_ge(xT_full, KT * b + k + 1)
                        nc.vector.tensor_copy(xT[h][:, k, :], ps_t[k][:, :]).then_inc(xT_copied, 1)
                if st.has(1):
                    h, n, b = st.half(1), st.turn(1), st.item(1)
                    if st.reuses(1):
                        dve.wait_ge(out_full[1], 2 * (b - 1))
                    for v in range(2):
                        dve.wait_ge(ring_full[v], 3 * b + 3)
                        nc.vector.tensor_tensor(vals[h][:, 2 * v:2 * v + 2, 0:D],
                                                ring[v][:, :].rearrange("p (t d) -> p t d", d=D),
                                                b_v[:, :].unsqueeze(1).to_broadcast([P, 2, D]),
                                                ALU.add).then_inc(ring_free[v], 1)
                    for r in range(2):
                        dve.wait_ge(ring_free[r], 3 * b + 2)
                    nc.vector.tensor_scalar(turns[:, :, :], theta[:, :, :], 1.0 / (2.0 * math.pi), MAGIC,
                                            ALU.mult, ALU.add).then_inc(reduced, 1)
                    dve.wait_ge(reduced, 5 * b + 1)
                    nc.vector.tensor_scalar(turns[:, :, :], turns[:, :, :], MAGIC, None,
                                            ALU.subtract).then_inc(reduced, 1)
                    dve.wait_ge(reduced, 5 * b + 2)
                    nc.vector.scalar_tensor_tensor(out=rest[:, :, :], in0=turns[:, :, :], scalar=-C1,
                                                   in1=theta[:, :, :], op0=ALU.mult,
                                                   op1=ALU.add).then_inc(reduced, 1)
                    dve.wait_ge(reduced, 5 * b + 3)
                    nc.vector.scalar_tensor_tensor(out=rest[:, :, :], in0=turns[:, :, :], scalar=-C2,
                                                   in1=rest[:, :, :], op0=ALU.mult,
                                                   op1=ALU.add).then_inc(reduced, 1)
                    dve.wait_ge(reduced, 5 * b + 4)
                    dve.wait_ge(trig_in_used, 3 * b)
                    nc.vector.tensor_scalar(sin_in[:, :, :], rest[:, :, :], -PI_IN, PI_IN,
                                            ALU.max, ALU.min).then_inc(reduced, 1)
                if st.has(3):
                    h, n, b = st.half(3), st.turn(3), st.item(3)
                    dve.wait_ge(xin_loaded[h], 16 * (n + 1))
                    for t in range(TT):
                        nc.vector.bn_stats(stats[:, t, :], xin[h][:, t, :])
                    dve.drain()
                    for t in range(TT):
                        ins = nc.vector.bn_aggr(mv[h][:, t, :], stats[:, t, :])
                    ins.then_inc(mv_done, 1)
                    dve.wait_ge(mv_done, b + 1)
                    nc.vector.tensor_scalar(var_eps[h][:, :], mv[h][:, :, 1], EPS, None,
                                            ALU.add).then_inc(var_done, 1)
                if st.has(0):
                    h, n, b = st.half(0), st.turn(0), st.item(0)
                    dve.wait_ge(xres_loaded[h], 16 * (n + 1))
                    if st.reuses(0):
                        dve.wait_ge(stored[h], 16 * n)
                    for t in range(TT):
                        r = t % 2
                        dve.wait_ge(out_full[r], 2 * b + t // 2 + 1)
                        nc.vector.reciprocal(rden[:, t:t + 1], ps_o[r][:, D:D + 1]).then_inc(rden_done, 1)
                        dve.wait_ge(rden_done, TT * b + t + 1)
                        ins = nc.vector.scalar_tensor_tensor(out=xout[h][:, t, :], in0=ps_o[r][:, 0:D],
                                                             scalar=rden[:, t:t + 1], in1=xres[h][:, t, :],
                                                             op0=ALU.mult, op1=ALU.add)
                        ins.then_inc(out_free[r], 1)
                if st.has(3):
                    h, n, b = st.half(3), st.turn(3), st.item(3)
                    dve.wait_ge(rstd_done, b + 1)
                    if st.reuses(3):
                        dve.wait_ge(xT_full, KT * (b - 1))
                    for t in range(TT):
                        ins = nc.vector.tensor_scalar(xn[h][:, t, :], xin[h][:, t, :], mv[h][:, t, 0:1],
                                                      rstd[h][:, t:t + 1], ALU.subtract, ALU.mult)
                        ins.then_inc(xn_ready, 1)

            run_steps(dve, emit, NB, 3)

        @block.scalar
        def _(act):
            act.wait_ge(shift_set, 5)

            def emit(st):
                if st.has(1):
                    b = st.item(1)
                    act.wait_ge(reduced, 5 * b)
                    for f in range(NF):
                        r = f % 2
                        act.wait_ge(ring_full[r], 3 * b + f // 2 + 1)
                        nc.scalar.activation(theta[:, f, :], ring[r][:, :], ACT.Identity,
                                             bias=shift[:, f:f + 1], scale=wl_c[:, f:f + 1])\
                            .then_inc(ring_free[r], 1)
                if st.has(0):
                    h, n, b = st.half(0), st.turn(0), st.item(0)
                    if st.reuses(0):
                        act.wait_ge(out_full[1], 2 * (b - 1))
                    for t in range(TT):
                        act.wait_ge(sim_full, TT * b + t + 1)
                        nc.scalar.activation(probs[h][:, t, :], ps_s[t % 2][:, :], ACT.Exp,
                                             scale=1.0 / math.sqrt(D)).then_inc(probs_ready, 1)
                if st.has(1):
                    h, n, b = st.half(1), st.turn(1), st.item(1)
                    if st.reuses(1):
                        act.wait_ge(sim_full, TT * (b - 1))
                    act.wait_ge(reduced, 5 * b + 5)
                    nc.scalar.activation(sin_f[h][:, :, :], sin_in[:, :, :], ACT.Sin).then_inc(trig_in_used, 1)
                    nc.scalar.activation(cos_in[:, :, :], sin_in[:, :, :], ACT.Abs).then_inc(trig_in_used, 1)
                    act.wait_ge(trig_in_used, 3 * b + 2)
                    nc.scalar.activation(cos_f[h][:, :, :], cos_in[:, :, :], ACT.Sin, bias=half_pi[:, 0:1],
                                         scale=-1.0).then_inc(trig_in_used, 1)

            run_steps(act, emit, NB, 3)

        @block.tensor
        def _(pe):
            pe.wait_ge(w_loaded, 7 * 16)

            def take(st, use):
                r = use % 2
                pe.wait_ge(ring_free[r], 3 * st.item(1) + use // 2)
                return r

            def emit(st):
                if st.has(2):
                    h, b = st.half(2), st.item(2)
                    pe.wait_ge(xn_ready, TT * (b + 1))
                    for k in range(KT):
                        if st.has(1):
                            pe.wait_ge(xT_copied, KT * (b - 1) + k + 1)
                        for t in range(TT):
                            ins = nc.tensor.transpose(ps_t[k][:, t * P:(t + 1) * P],
                                                      xn[h][:, t, k * P:(k + 1) * P], id_sb[:, :])
                        ins.then_inc(xT_full, 1)
                if st.has(1):
                    h, b = st.half(1), st.item(1)
                    pe.wait_ge(xT_copied, KT * (b + 1))
                    for f in range(NF):
                        r = take(st, f)
                        for k in range(KT):
                            ins = nc.tensor.matmul(ring[r][:, :], w_qk[:, k, f * P:(f + 1) * P], xT[h][:, k, :],
                                                   start=(k == 0), stop=(k == KT - 1))
                        ins.then_inc(ring_full[r], 1)
                    for v in range(2):
                        r = take(st, NF + v)
                        for u in range(2):
                            t = 2 * v + u
                            for k in range(KT):
                                ins = nc.tensor.matmul(ring[r][:, u * D:(u + 1) * D],
                                                       xT[h][:, k, t * P:(t + 1) * P], w_v[:, k, :],
                                                       start=(k == 0), stop=(k == KT - 1))
                        ins.then_inc(ring_full[r], 1)
                if st.has(0):
                    h, n, b = st.half(0), st.turn(0), st.item(0)
                    pe.wait_ge(trig_in_used, 3 * b + 3)
                    for t in range(TT):
                        if t >= 2:
                            pe.wait_ge(probs_ready, TT * b + t - 1)
                        for m, feats in enumerate((cos_f[h], sin_f[h])):
                            for k in range(KT):
                                ins = nc.tensor.matmul(ps_s[t % 2][:, :], feats[:, KT + k, t * P:(t + 1) * P],
                                                       feats[:, k, :], start=(m == 0 and k == 0),
                                                       stop=(m == 1 and k == KT - 1))
                        ins.then_inc(sim_full, 1)
                    pe.wait_ge(probs_ready, TT * (b + 1))
                    for r in range(2):
                        pe.wait_ge(ring_free[r], 3 * b + 3)
                    for s in range(TT):
                        r = s % 2
                        pe.wait_ge(out_free[r], 2 * b + s // 2)
                        for t in range(TT):
                            ins = nc.tensor.matmul(ps_o[r][:, 0:D + 1], probs[h][:, t, s * P:(s + 1) * P],
                                                   vals[h][:, t, :], start=(t == 0), stop=(t == TT - 1))
                        ins.then_inc(out_full[r], 1)

            run_steps(pe, emit, NB, 3)



def expert_ffn(nc, tag, x, weights, indices, experts, w1aT, w1b, w2aT, w2b, ident):
    D = x.shape[2]
    TOK, TOPK = weights.shape
    ER, FF = w1b.shape
    E = experts.shape[1]
    R = ER // E
    GRP = 512
    NG, TT, KT = TOK // GRP, GRP // P, D // P
    PAIRS, FT = ER // P, FF // P
    NT = TOK // P
    UPS = PAIRS * FT
    UB = 3
    xf = x.rearrange("b s d -> (b s) d")
    with ExitStack() as ctx:
        def sb(name, shape, dt=F32):
            return ctx.enter_context(nc.sbuf_tensor(tag + name, shape, dt))

        def sem(name):
            return ctx.enter_context(nc.semaphore(tag + name))

        x_all = sb("x_all", [P, NT, D])
        a_all = sb("a_all", [P, PAIRS, TOK])
        gate_all = sb("gate_all", [P, PAIRS, TOK])
        w_1a = sb("w_1a", [P, KT, ER])
        w_1b = sb("w_1b", [P, PAIRS, FF])
        w_2a = sb("w_2a", [P, FT, ER])
        w_2b = sb("w_2b", [P, PAIRS, D])
        id_sb = sb("ident", [P, P])
        ex_sb = sb("experts", [P, E])
        g_w = sb("g_w", [P, NT, TOPK])
        g_i = sb("g_i", [P, NT, TOPK], I32)
        g_f = sb("g_f", [P, NT, TOPK])
        hit = [sb(f"hit{k}", [P, NT, E]) for k in range(TOPK)]
        gate = sb("gate", [P, NT, E])
        gate_x = sb("gate_x", [P, TT, E, R])
        stats = sb("stats", [P, NT, 6])
        mv = sb("mv", [P, NT, 2])
        var_eps = sb("var_eps", [P, NT])
        neg_half = sb("neg_half", [P, NT])
        rstd = sb("rstd", [P, NT])
        xn = sb("xn", [P, TT, D])
        xT = sb("xT", [P, KT, GRP])
        a_cur = sb("a_cur", [P, PAIRS, GRP])
        hid = [sb(f"hid{u}", [P, 2, GRP]) for u in range(UB)]
        c_sb = sb("c_sb", [P, PAIRS, GRP])
        x_new = sb("x_new", [P, TT, D])
        ps_up = [ctx.enter_context(nc.psum_tensor(f"{tag}ps_up{u}", [P, 2, 512], F32)) for u in range(UB)]
        ps_c = ctx.enter_context(nc.psum_tensor(tag + "ps_c", [P, 512], F32))
        ps_y = ctx.enter_context(nc.psum_tensor(tag + "ps_y", [P, 512], F32))
        T_BANK = [ps_up[0][:, k, :] for k in range(KT)]
        A_BANK = [ps_up[1 + p // 2][:, p % 2, :] for p in range(PAIRS)]
        Y_BANK = [ps_y[:, 0:D], ps_c[:, 0:D]]
        G_BANK = [ps_c[:, :], ps_y[:, :], T_BANK[0], T_BANK[1]]

        x_loaded = sem("x_loaded")
        w_loaded = sem("w_loaded")
        w2_loaded = sem("w2_loaded")
        half_set = sem("half_set")
        mv_done = sem("mv_done")
        var_done = sem("var_done")
        rstd_done = sem("rstd_done")
        gate_steps = sem("gate_steps")
        xn_ready = sem("xn_ready")
        gate_x_ready = sem("gate_x_ready")
        xT_full = sem("xT_full")
        xT_ready = sem("xT_ready")
        a_full = sem("a_full")
        a_copied = sem("a_copied")
        gate_full = sem("gate_full")
        gate_copied = sem("gate_copied")
        a_cur_ready = sem("a_cur_ready")
        up_done = sem("up_done")
        gelu_done = sem("gelu_done")
        down_done = sem("down_done")
        c_ready = sem("c_ready")
        y_full = sem("y_full")
        y_ready = sem("y_ready")
        stored = sem("stored")

        block = ctx.enter_context(nc.Block())

        @block.sync
        def _(sp):
            for g in range(NG):
                sp.dma_start(x_all[:, g * TT:(g + 1) * TT, :],
                             xf[g * GRP:(g + 1) * GRP, :].rearrange("(t p) d -> p t d", p=P)).then_inc(x_loaded, 16)
            sp.dma_start(g_w[:, :, :], weights.rearrange("(t p) k -> p t k", p=P)).then_inc(w_loaded, 16)
            sp.dma_start(g_i[:, :, :], indices.rearrange("(t p) k -> p t k", p=P)).then_inc(w_loaded, 16)
            sp.dma_start(ex_sb[:, :], experts).then_inc(w_loaded, 16)
            sp.dma_start(id_sb[:, :], ident).then_inc(w_loaded, 16)
            sp.dma_start(w_1a[:, :, :], w1aT.rearrange("(k p) e -> p k e", p=P)).then_inc(w_loaded, 16)
            sp.dma_start(w_1b[:, :, :], w1b.rearrange("(q p) f -> p q f", p=P)).then_inc(w2_loaded, 16)
            sp.dma_start(w_2a[:, :, :], w2aT.rearrange("(q p) e -> p q e", p=P)).then_inc(w2_loaded, 16)
            sp.dma_start(w_2b[:, :, :], w2b.rearrange("(q p) d -> p q d", p=P)).then_inc(w2_loaded, 16)
            with sp.Fori(0, NG) as g:
                sp.wait_ge(y_ready, TT * g + TT + 2)
                sp.dma_start(xf[bass.ds(g * GRP, GRP), :].rearrange("(t p) d -> p t d", p=P),
                             x_new[:, :, :]).then_inc(stored, 16)
            sp.wait_ge(stored, 16 * NG + 16)

        @block.gpsimd
        def _(pool):
            nc.gpsimd.memset(neg_half[:, :], -0.5).then_inc(half_set, 1)
            pool.wait_ge(half_set, 1)
            pool.wait_ge(var_done, 1)
            nc.gpsimd.tensor_tensor(rstd[:, :], var_eps[:, :], neg_half[:, :], ALU.pow).then_inc(rstd_done, 1)

        @block.vector
        def _(dve):
            dve.sem_inc(gelu_done, UB)
            dve.sem_inc(down_done, UB)
            dve.sem_inc(c_ready, 1)
            dve.sem_inc(y_ready, 2)
            dve.sem_inc(stored, 16)
            dve.wait_ge(x_loaded, 16 * NG)
            for t in range(NT):
                nc.vector.bn_stats(stats[:, t, :], x_all[:, t, :])
            dve.drain()
            for t in range(NT):
                ins = nc.vector.bn_aggr(mv[:, t, :], stats[:, t, :])
            ins.then_inc(mv_done, 1)
            dve.wait_ge(mv_done, 1)
            nc.vector.tensor_scalar(var_eps[:, :], mv[:, :, 1], EPS, None, ALU.add).then_inc(var_done, 1)
            dve.wait_ge(w_loaded, 5 * 16)
            nc.vector.tensor_copy(g_f[:, :, :], g_i[:, :, :]).then_inc(gate_steps, 1)
            dve.wait_ge(gate_steps, 1)
            for k in range(TOPK):
                nc.vector.tensor_tensor(hit[k][:, :, :], ex_sb[:, :].unsqueeze(1).to_broadcast([P, NT, E]),
                                        g_f[:, :, k:k + 1].to_broadcast([P, NT, E]),
                                        ALU.is_equal).then_inc(gate_steps, 1)
            dve.wait_ge(gate_steps, 1 + TOPK)
            for k in range(TOPK):
                nc.vector.tensor_tensor(hit[k][:, :, :], hit[k][:, :, :],
                                        g_w[:, :, k:k + 1].to_broadcast([P, NT, E]),
                                        ALU.mult).then_inc(gate_steps, 1)
            dve.wait_ge(gate_steps, 1 + 2 * TOPK)
            nc.vector.tensor_tensor(gate[:, :, :], hit[0][:, :, :], hit[1][:, :, :],
                                    ALU.add).then_inc(gate_steps, 1)
            dve.wait_ge(gate_steps, 2 + 2 * TOPK)
            dve.wait_ge(rstd_done, 1)
            for g in range(NG):
                if g:
                    dve.wait_ge(xT_full, g)
                    dve.wait_ge(gate_full, PAIRS * g)
                for t in range(TT):
                    n = g * TT + t
                    ins = nc.vector.tensor_scalar(xn[:, t, :], x_all[:, n, :], mv[:, n, 0:1], rstd[:, n:n + 1],
                                                  ALU.subtract, ALU.mult)
                ins.then_inc(xn_ready, 1)
                nc.vector.tensor_copy(gate_x[:, :, :, :], gate[:, g * TT:(g + 1) * TT, :].unsqueeze(3)
                                      .to_broadcast([P, TT, E, R])).then_inc(gate_x_ready, 1)
            dve.wait_ge(a_copied, PAIRS * NG)
            dve.wait_ge(gate_copied, PAIRS * NG)
            with dve.Fori(0, NG) as g:
                dve.wait_ge(up_done, UPS * g + UPS)
                nc.vector.tensor_copy(a_cur[:, :, :], a_all[:, :, bass.ds(g * GRP, GRP)]).then_inc(a_cur_ready, 1)
                for p in range(PAIRS):
                    dve.wait_ge(down_done, UPS * g + FT * (p + 1) + UB)
                    if p == 0:
                        dve.wait_ge(y_full, TT * g + TT)
                    nc.vector.tensor_tensor(c_sb[:, p, :], ps_c[:, :], gate_all[:, p, bass.ds(g * GRP, GRP)],
                                            ALU.mult).then_inc(c_ready, 1)
                dve.wait_ge(stored, 16 * g + 16)
                for t in range(TT):
                    dve.wait_ge(y_full, TT * g + t + 1 + TT)
                    nc.vector.tensor_tensor(x_new[:, t, :], Y_BANK[t % 2],
                                            x_all[:, bass.ds(g * TT + t, 1), :].rearrange("p a d -> p (a d)"),
                                            ALU.add).then_inc(y_ready, 1)

        @block.scalar
        def _(act):
            for g in range(NG):
                act.wait_ge(xT_full, g + 1)
                for k in range(KT):
                    nc.scalar.activation(xT[:, k, :], T_BANK[k], ACT.Copy).then_inc(xT_ready, 1)
                for p in range(PAIRS):
                    if p == 2:
                        for q in range(PAIRS):
                            act.wait_ge(a_full, PAIRS * g + q + 1)
                            nc.scalar.activation(a_all[:, q, g * GRP:(g + 1) * GRP], A_BANK[q],
                                                 ACT.Copy).then_inc(a_copied, 1)
                    act.wait_ge(gate_full, PAIRS * g + p + 1)
                    nc.scalar.activation(gate_all[:, p, g * GRP:(g + 1) * GRP], G_BANK[p],
                                         ACT.Copy).then_inc(gate_copied, 1)
            with act.Fori(0, NG) as g:
                for k in range(UPS):
                    u = k % UB
                    act.wait_ge(up_done, UPS * g + k + 1 + UPS)
                    act.wait_ge(down_done, UPS * g + k + 1)
                    nc.scalar.activation(hid[u][:, :, :], ps_up[u][:, :, :], ACT.Gelu).then_inc(gelu_done, 1)

        @block.tensor
        def _(pe):
            pe.wait_ge(w_loaded, 5 * 16)
            pe.sem_inc(up_done, UPS)
            pe.sem_inc(y_full, TT)

            def spread_gates(g, p):
                if g:
                    pe.wait_ge(gate_copied, PAIRS * (g - 1) + p + 1)
                for t in range(TT):
                    ins = nc.tensor.matmul(G_BANK[p][:, t * P:(t + 1) * P],
                                           gate_x[:, t, 2 * p:2 * p + 2, :].rearrange("p e r -> p (e r)"),
                                           id_sb[:, :], start=True, stop=True)
                ins.then_inc(gate_full, 1)

            for g in range(NG):
                pe.wait_ge(xn_ready, g + 1)
                if g:
                    pe.wait_ge(gate_copied, PAIRS * g)
                for k in range(KT):
                    for t in range(TT):
                        ins = nc.tensor.transpose(T_BANK[k][:, t * P:(t + 1) * P], xn[:, t, k * P:(k + 1) * P],
                                                  id_sb[:, :])
                ins.then_inc(xT_full, 1)
                pe.wait_ge(gate_x_ready, g + 1)
                for p in range(2):
                    spread_gates(g, p)
                pe.wait_ge(xT_ready, KT * (g + 1))
                for p in range(PAIRS):
                    if g:
                        pe.wait_ge(a_copied, PAIRS * (g - 1) + p + 1)
                    for k in range(KT):
                        ins = nc.tensor.matmul(A_BANK[p], w_1a[:, k, p * P:(p + 1) * P], xT[:, k, :],
                                               start=(k == 0), stop=(k == KT - 1))
                    ins.then_inc(a_full, 1)
                for p in range(2, PAIRS):
                    spread_gates(g, p)
            pe.wait_ge(a_copied, PAIRS * NG)
            pe.wait_ge(gate_copied, PAIRS * NG)
            pe.wait_ge(w2_loaded, 3 * 16)

            def up(g, k):
                p, f, u = k // FT, k % FT, k % UB
                pe.wait_ge(gelu_done, UPS * g + k + 1)
                for e in range(2):
                    rows = slice(e * R, (e + 1) * R)
                    ins = nc.tensor.matmul(ps_up[u][:, e, :], w_1b[rows, p, f * P:(f + 1) * P], a_cur[rows, p, :],
                                           start=True, stop=True)
                ins.then_inc(up_done, 1)

            def down(g, k):
                p, f, u = k // FT, k % FT, k % UB
                pe.wait_ge(gelu_done, UPS * g + k + 1 + UB)
                if f == 0:
                    pe.wait_ge(c_ready, PAIRS * g + p + 1)
                    if p == 0:
                        pe.wait_ge(y_ready, TT * g + 2)
                for e in range(2):
                    cols = slice(p * P + e * R, p * P + (e + 1) * R)
                    ins = nc.tensor.matmul(ps_c[e * R:(e + 1) * R, :], w_2a[:, f, cols], hid[u][:, e, :],
                                           start=(f == 0), stop=(f == FT - 1), skip_group_check=True)
                ins.then_inc(down_done, 1)

            with pe.Fori(0, NG) as g:
                pe.wait_ge(a_cur_ready, g + 1)
                up(g, 0)
                up(g, 1)
                for k in range(UPS):
                    if k + 2 < UPS:
                        up(g, k + 2)
                    down(g, k)
                pe.wait_ge(c_ready, PAIRS * (g + 1) + 1)
                for t in range(TT):
                    pe.wait_ge(y_ready, TT * g + t + 1)
                    for p in range(PAIRS):
                        ins = nc.tensor.matmul(Y_BANK[t % 2], c_sb[:, p, t * P:(t + 1) * P],
                                               w_2b[:, p, :], start=(p == 0), stop=(p == PAIRS - 1))
                    ins.then_inc(y_full, 1)



def mamba(nc, x_in, out, w_in, conv_w, conv_b, norm_w, w_x, w_dt, b_dt, a_log, d_skip, w_out,
          pick_block, pick_bc, sum_n, ident):
    NB, S, D = x_in.shape
    DI = w_out.shape[0]
    K = conv_w.shape[2]
    R = w_dt.shape[0]
    RX = w_x.shape[1]
    N = (RX - R) // 2
    TT, KT, CT = S // P, D // P, DI // P
    CH = 32
    Q = P // CH
    G = N // Q
    BLK = DI // CH
    BPT = BLK // CT
    PAD = K - 1
    RING = 4
    F_T, F_U, F_Z = 0, KT, KT + CT
    F_X = F_Z + CT
    F_DT = F_X + 1
    F_BC = F_DT + CT
    F_ALL = F_BC + 2 * G
    F_PER = [(F_ALL + 1) // 2, F_ALL // 2]
    with ExitStack() as ctx:
        def sb(name, shape, dt=F32):
            return ctx.enter_context(nc.sbuf_tensor("m_" + name, shape, dt))

        def sem(name):
            return ctx.enter_context(nc.semaphore("m_" + name))

        def bank(name):
            return ctx.enter_context(nc.psum_tensor("m_" + name, [P, 512], F32))

        win = sb("win", [P, KT, 2 * DI])
        wx = sb("wx", [P, CT, RX])
        wdt = sb("wdt", [RX, DI])
        wout = sb("wout", [P, CT, D])
        cw = sb("cw", [P, CT, K])
        cb = sb("cb", [P, CT])
        nw = sb("nw", [P, KT])
        bdt = sb("bdt", [P, CT])
        dsk = sb("dsk", [P, CT])
        nega = sb("nega", [P, BLK, G])
        pick_b = sb("pick_b", [P, BPT, P])
        pick_s = sb("pick_s", [RX, 2 * G, P])
        sum_q = sb("sum_q", [P, CH])
        id_sb = sb("ident", [P, P])
        neg_half = sb("neg_half", [P, TT])
        xin = sb("xin", [P, TT, D])
        xl = sb("xl", [P, TT, D])
        res_in = sb("res_in", [P, TT, D])
        x_new = sb("x_new", [P, TT, D])
        stats = sb("stats", [P, TT, 6])
        mv = sb("mv", [P, TT, 2])
        var_eps = sb("var_eps", [P, TT])
        rstd = sb("rstd", [P, TT])
        ms_eps = sb("ms_eps", [P, TT])
        rrms = sb("rrms", [P, TT])
        hT = sb("hT", [P, KT, S])
        fr1 = sb("fr1", [P, 2, PAD + S])
        fr2 = sb("fr2", [P, 2, S])
        fr3 = sb("fr3", [P, 2, S])
        xd = sb("xd", [RX, S])
        dt_sb = [sb(f"dt{h}", [P, CT, S]) for h in range(2)]
        du_sb = [sb(f"du{h}", [P, CT, S]) for h in range(2)]
        u_sb = [sb(f"u{h}", [P, CT, S]) for h in range(2)]
        z_sb = [sb(f"z{h}", [P, CT, S]) for h in range(2)]
        bc_sb = [sb(f"bc{h}", [P, 2 * G, S]) for h in range(2)]
        decay = [sb(f"decay{r}", [P, G, S]) for r in range(2)]
        state = [sb(f"state{r}", [P, G, S]) for r in range(RING)]
        ps_dt = [bank(f"ps_dt{r}") for r in range(2)]
        ps_du = [bank(f"ps_du{r}") for r in range(2)]
        ps_y = [bank(f"ps_y{r}") for r in range(2)]
        ps_f = [bank(f"ps_f{r}") for r in range(2)]

        w_loaded = sem("w_loaded")
        a_ready = sem("a_ready")
        scaled = sem("scaled")
        half_set = sem("half_set")
        xin_loaded = sem("xin_loaded")
        mv_done = sem("mv_done")
        var_done = sem("var_done")
        rstd_done = sem("rstd_done")
        ms_done = sem("ms_done")
        rrms_done = sem("rrms_done")
        xl_ready = sem("xl_ready")
        res_ready = sem("res_ready")
        res_stored = sem("res_stored")
        xh_ready = sem("xh_ready")
        f_full = [sem(f"f_full{r}") for r in range(2)]
        f_free = [sem(f"f_free{r}") for r in range(2)]
        hT_ready = sem("hT_ready")
        taps = sem("taps")
        conv_done = sem("conv_done")
        u_tanh = sem("u_tanh")
        u_ready = sem("u_ready")
        z_tanh = sem("z_tanh")
        z_ready = sem("z_ready")
        xd_ready = sem("xd_ready")
        sp_in = sem("sp_in")
        sp_exp = sem("sp_exp")
        sp_ln = sem("sp_ln")
        sp_steps = sem("sp_steps")
        dt_ready = sem("dt_ready")
        bc_ready = sem("bc_ready")
        rep_done = sem("rep_done")
        decay_ready = sem("decay_ready")
        drive_ready = sem("drive_ready")
        scanned = sem("scanned")
        weighed = sem("weighed")
        summed = sem("summed")
        y_read = sem("y_read")
        y_skip = sem("y_skip")
        gated = sem("gated")
        o_full = sem("o_full")
        o_read = sem("o_read")
        res_back = sem("res_back")
        stored = sem("stored")
        NW = 15

        def rows(t, b):
            return t[bass.ds(b, 1), :, :].rearrange("a (t p) d -> p (a t) d", p=P)

        def f_count(b, use):
            return F_PER[use % 2] * b + use // 2 + 1

        def f_read(b, use):
            return [(F_BC + 1) // 2, F_BC // 2][use % 2] * b + use // 2 + 1

        block = ctx.enter_context(nc.Block())

        @block.sync
        def _(sp):
            for dst, src in ((id_sb[:, :], ident), (win[:, :, :], w_in.rearrange("(k p) e -> p k e", p=P)),
                             (wx[:, :, :], w_x.rearrange("(k p) e -> p k e", p=P)),
                             (wdt[0:R, :], w_dt), (wout[:, :, :], w_out.rearrange("(k p) e -> p k e", p=P)),
                             (cw[:, :, :], conv_w), (cb[:, :], conv_b), (nw[:, :], norm_w), (bdt[:, :], b_dt),
                             (dsk[:, :], d_skip), (nega[:, :, :], a_log), (pick_b[:, :, :], pick_block),
                             (pick_s[:, :, :], pick_bc), (sum_q[:, :], sum_n)):
                sp.dma_start(dst, src).then_inc(w_loaded, 16)

            def emit(st):
                if st.has(-1):
                    b = st.item(-1)
                    sp.wait_ge(res_stored, 16 * (b + 1))
                    sp.dma_start(res_in[:, :, :], rows(out, b)).then_inc(res_back, 16)
                    sp.wait_ge(o_read, 2 * (b + 1))
                    sp.dma_start(rows(out, b), x_new[:, :, :]).then_inc(stored, 16)
                if st.has(2):
                    b = st.item(2)
                    if st.has(1):
                        sp.wait_ge(res_stored, 16 * b)
                    sp.dma_start(xin[:, :, :], rows(x_in, b)).then_inc(xin_loaded, 16)
                    sp.wait_ge(res_ready, b + 1)
                    sp.dma_start(rows(out, b), xin[:, :, :]).then_inc(res_stored, 16)

            run_steps(sp, emit, NB, 2, 1)
            sp.wait_ge(stored, 16 * NB)

        @block.gpsimd
        def _(pool):
            nc.gpsimd.memset(neg_half[:, :], -0.5).then_inc(half_set, 1)
            pool.wait_ge(half_set, 1)

            def emit(st):
                for q in range(BLK):
                    if st.has(0):
                        h, b = st.half(0), st.item(0)
                        c = BLK * b + q
                        pool.wait_ge(scanned, c + 1)
                        if q == 0:
                            pool.wait_ge(bc_ready, 2 * G * (b + 1))
                        s = state[q % RING]
                        nc.gpsimd.tensor_tensor(s[:, :, :], s[:, :, :], bc_sb[h][:, G:2 * G, :],
                                                ALU.mult).then_inc(weighed, 1)
                    if st.has(2) and q == 12:
                        pool.wait_ge(var_done, st.item(2) + 1)
                        nc.gpsimd.tensor_tensor(rstd[:, :], var_eps[:, :], neg_half[:, :],
                                                ALU.pow).then_inc(rstd_done, 1)
                    if st.has(2) and q == 13:
                        pool.wait_ge(ms_done, 3 * (st.item(2) + 1))
                        nc.gpsimd.tensor_tensor(rrms[:, :], ms_eps[:, :], neg_half[:, :],
                                                ALU.pow).then_inc(rrms_done, 1)

            run_steps(pool, emit, NB, 2, 1)

        @block.vector
        def _(dve):
            dve.wait_ge(w_loaded, 16 * 14)
            nc.vector.memset(wdt[R:RX, :], 0.0).then_inc(scaled, 1)
            nc.vector.memset(fr1[:, :, 0:PAD], 0.0).then_inc(scaled, 1)
            for r in range(2):
                nc.vector.memset(decay[r][:, :, 0:1], 0.0).then_inc(scaled, 1)
            nc.vector.tensor_scalar(cw[:, :, :], cw[:, :, :], 0.5, None, ALU.mult).then_inc(scaled, 1)
            nc.vector.tensor_scalar(cb[:, :], cb[:, :], 0.5, None, ALU.mult).then_inc(scaled, 1)
            nc.vector.tensor_scalar(win[:, :, DI:2 * DI], win[:, :, DI:2 * DI], 0.5, None,
                                    ALU.mult).then_inc(scaled, 1)
            dve.wait_ge(a_ready, 1)
            nc.vector.tensor_scalar(nega[:, :, :], nega[:, :, :], -1.0, None, ALU.mult).then_inc(scaled, 1)

            def front(st, q):
                h, b = st.half(1), st.item(1)
                if 4 <= q < 4 + CT:
                    c = q - 4
                    r = c % 2
                    dve.wait_ge(taps, 2 * (CT * b + c + 1))
                    for k in range(PAD):
                        if k:
                            dve.wait_ge(conv_done, PAD * (CT * b + c) + k)
                        nc.vector.scalar_tensor_tensor(out=fr2[:, r, :], in0=fr1[:, r, k:k + S],
                                                       scalar=cw[:, c, k:k + 1], in1=fr2[:, r, :],
                                                       op0=ALU.mult, op1=ALU.add).then_inc(conv_done, 1)
                if 5 <= q < 5 + CT:
                    c = q - 5
                    r = c % 2
                    if c == 0 and st.reuses(1):
                        dve.wait_ge(o_full, 2 * (b - 1))
                    dve.wait_ge(u_tanh, CT * b + c + 1)
                    nc.vector.scalar_tensor_tensor(out=u_sb[h][:, c, :], in0=fr3[:, r, :], scalar=1.0,
                                                   in1=fr2[:, r, :], op0=ALU.add,
                                                   op1=ALU.mult).then_inc(u_ready, 1)
                if 8 <= q < 10:
                    for c in (2 * (q - 8), 2 * (q - 8) + 1):
                        use = F_Z + c
                        dve.wait_ge(z_tanh, CT * b + c + 1)
                        nc.vector.scalar_tensor_tensor(out=z_sb[h][:, c, :], in0=z_sb[h][:, c, :], scalar=1.0,
                                                       in1=ps_f[use % 2][:, :], op0=ALU.add,
                                                       op1=ALU.mult).then_inc(f_free[use % 2], 1)
                if 11 <= q < 13:
                    i = q - 11
                    n = 2 * b + i
                    dve.wait_ge(sp_exp, n + 1)
                    w = fr1[:, :, PAD:PAD + S]
                    nc.vector.tensor_scalar(w, fr2[:, :, :], 1.0, -1.0, ALU.add, ALU.add).then_inc(sp_steps, 1)
                    dve.wait_ge(sp_steps, 3 * n + 1)
                    nc.vector.tensor_tensor(w, fr2[:, :, :], w, ALU.subtract).then_inc(sp_steps, 1)
                    dve.wait_ge(sp_steps, 3 * n + 2)
                    dve.wait_ge(sp_ln, n + 1)
                    nc.vector.tensor_tensor(w, fr3[:, :, :], w, ALU.add).then_inc(sp_steps, 1)
                    dve.wait_ge(sp_steps, 3 * n + 3)
                    pair = slice(2 * i, 2 * i + 2)
                    nc.vector.scalar_tensor_tensor(out=dt_sb[h][:, pair, :], in0=hT[:, :, :], scalar=0.0, in1=w,
                                                   op0=ALU.max, op1=ALU.add).then_inc(dt_ready, 1)
                    dve.wait_ge(dt_ready, 4 * b + 2 * i + 1)
                    nc.vector.tensor_tensor(du_sb[h][:, pair, :], dt_sb[h][:, pair, :], u_sb[h][:, pair, :],
                                            ALU.mult).then_inc(dt_ready, 1)
                if 10 <= q < 12:
                    i = q - 10
                    for k in range(2):
                        c = 2 * i + k
                        use = F_DT + c
                        dve.wait_ge(f_full[use % 2], f_count(b, use))
                        if i and k == 0:
                            dve.wait_ge(dt_ready, 4 * b + 1)
                        nc.vector.tensor_scalar(hT[:, k, :], ps_f[use % 2][:, :], bdt[:, c:c + 1], None,
                                                ALU.add).then_inc(f_free[use % 2], 1)

            def norm(st, q):
                b = st.item(2)
                if q == 11:
                    dve.wait_ge(xin_loaded, 16 * (b + 1))
                    for t in range(TT):
                        nc.vector.bn_stats(stats[:, t, :], xin[:, t, :])
                    dve.drain()
                    for t in range(TT):
                        ins = nc.vector.bn_aggr(mv[:, t, :], stats[:, t, :])
                    ins.then_inc(mv_done, 1)
                    dve.wait_ge(mv_done, b + 1)
                    nc.vector.tensor_scalar(var_eps[:, :], mv[:, :, 1], EPS, None, ALU.add).then_inc(var_done, 1)
                if q == 13:
                    dve.wait_ge(rstd_done, b + 1)
                    nc.vector.tensor_tensor(ms_eps[:, :], rstd[:, :], rstd[:, :], ALU.mult).then_inc(ms_done, 1)
                    dve.wait_ge(ms_done, 3 * b + 1)
                    nc.vector.tensor_tensor(ms_eps[:, :], ms_eps[:, :], mv[:, :, 1], ALU.mult).then_inc(ms_done, 1)
                    dve.wait_ge(ms_done, 3 * b + 2)
                    nc.vector.tensor_scalar(ms_eps[:, :], ms_eps[:, :], EPS, None, ALU.add).then_inc(ms_done, 1)
                    if st.has(1):
                        dve.wait_ge(f_full[1], f_count(b - 1, F_T + 1))
                    for t in range(TT):
                        ins = nc.vector.tensor_scalar(xl[:, t, :], xin[:, t, :], mv[:, t, 0:1], rstd[:, t:t + 1],
                                                      ALU.subtract, ALU.mult)
                    ins.then_inc(xl_ready, 1)
                    dve.wait_ge(xl_ready, b + 1)
                    nc.vector.tensor_tensor(xin[:, :, :], xin[:, :, :], xl[:, :, :], ALU.add).then_inc(res_ready, 1)

            def read_y(st, o, c):
                h, b = st.half(o), st.item(o)
                n = CT * b + c
                dve.wait_ge(summed, BLK // 2 * b + BPT // 2 * (c + 1))
                nc.vector.scalar_tensor_tensor(out=u_sb[h][:, c, :], in0=u_sb[h][:, c, :], scalar=dsk[:, c:c + 1],
                                               in1=ps_y[c % 2][:, :], op0=ALU.mult, op1=ALU.add).then_inc(y_read, 1)
                dve.wait_ge(y_read, n + 1)
                nc.vector.tensor_tensor(u_sb[h][:, c, :], u_sb[h][:, c, :], z_sb[h][:, c, :],
                                        ALU.mult).then_inc(gated, 1)

            def emit(st):
                for q in range(BLK):
                    if st.has(0):
                        h, b = st.half(0), st.item(0)
                        c = BLK * b + q
                        s = state[q % RING]
                        dve.wait_ge(rep_done, 2 * (c + 1))
                        if q == 0:
                            dve.wait_ge(bc_ready, 2 * G * b + G)
                        if q >= RING or st.has(-1):
                            dve.wait_ge(summed, BLK // 2 * b + (q - RING) // 2 + 1)
                        nc.vector.tensor_tensor(s[:, :, :], ps_du[q % 2][:, :].unsqueeze(1).to_broadcast([P, G, S]),
                                                bc_sb[h][:, 0:G, :], ALU.mult).then_inc(drive_ready, 1)
                        dve.wait_ge(drive_ready, c + 1)
                        dve.wait_ge(decay_ready, G * (c + 1))
                        flat = s[:, :, :].rearrange("p g t -> p (g t)")
                        nc.vector.tensor_tensor_scan(flat, decay[q % 2][:, :, :].rearrange("p g t -> p (g t)"),
                                                     flat, 0.0, ALU.mult, ALU.add).then_inc(scanned, 1)
                    if q in (7, 11, 15) and st.has(0):
                        read_y(st, 0, (q - 7) // 4)
                    if q == 3 and st.has(-1):
                        read_y(st, -1, CT - 1)
                    if st.has(-1) and q in (4, 5):
                        b = st.item(-1)
                        v = q - 4
                        dve.wait_ge(res_back, 16 * (b + 1))
                        dve.wait_ge(o_full, 2 * b + v + 1)
                        if v == 0 and st.has(-2):
                            dve.wait_ge(stored, 16 * b)
                        nc.vector.tensor_tensor(x_new[:, 2 * v:2 * v + 2, :], res_in[:, 2 * v:2 * v + 2, :],
                                                ps_y[1][:, :].rearrange("p (t d) -> p t d", d=D),
                                                ALU.add).then_inc(o_read, 1)
                    if st.has(1):
                        front(st, q)
                    if st.has(2):
                        norm(st, q)

            run_steps(dve, emit, NB, 2, 1)

        @block.scalar
        def _(act):
            act.wait_ge(w_loaded, 16 * 14)
            nc.scalar.activation(nega[:, :, :], nega[:, :, :], ACT.Exp).then_inc(a_ready, 1)
            act.wait_ge(scaled, 8)

            def front(st, q):
                h, b = st.half(1), st.item(1)
                if q == 1:
                    for k in range(KT):
                        use = F_T + k
                        act.wait_ge(f_full[use % 2], f_count(b, use))
                        if k == 0 and st.has(0):
                            act.wait_ge(dt_ready, 4 * b)
                        nc.scalar.activation(hT[:, k, :], ps_f[use % 2][:, :], ACT.Copy,
                                             scale=nw[:, k:k + 1]).then_inc(f_free[use % 2], 1)
                if 5 <= q < 5 + CT:
                    c = q - 5
                    r = c % 2
                    act.wait_ge(conv_done, PAD * (CT * b + c + 1))
                    nc.scalar.activation(fr3[:, r, :], fr2[:, r, :], ACT.Tanh).then_inc(u_tanh, 1)
                if 3 <= q < 3 + CT:
                    c = q - 3
                    r = c % 2
                    use = F_U + c
                    act.wait_ge(f_full[use % 2], f_count(b, use))
                    if c >= 2:
                        act.wait_ge(u_ready, CT * b + c - 1)
                    nc.scalar.activation(fr2[:, r, :], ps_f[use % 2][:, :], ACT.Identity, bias=cb[:, c:c + 1],
                                         scale=cw[:, c, PAD:K]).then_inc(taps, 1)
                    nc.scalar.activation(fr1[:, r, PAD:PAD + S], ps_f[use % 2][:, :], ACT.Copy).then_inc(taps, 1)
                    act.wait_ge(taps, 2 * (CT * b + c + 1))
                    act.sem_inc(f_free[use % 2], 1)
                if 7 <= q < 9:
                    for c in (2 * (q - 7), 2 * (q - 7) + 1):
                        use = F_Z + c
                        act.wait_ge(f_full[use % 2], f_count(b, use))
                        if c == 0 and st.reuses(1):
                            act.wait_ge(gated, CT * (b - 1))
                        nc.scalar.activation(z_sb[h][:, c, :], ps_f[use % 2][:, :], ACT.Tanh).then_inc(z_tanh, 1)
                if q == 9:
                    use = F_X
                    act.wait_ge(f_full[use % 2], f_count(b, use))
                    if st.has(0):
                        act.wait_ge(bc_ready, 2 * G * b)
                    nc.scalar.activation(xd[:, :], ps_f[use % 2][0:RX, :], ACT.Copy).then_inc(f_free[use % 2], 1)
                if 10 <= q < 12:
                    i = q - 10
                    n = 2 * b + i
                    for k in range(2):
                        use = F_DT + 2 * i + k
                        act.wait_ge(f_free[use % 2], f_read(b, use))
                    if i:
                        act.wait_ge(dt_ready, 4 * b + 1)
                    nc.scalar.activation(fr2[:, :, :], hT[:, :, :], ACT.Abs).then_inc(sp_in, 1)
                    act.wait_ge(sp_in, n + 1)
                    nc.scalar.activation(fr2[:, :, :], fr2[:, :, :], ACT.Exp, scale=-1.0).then_inc(sp_exp, 1)
                    act.wait_ge(sp_exp, n + 1)
                    nc.scalar.activation(fr3[:, :, :], fr2[:, :, :], ACT.Ln, bias=1.0).then_inc(sp_ln, 1)
                if 12 <= q < 16:
                    for k in range(2):
                        g = 2 * (q - 12) + k
                        use = F_BC + g
                        act.wait_ge(f_full[use % 2], f_count(b, use))
                        nc.scalar.activation(bc_sb[h][:, g, :], ps_f[use % 2][:, :], ACT.Copy).then_inc(bc_ready, 1)

            def emit(st):
                for q in range(BLK):
                    if st.has(0):
                        b = st.item(0)
                        c = BLK * b + q
                        act.wait_ge(rep_done, 2 * c + 1)
                        if q >= 2 or st.has(-1):
                            act.wait_ge(scanned, c - 1)
                        for g in range(G):
                            nc.scalar.activation(decay[q % 2][:, g, 1:S], ps_dt[q % 2][:, 1:S], ACT.Exp,
                                                 scale=nega[:, q, g:g + 1]).then_inc(decay_ready, 1)
                    if st.has(1):
                        front(st, q)
                    if st.has(2) and q == 14:
                        b = st.item(2)
                        act.wait_ge(rrms_done, b + 1)
                        act.wait_ge(res_ready, b + 1)
                        for t in range(TT):
                            nc.scalar.activation(xl[:, t, :], xl[:, t, :], ACT.Copy,
                                                 scale=rrms[:, t:t + 1]).then_inc(xh_ready, 1)

            run_steps(act, emit, NB, 2, 1)

        @block.tensor
        def _(pe):
            pe.wait_ge(w_loaded, 16 * 14)
            pe.wait_ge(scaled, 8)

            def take(st, use):
                b = st.item(1)
                if use >= 2:
                    if use - 2 >= F_BC:
                        pe.wait_ge(bc_ready, 2 * G * b + use - 2 - F_BC + 1)
                    else:
                        pe.wait_ge(f_free[use % 2], f_read(b, use - 2))
                elif st.has(0):
                    pe.wait_ge(bc_ready, 2 * G * b)
                return ps_f[use % 2]

            def front(st, q):
                h, b = st.half(1), st.item(1)
                if q == 1:
                    pe.wait_ge(xh_ready, TT * (b + 1))
                    for k in range(KT):
                        f = take(st, F_T + k)
                        for t in range(TT):
                            ins = nc.tensor.transpose(f[:, t * P:(t + 1) * P], xl[:, t, k * P:(k + 1) * P],
                                                      id_sb[:, :])
                        ins.then_inc(f_full[k % 2], 1)
                if 3 <= q < 3 + CT or 7 <= q < 9:
                    if q == 3:
                        for k in range(KT):
                            pe.wait_ge(f_free[k], f_read(b, F_T + k))
                    for e in (q - 3,) if q < 7 else (CT + 2 * (q - 7), CT + 2 * (q - 7) + 1):
                        use = F_U + e
                        f = take(st, use)
                        for k in range(KT):
                            ins = nc.tensor.matmul(f[:, :], win[:, k, e * P:(e + 1) * P], hT[:, k, :],
                                                   start=(k == 0), stop=(k == KT - 1))
                        ins.then_inc(f_full[use % 2], 1)
                if q == 9:
                    f = take(st, F_X)
                    pe.wait_ge(u_ready, CT * (b + 1))
                    for c in range(CT):
                        ins = nc.tensor.matmul(f[0:RX, :], wx[:, c, :], u_sb[h][:, c, :],
                                               start=(c == 0), stop=(c == CT - 1))
                    ins.then_inc(f_full[F_X % 2], 1)
                if 10 <= q < 12:
                    for c in (2 * (q - 10), 2 * (q - 10) + 1):
                        use = F_DT + c
                        f = take(st, use)
                        pe.wait_ge(f_free[F_X % 2], f_read(b, F_X))
                        nc.tensor.matmul(f[:, :], wdt[:, c * P:(c + 1) * P], xd[:, :], start=True,
                                         stop=True).then_inc(f_full[use % 2], 1)
                if 12 <= q < 16:
                    for k in range(2):
                        g = 2 * (q - 12) + k
                        use = F_BC + g
                        f = take(st, use)
                        nc.tensor.matmul(f[:, :], pick_s[:, g, :], xd[:, :], start=True,
                                         stop=True).then_inc(f_full[use % 2], 1)

            def repeat(st, o, q):
                h, b = st.half(o), st.item(o)
                c, r = BLK * b + q, q % 2
                if q == 0:
                    pe.wait_ge(dt_ready, 4 * (b + 1))
                if q >= 2 or st.has(o - 1):
                    pe.wait_ge(decay_ready, G * (c - 1))
                nc.tensor.matmul(ps_dt[r][:, :], pick_b[:, q % BPT, :], dt_sb[h][:, q // BPT, :],
                                 start=True, stop=True).then_inc(rep_done, 1)
                if q >= 2 or st.has(o - 1):
                    pe.wait_ge(drive_ready, c - 1)
                nc.tensor.matmul(ps_du[r][:, :], pick_b[:, q % BPT, :], du_sb[h][:, q // BPT, :],
                                 start=True, stop=True).then_inc(rep_done, 1)

            def sum_pair(st, o, q):
                b = st.item(o)
                tile = q // BPT
                if q % BPT == 0:
                    if tile >= 2:
                        pe.wait_ge(y_read, CT * b + tile - 1)
                    elif st.has(o - 1):
                        if tile == 0:
                            pe.wait_ge(y_read, CT * b - 1)
                        else:
                            pe.wait_ge(o_read, 2 * b)
                pe.wait_ge(weighed, BLK * b + q + 2)
                for g in range(G):
                    for k in range(2):
                        p0 = CH * ((q + k) % BPT)
                        ins = nc.tensor.matmul(ps_y[tile % 2][p0:p0 + CH, :], sum_q[:, :],
                                               state[(q + k) % RING][:, g, :], start=(g == 0), stop=(g == G - 1),
                                               skip_group_check=True)
                ins.then_inc(summed, 1)

            def project(st, v):
                h, b = st.half(-1), st.item(-1)
                pe.wait_ge(gated, CT * (b + 1))
                if v:
                    pe.wait_ge(o_read, 2 * b + 1)
                for u in range(2):
                    t = 2 * v + u
                    for c in range(CT):
                        ins = nc.tensor.matmul(ps_y[1][:, u * D:(u + 1) * D], u_sb[h][:, c, t * P:(t + 1) * P],
                                               wout[:, c, :], start=(c == 0), stop=(c == CT - 1))
                ins.then_inc(o_full, 1)

            def emit(st):
                for q in range(BLK):
                    if q % 2 == 0 and q >= RING and st.has(0):
                        sum_pair(st, 0, q - RING)
                    if q % 2 == 0 and q < RING and st.has(-1):
                        sum_pair(st, -1, BLK + q - RING)
                    if q == 0 and st.has(0) and not st.has(-1):
                        repeat(st, 0, 0)
                    if q < BLK - 1 and st.has(0):
                        repeat(st, 0, q + 1)
                    if q in (4, 5) and st.has(-1):
                        project(st, q - 4)
                    if st.has(1):
                        front(st, q)
                    if q == BLK - 1 and st.has(1) and st.has(0):
                        repeat(st, 1, 0)

            run_steps(pe, emit, NB, 2, 1)


def _transposed(a):
    return np.swapaxes(a, -1, -2)


def _columns(v):
    return v.reshape(-1, P).T


def kernel(**inputs):
    import concourse.bacc as _bacc
    from concourse.bass_utils import run_bass_kernel_spmd as _run

    x = inputs["L0_attn_a_x"]
    NB, S, D = x.shape
    a = {k[len("L0_attn_a_"):]: v for k, v in inputs.items() if k.startswith("L0_attn_a_")}
    m = {k[len("L0_attn_b_"):]: v for k, v in inputs.items() if k.startswith("L0_attn_b_")}
    f = {k[len("L0_ffn_"):]: v for k, v in inputs.items() if k.startswith("L0_ffn_")}
    wave = np.arange(1, D + 1, dtype=np.float32) * np.float32(2.0 * math.pi / D)
    inv = (np.float32(1.0) / (wave + np.float32(1e-8))).astype(np.float32)
    DI, N = m["A_log"].shape
    R, CH, E = m["dt_proj_w"].shape[0], 32, 8
    Q = P // CH
    G = N // Q
    part = np.arange(P)
    pick_block = (part[:, None, None] == CH * np.arange(Q)[None, :, None] + (part % CH)[None, None, :])
    state_row = R + Q * np.arange(2 * G)[:, None] + (part // CH)[None, :]
    pick_bc = np.arange(R + 2 * N)[:, None, None] == state_row[None, :, :]
    sum_n = (part % CH)[:, None] == np.arange(CH)[None, :]
    lay = {
        "x": x,
        "wqkT": np.concatenate([_transposed(a["Wq"]), _transposed(a["Wk"])], axis=1),
        "wvT": _transposed(a["Wv"]),
        "bqk": np.concatenate([_columns(a["bq"]), _columns(a["bk"])], axis=1),
        "bv": a["bv"].reshape(1, D),
        "phase": np.concatenate([_columns(a["phase_bias"])] * 2, axis=1),
        "inv_wl": np.concatenate([_columns(inv)] * 2, axis=1),
        "ident": np.eye(P, dtype=np.float32),
        "experts": np.tile(np.arange(E, dtype=np.float32), (P, 1)),
        "weights": f["expert_weights"],
        "indices": f["expert_indices"],
        "w1aT": _transposed(f["w1_A"]),
        "w1b": f["w1_B"],
        "w2aT": _transposed(f["w2_A"]),
        "w2b": f["w2_B"],
        "w_in": m["in_proj_w"],
        "conv_w": m["conv_w"].reshape(-1, P, m["conv_w"].shape[1]).transpose(1, 0, 2),
        "conv_b": _columns(m["conv_b"]),
        "norm_w": _columns(m["norm_w"]),
        "w_x": m["x_proj_w"],
        "w_dt": m["dt_proj_w"],
        "b_dt": _columns(m["dt_proj_b"]),
        "a_log": m["A_log"].reshape(DI // CH, CH, G, Q).transpose(3, 1, 0, 2).reshape(P, DI // CH, G),
        "d_skip": _columns(m["D"]),
        "w_out": m["out_proj_w"],
        "pick_block": pick_block.astype(np.float32),
        "pick_bc": pick_bc.astype(np.float32),
        "sum_n": sum_n.astype(np.float32),
    }
    nc = _bacc.Bacc("TRN2", target_bir_lowering=False, num_devices=1)
    arrays, ap = {}, {}
    for name, v in lay.items():
        arrays[name] = np.ascontiguousarray(v)
        ap[name] = nc.dram_tensor(name, v.shape, mybir.dt.from_np(v.dtype), kind="ExternalInput").ap()
    out = nc.dram_tensor("out", x.shape, F32, kind="ExternalOutput").ap()
    x1 = nc.dram_tensor("x1", x.shape, F32, kind="Internal").ap()
    ffn_args = [ap[n] for n in ("weights", "indices", "experts", "w1aT", "w1b", "w2aT", "w2b", "ident")]
    attention(nc, ap["x"], ap["wqkT"], ap["wvT"], ap["bqk"], ap["bv"], ap["phase"], ap["inv_wl"], ap["ident"], x1)
    expert_ffn(nc, "f1_", x1, *ffn_args)
    mamba(nc, x1, out, *(ap[n] for n in (
        "w_in", "conv_w", "conv_b", "norm_w", "w_x", "w_dt", "b_dt", "a_log", "d_skip", "w_out",
        "pick_block", "pick_bc", "sum_n", "ident")))
    expert_ffn(nc, "f2_", out, *ffn_args)
    r = _run(nc, [arrays], core_ids=[0])
    return r.results[0]["out"]
```

```python
import concourse.bass as bass
from concourse import mybir
from contextlib import ExitStack
import math
import numpy as np

F32 = mybir.dt.float32
I32 = mybir.dt.int32
F32R = mybir.dt.float32r
ALU = mybir.AluOpType
ACT = mybir.ActivationFunctionType
P = 128
EPS = 1e-5


class Step:

    def __init__(self, base, j, items):
        self.base, self.j, self.items = base, j, items

    def has(self, o):
        return not isinstance(self.base, int) or 0 <= 2 * self.base + self.j + o < self.items

    def reuses(self, o):
        return not isinstance(self.base, int) or 2 * self.base + self.j + o >= 2

    def item(self, o):
        return 2 * self.base + (self.j + o)

    def half(self, o):
        return (self.j + o) % 2

    def turn(self, o):
        return self.base + (self.j + o) // 2


def run_steps(eng, emit, items, ahead, after=0):
    for s in range(-ahead, 2):
        emit(Step(s // 2, s % 2, items))
    pairs = (items - ahead) // 2
    with eng.Fori(1, pairs) as i:
        emit(Step(i, 0, items))
        emit(Step(i, 1, items))
    for s in range(2 * pairs, items + after):
        emit(Step(s // 2, s % 2, items))


def attention(nc, x, wqkT, wvT, bqk, bv, phase, inv_wl, ident, x1):
    NB, S, D = x.shape
    TT, KT = S // P, D // P
    NF = 2 * KT
    MAGIC = 1.5 * 2.0 ** 23
    C1 = 6.28125
    C2 = 2.0 * math.pi - C1
    PI_IN = 3.1415925
    with ExitStack() as ctx:
        def sb(name, shape, dt=F32):
            return ctx.enter_context(nc.sbuf_tensor("a_" + name, shape, dt))

        def sem(name):
            return ctx.enter_context(nc.semaphore("a_" + name))

        w_qk = sb("w_qk", [P, KT, 2 * D])
        w_v = sb("w_v", [P, KT, D])
        b_v = sb("b_v", [P, D])
        id_sb = sb("ident", [P, P])
        bqk_c = sb("bqk_c", [P, NF])
        wl_c = sb("wl_c", [P, NF])
        ph_c = sb("ph_c", [P, NF])
        shift = sb("shift", [P, NF])
        half_pi = sb("half_pi", [P, 1])
        neg_half = sb("neg_half", [P, TT])
        xin = [sb(f"xin{h}", [P, TT, D]) for h in range(2)]
        xn = [sb(f"xn{h}", [P, TT, D]) for h in range(2)]
        xT = [sb(f"xT{h}", [P, KT, S]) for h in range(2)]
        xres = [sb(f"xres{h}", [P, TT, D]) for h in range(2)]
        xout = [sb(f"xout{h}", [P, TT, D]) for h in range(2)]
        stats = sb("stats", [P, TT, 6])
        mv = [sb(f"mv{h}", [P, TT, 2]) for h in range(2)]
        var_eps = [sb(f"var_eps{h}", [P, TT]) for h in range(2)]
        rstd = [sb(f"rstd{h}", [P, TT]) for h in range(2)]
        theta = sb("theta", [P, NF, S])
        turns = sb("turns", [P, NF, S])
        rest = sb("rest", [P, NF, S])
        sin_in = sb("sin_in", [P, NF, S])
        cos_in = sb("cos_in", [P, NF, S])
        sin_f = [sb(f"sin_f{h}", [P, NF, S]) for h in range(2)]
        cos_f = [sb(f"cos_f{h}", [P, NF, S]) for h in range(2)]
        vals = [sb(f"vals{h}", [P, TT, D + 1]) for h in range(2)]
        probs = [sb(f"probs{h}", [P, TT, S]) for h in range(2)]
        rden = sb("rden", [P, TT])
        ps_t = [ctx.enter_context(nc.psum_tensor(f"a_ps_t{r}", [P, 512], F32)) for r in range(2)]
        ring = [ctx.enter_context(nc.psum_tensor(f"a_ring{r}", [P, 512], F32)) for r in range(2)]
        ps_s = [ctx.enter_context(nc.psum_tensor(f"a_ps_s{r}", [P, 512], F32)) for r in range(2)]
        ps_o = [ctx.enter_context(nc.psum_tensor(f"a_ps_o{r}", [P, 512], F32)) for r in range(2)]

        w_loaded = sem("w_loaded")
        consts_set = sem("consts_set")
        shift_set = sem("shift_set")
        xin_loaded = [sem(f"xin_loaded{h}") for h in range(2)]
        xres_loaded = [sem(f"xres_loaded{h}") for h in range(2)]
        mv_done = sem("mv_done")
        var_done = sem("var_done")
        rstd_done = sem("rstd_done")
        xn_ready = sem("xn_ready")
        xT_full = sem("xT_full")
        xT_copied = sem("xT_copied")
        ring_full = [sem(f"ring_full{r}") for r in range(2)]
        ring_free = [sem(f"ring_free{r}") for r in range(2)]
        reduced = sem("reduced")
        trig_in_used = sem("trig_in_used")
        sim_full = sem("sim_full")
        probs_ready = sem("probs_ready")
        out_full = [sem(f"out_full{r}") for r in range(2)]
        rden_done = sem("rden_done")
        out_free = [sem(f"out_free{r}") for r in range(2)]
        stored = [sem(f"stored{h}") for h in range(2)]

        def rows(t, b):
            return t[bass.ds(b, 1), :, :].rearrange("a (t p) d -> p (a t) d", p=P)

        block = ctx.enter_context(nc.Block())

        @block.sync
        def _(sp):
            sp.dma_start(id_sb[:, :], ident).then_inc(w_loaded, 16)
            sp.dma_start(w_qk[:, :, :], wqkT.rearrange("(k p) e -> p k e", p=P)).then_inc(w_loaded, 16)
            sp.dma_start(w_v[:, :, :], wvT.rearrange("(k p) e -> p k e", p=P)).then_inc(w_loaded, 16)
            sp.dma_start(b_v[:, :], bv.to_broadcast([P, D])).then_inc(w_loaded, 16)
            sp.dma_start(bqk_c[:, :], bqk).then_inc(w_loaded, 16)
            sp.dma_start(wl_c[:, :], inv_wl).then_inc(w_loaded, 16)
            sp.dma_start(ph_c[:, :], phase).then_inc(w_loaded, 16)

            def emit(st):
                if st.has(3):
                    h, n = st.half(3), st.turn(3)
                    if st.reuses(3):
                        sp.wait_ge(xn_ready, TT * (st.item(3) - 1))
                    sp.dma_start(xin[h][:, :, :], rows(x, st.item(3))).then_inc(xin_loaded[h], 16)
                if st.has(0):
                    h, n = st.half(0), st.turn(0)
                    if st.reuses(0):
                        sp.wait_ge(out_free[1], 2 * (st.item(0) - 1))
                    sp.dma_start(xres[h][:, :, :], rows(x, st.item(0))).then_inc(xres_loaded[h], 16)
                    for r in range(2):
                        sp.wait_ge(out_free[r], 2 * st.item(0) + 2)
                    sp.dma_start(rows(x1, st.item(0)), xout[h][:, :, :]).then_inc(stored[h], 16)

            run_steps(sp, emit, NB, 3)
            for h in range(2):
                sp.wait_ge(stored[h], 16 * (NB // 2))

        @block.gpsimd
        def _(pool):
            nc.gpsimd.memset(neg_half[:, :], -0.5).then_inc(consts_set, 1)
            pool.wait_ge(consts_set, 1)

            def emit(st):
                if st.has(3):
                    h = st.half(3)
                    pool.wait_ge(var_done, st.item(3) + 1)
                    nc.gpsimd.tensor_tensor(rstd[h][:, :], var_eps[h][:, :], neg_half[:, :],
                                            ALU.pow).then_inc(rstd_done, 1)

            run_steps(pool, emit, NB, 3)

        @block.vector
        def _(dve):
            nc.vector.memset(half_pi[:, :], math.pi / 2).then_inc(shift_set, 1)
            for h in range(2):
                nc.vector.memset(vals[h][:, :, D:D + 1], 1.0).then_inc(shift_set, 1)
            dve.wait_ge(w_loaded, 7 * 16)
            nc.vector.tensor_tensor(shift[:, :], bqk_c[:, :], wl_c[:, :], ALU.mult).then_inc(shift_set, 1)
            dve.wait_ge(shift_set, 4)
            nc.vector.tensor_tensor(shift[:, :], shift[:, :], ph_c[:, :], ALU.add).then_inc(shift_set, 1)

            def emit(st):
                if st.has(2):
                    h, n = st.half(2), st.turn(2)
                    b = st.item(2)
                    if st.reuses(2):
                        dve.wait_ge(ring_full[1], 3 * (b - 1))
                    for k in range(KT):
                        dve.wait_ge(xT_full, KT * b + k + 1)
                        nc.vector.tensor_copy(xT[h][:, k, :], ps_t[k][:, :]).then_inc(xT_copied, 1)
                if st.has(1):
                    h, n, b = st.half(1), st.turn(1), st.item(1)
                    if st.reuses(1):
                        dve.wait_ge(out_full[1], 2 * (b - 1))
                    for v in range(2):
                        dve.wait_ge(ring_full[v], 3 * b + 3)
                        nc.vector.tensor_tensor(vals[h][:, 2 * v:2 * v + 2, 0:D],
                                                ring[v][:, :].rearrange("p (t d) -> p t d", d=D),
                                                b_v[:, :].unsqueeze(1).to_broadcast([P, 2, D]),
                                                ALU.add).then_inc(ring_free[v], 1)
                    for r in range(2):
                        dve.wait_ge(ring_free[r], 3 * b + 2)
                    nc.vector.tensor_scalar(turns[:, :, :], theta[:, :, :], 1.0 / (2.0 * math.pi), MAGIC,
                                            ALU.mult, ALU.add).then_inc(reduced, 1)
                    dve.wait_ge(reduced, 5 * b + 1)
                    nc.vector.tensor_scalar(turns[:, :, :], turns[:, :, :], MAGIC, None,
                                            ALU.subtract).then_inc(reduced, 1)
                    dve.wait_ge(reduced, 5 * b + 2)
                    nc.vector.scalar_tensor_tensor(out=rest[:, :, :], in0=turns[:, :, :], scalar=-C1,
                                                   in1=theta[:, :, :], op0=ALU.mult,
                                                   op1=ALU.add).then_inc(reduced, 1)
                    dve.wait_ge(reduced, 5 * b + 3)
                    nc.vector.scalar_tensor_tensor(out=rest[:, :, :], in0=turns[:, :, :], scalar=-C2,
                                                   in1=rest[:, :, :], op0=ALU.mult,
                                                   op1=ALU.add).then_inc(reduced, 1)
                    dve.wait_ge(reduced, 5 * b + 4)
                    dve.wait_ge(trig_in_used, 3 * b)
                    nc.vector.tensor_scalar(sin_in[:, :, :], rest[:, :, :], -PI_IN, PI_IN,
                                            ALU.max, ALU.min).then_inc(reduced, 1)
                if st.has(3):
                    h, n, b = st.half(3), st.turn(3), st.item(3)
                    dve.wait_ge(xin_loaded[h], 16 * (n + 1))
                    for t in range(TT):
                        nc.vector.bn_stats(stats[:, t, :], xin[h][:, t, :])
                    dve.drain()
                    for t in range(TT):
                        ins = nc.vector.bn_aggr(mv[h][:, t, :], stats[:, t, :])
                    ins.then_inc(mv_done, 1)
                    dve.wait_ge(mv_done, b + 1)
                    nc.vector.tensor_scalar(var_eps[h][:, :], mv[h][:, :, 1], EPS, None,
                                            ALU.add).then_inc(var_done, 1)
                if st.has(0):
                    h, n, b = st.half(0), st.turn(0), st.item(0)
                    dve.wait_ge(xres_loaded[h], 16 * (n + 1))
                    if st.reuses(0):
                        dve.wait_ge(stored[h], 16 * n)
                    for t in range(TT):
                        r = t % 2
                        dve.wait_ge(out_full[r], 2 * b + t // 2 + 1)
                        nc.vector.reciprocal(rden[:, t:t + 1], ps_o[r][:, D:D + 1]).then_inc(rden_done, 1)
                        dve.wait_ge(rden_done, TT * b + t + 1)
                        ins = nc.vector.scalar_tensor_tensor(out=xout[h][:, t, :], in0=ps_o[r][:, 0:D],
                                                             scalar=rden[:, t:t + 1], in1=xres[h][:, t, :],
                                                             op0=ALU.mult, op1=ALU.add)
                        ins.then_inc(out_free[r], 1)
                if st.has(3):
                    h, n, b = st.half(3), st.turn(3), st.item(3)
                    dve.wait_ge(rstd_done, b + 1)
                    if st.reuses(3):
                        dve.wait_ge(xT_full, KT * (b - 1))
                    for t in range(TT):
                        ins = nc.vector.tensor_scalar(xn[h][:, t, :], xin[h][:, t, :], mv[h][:, t, 0:1],
                                                      rstd[h][:, t:t + 1], ALU.subtract, ALU.mult)
                        ins.then_inc(xn_ready, 1)

            run_steps(dve, emit, NB, 3)

        @block.scalar
        def _(act):
            act.wait_ge(shift_set, 5)

            def emit(st):
                if st.has(1):
                    b = st.item(1)
                    act.wait_ge(reduced, 5 * b)
                    for f in range(NF):
                        r = f % 2
                        act.wait_ge(ring_full[r], 3 * b + f // 2 + 1)
                        nc.scalar.activation(theta[:, f, :], ring[r][:, :], ACT.Identity,
                                             bias=shift[:, f:f + 1], scale=wl_c[:, f:f + 1])\
                            .then_inc(ring_free[r], 1)
                if st.has(0):
                    h, n, b = st.half(0), st.turn(0), st.item(0)
                    if st.reuses(0):
                        act.wait_ge(out_full[1], 2 * (b - 1))
                    for t in range(TT):
                        act.wait_ge(sim_full, TT * b + t + 1)
                        nc.scalar.activation(probs[h][:, t, :], ps_s[t % 2][:, :], ACT.Exp,
                                             scale=1.0 / math.sqrt(D)).then_inc(probs_ready, 1)
                if st.has(1):
                    h, n, b = st.half(1), st.turn(1), st.item(1)
                    if st.reuses(1):
                        act.wait_ge(sim_full, TT * (b - 1))
                    act.wait_ge(reduced, 5 * b + 5)
                    nc.scalar.activation(sin_f[h][:, :, :], sin_in[:, :, :], ACT.Sin).then_inc(trig_in_used, 1)
                    nc.scalar.activation(cos_in[:, :, :], sin_in[:, :, :], ACT.Abs).then_inc(trig_in_used, 1)
                    act.wait_ge(trig_in_used, 3 * b + 2)
                    nc.scalar.activation(cos_f[h][:, :, :], cos_in[:, :, :], ACT.Sin, bias=half_pi[:, 0:1],
                                         scale=-1.0).then_inc(trig_in_used, 1)

            run_steps(act, emit, NB, 3)

        @block.tensor
        def _(pe):
            pe.wait_ge(w_loaded, 7 * 16)

            def take(st, use):
                r = use % 2
                pe.wait_ge(ring_free[r], 3 * st.item(1) + use // 2)
                return r

            def emit(st):
                if st.has(2):
                    h, b = st.half(2), st.item(2)
                    pe.wait_ge(xn_ready, TT * (b + 1))
                    for k in range(KT):
                        if st.has(1):
                            pe.wait_ge(xT_copied, KT * (b - 1) + k + 1)
                        for t in range(TT):
                            ins = nc.tensor.transpose(ps_t[k][:, t * P:(t + 1) * P],
                                                      xn[h][:, t, k * P:(k + 1) * P], id_sb[:, :])
                        ins.then_inc(xT_full, 1)
                if st.has(1):
                    h, b = st.half(1), st.item(1)
                    pe.wait_ge(xT_copied, KT * (b + 1))
                    for f in range(NF):
                        r = take(st, f)
                        for k in range(KT):
                            ins = nc.tensor.matmul(ring[r][:, :], w_qk[:, k, f * P:(f + 1) * P], xT[h][:, k, :],
                                                   start=(k == 0), stop=(k == KT - 1))
                        ins.then_inc(ring_full[r], 1)
                    for v in range(2):
                        r = take(st, NF + v)
                        for u in range(2):
                            t = 2 * v + u
                            for k in range(KT):
                                ins = nc.tensor.matmul(ring[r][:, u * D:(u + 1) * D],
                                                       xT[h][:, k, t * P:(t + 1) * P], w_v[:, k, :],
                                                       start=(k == 0), stop=(k == KT - 1))
                        ins.then_inc(ring_full[r], 1)
                if st.has(0):
                    h, n, b = st.half(0), st.turn(0), st.item(0)
                    pe.wait_ge(trig_in_used, 3 * b + 3)
                    for t in range(TT):
                        if t >= 2:
                            pe.wait_ge(probs_ready, TT * b + t - 1)
                        for m, feats in enumerate((cos_f[h], sin_f[h])):
                            for k in range(KT):
                                ins = nc.tensor.matmul(ps_s[t % 2][:, :], feats[:, KT + k, t * P:(t + 1) * P],
                                                       feats[:, k, :], start=(m == 0 and k == 0),
                                                       stop=(m == 1 and k == KT - 1))
                        ins.then_inc(sim_full, 1)
                    pe.wait_ge(probs_ready, TT * (b + 1))
                    for r in range(2):
                        pe.wait_ge(ring_free[r], 3 * b + 3)
                    for s in range(TT):
                        r = s % 2
                        pe.wait_ge(out_free[r], 2 * b + s // 2)
                        for t in range(TT):
                            ins = nc.tensor.matmul(ps_o[r][:, 0:D + 1], probs[h][:, t, s * P:(s + 1) * P],
                                                   vals[h][:, t, :], start=(t == 0), stop=(t == TT - 1))
                        ins.then_inc(out_full[r], 1)

            run_steps(pe, emit, NB, 3)



def expert_ffn(nc, tag, x, weights, indices, experts, w1aT, w1b, w2aT, w2b, ident):
    D = x.shape[2]
    TOK, TOPK = weights.shape
    ER, FF = w1b.shape
    E = experts.shape[1]
    R = ER // E
    GRP = 512
    NG, TT, KT = TOK // GRP, GRP // P, D // P
    PAIRS, FT = ER // P, FF // P
    NT = TOK // P
    UPS = PAIRS * FT
    UB = 3
    xf = x.rearrange("b s d -> (b s) d")
    with ExitStack() as ctx:
        def sb(name, shape, dt=F32, stage=None):
            return (stage or ctx).enter_context(nc.sbuf_tensor(tag + name, shape, dt))

        def sem(name):
            return ctx.enter_context(nc.semaphore(tag + name))

        x_all = sb("x_all", [P, NT, D])
        xT_all = sb("xT_all", [P, KT, TOK])
        gate_all = sb("gate_all", [P, PAIRS, TOK])
        w_1a = sb("w_1a", [P, KT, E, 2, R])
        w_hi = sb("w_hi", [P, E, FF], F32R)
        w_lo = sb("w_lo", [P, E, FF], F32R)
        w_2a = sb("w_2a", [P, FT, ER])
        w_2b = sb("w_2b", [P, PAIRS, D])
        ps_up = [ctx.enter_context(nc.psum_tensor(f"{tag}ps_up{u}", [P, 2, 512], F32)) for u in range(UB)]
        ps_c = ctx.enter_context(nc.psum_tensor(tag + "ps_c", [P, 512], F32))
        ps_y = ctx.enter_context(nc.psum_tensor(tag + "ps_y", [P, 512], F32))
        T_BANK = [ps_up[0][:, k, :] for k in range(KT)]
        G_BANK = [ps_up[1 + p // 2][:, p % 2, :] for p in range(PAIRS)]

        x_loaded = sem("x_loaded")
        w_loaded = sem("w_loaded")
        w2_loaded = sem("w2_loaded")
        raw_loaded = [sem(f"raw_loaded{r}") for r in range(2)]
        half_set = sem("half_set")
        mv_done = sem("mv_done")
        var_done = sem("var_done")
        rstd_done = sem("rstd_done")
        gate_steps = sem("gate_steps")
        xn_ready = sem("xn_ready")
        gate_x_ready = sem("gate_x_ready")
        xT_full = sem("xT_full")
        xT_ready = sem("xT_ready")
        gate_full = sem("gate_full")
        gate_copied = sem("gate_copied")
        w_high = sem("w_high")
        w_low = sem("w_low")
        a_full = sem("a_full")
        a_high = sem("a_high")
        a_ready = sem("a_ready")
        up_done = sem("up_done")
        gelu_done = sem("gelu_done")
        down_done = sem("down_done")
        c_ready = sem("c_ready")
        y_full = sem("y_full")
        y_ready = sem("y_ready")
        stored = sem("stored")

        with ExitStack() as one:
            id_sb = sb("ident", [P, P], stage=one)
            ex_sb = sb("experts", [P, E], stage=one)
            g_w = sb("g_w", [P, NT, TOPK], stage=one)
            g_i = sb("g_i", [P, NT, TOPK], I32, stage=one)
            g_f = sb("g_f", [P, NT, TOPK], stage=one)
            hit = [sb(f"hit{k}", [P, NT, E], stage=one) for k in range(TOPK)]
            gate = sb("gate", [P, NT, E], stage=one)
            gate_x = sb("gate_x", [P, TT, E, R], stage=one)
            stats = sb("stats", [P, NT, 6], stage=one)
            mv = sb("mv", [P, NT, 2], stage=one)
            var_eps = sb("var_eps", [P, NT], stage=one)
            neg_half = sb("neg_half", [P, NT], stage=one)
            rstd = sb("rstd", [P, NT], stage=one)
            xn = sb("xn", [P, TT, D], stage=one)
            raw = [sb(f"raw{r}", [P, 2, FF], stage=one) for r in range(2)]
            block = one.enter_context(nc.Block())

            @block.sync
            def _(sp):
                for g in range(NG):
                    sp.dma_start(x_all[:, g * TT:(g + 1) * TT, :],
                                 xf[g * GRP:(g + 1) * GRP, :].rearrange("(t p) d -> p t d", p=P))\
                        .then_inc(x_loaded, 16)
                sp.dma_start(g_w[:, :, :], weights.rearrange("(t p) k -> p t k", p=P)).then_inc(w_loaded, 16)
                sp.dma_start(g_i[:, :, :], indices.rearrange("(t p) k -> p t k", p=P)).then_inc(w_loaded, 16)
                sp.dma_start(ex_sb[:, :], experts).then_inc(w_loaded, 16)
                sp.dma_start(id_sb[:, :], ident).then_inc(w_loaded, 16)
                for p in range(PAIRS):
                    if p >= 2:
                        sp.wait_ge(w_low, p - 1)
                    for half in range(2):
                        sp.dma_start(raw[p % 2][half * R:(half + 1) * R, :, :],
                                     w1b[p * P:(p + 1) * P, :].rearrange("(e r) f -> r e f", r=R))\
                            .then_inc(raw_loaded[p % 2], 16)
                for half in range(2):
                    for k in range(KT):
                        sp.dma_start(w_1a[:, k, :, half, :],
                                     w1aT[k * P:(k + 1) * P, :].rearrange("p (e r) -> p e r", r=R))\
                            .then_inc(w2_loaded, 16)
                sp.dma_start(w_2a[:, :, :], w2aT.rearrange("(q p) e -> p q e", p=P)).then_inc(w2_loaded, 16)
                sp.dma_start(w_2b[:, :, :], w2b.rearrange("(q p) d -> p q d", p=P)).then_inc(w2_loaded, 16)

            @block.gpsimd
            def _(pool):
                nc.gpsimd.memset(neg_half[:, :], -0.5).then_inc(half_set, 1)
                pool.wait_ge(half_set, 1)
                pool.wait_ge(var_done, 1)
                nc.gpsimd.tensor_tensor(rstd[:, :], var_eps[:, :], neg_half[:, :], ALU.pow).then_inc(rstd_done, 1)

            @block.vector
            def _(dve):
                for g in range(NG):
                    dve.wait_ge(x_loaded, 16 * NG)
                    for t in range(TT):
                        nc.vector.bn_stats(stats[:, g * TT + t, :], x_all[:, g * TT + t, :])
                dve.drain()
                for t in range(NT):
                    ins = nc.vector.bn_aggr(mv[:, t, :], stats[:, t, :])
                ins.then_inc(mv_done, 1)
                dve.wait_ge(mv_done, 1)
                nc.vector.tensor_scalar(var_eps[:, :], mv[:, :, 1], EPS, None, ALU.add).then_inc(var_done, 1)
                dve.wait_ge(w_loaded, 4 * 16)
                nc.vector.tensor_copy(g_f[:, :, :], g_i[:, :, :]).then_inc(gate_steps, 1)
                dve.wait_ge(gate_steps, 1)
                for k in range(TOPK):
                    nc.vector.tensor_tensor(hit[k][:, :, :], ex_sb[:, :].unsqueeze(1).to_broadcast([P, NT, E]),
                                            g_f[:, :, k:k + 1].to_broadcast([P, NT, E]),
                                            ALU.is_equal).then_inc(gate_steps, 1)
                dve.wait_ge(gate_steps, 1 + TOPK)
                for k in range(TOPK):
                    nc.vector.tensor_tensor(hit[k][:, :, :], hit[k][:, :, :],
                                            g_w[:, :, k:k + 1].to_broadcast([P, NT, E]),
                                            ALU.mult).then_inc(gate_steps, 1)
                dve.wait_ge(gate_steps, 1 + 2 * TOPK)
                nc.vector.tensor_tensor(gate[:, :, :], hit[0][:, :, :], hit[1][:, :, :],
                                        ALU.add).then_inc(gate_steps, 1)
                dve.wait_ge(gate_steps, 2 + 2 * TOPK)
                dve.wait_ge(rstd_done, 1)
                for g in range(NG):
                    if g:
                        dve.wait_ge(xT_full, g)
                    for t in range(TT):
                        n = g * TT + t
                        ins = nc.vector.tensor_scalar(xn[:, t, :], x_all[:, n, :], mv[:, n, 0:1],
                                                      rstd[:, n:n + 1], ALU.subtract, ALU.mult)
                    ins.then_inc(xn_ready, 1)
                    if g:
                        dve.wait_ge(gate_full, PAIRS * g)
                    nc.vector.tensor_copy(gate_x[:, :, :, :], gate[:, g * TT:(g + 1) * TT, :].unsqueeze(3)
                                          .to_broadcast([P, TT, E, R])).then_inc(gate_x_ready, 1)
                    dve.wait_ge(w_high, g + 1)
                    pair = slice(2 * g, 2 * g + 2)
                    nc.vector.tensor_tensor(w_lo[:, pair, :], raw[g % 2][:, :, :], w_hi[:, pair, :].bitcast(F32),
                                            ALU.subtract).then_inc(w_low, 1)

            @block.scalar
            def _(act):
                for g in range(NG):
                    act.wait_ge(raw_loaded[g % 2], 32 * (g // 2 + 1))
                    nc.scalar.activation(w_hi[:, 2 * g:2 * g + 2, :], raw[g % 2][:, :, :], ACT.Copy)\
                        .then_inc(w_high, 1)
                    act.wait_ge(xT_full, g + 1)
                    for k in range(KT):
                        nc.scalar.activation(xT_all[:, k, g * GRP:(g + 1) * GRP], T_BANK[k],
                                             ACT.Copy).then_inc(xT_ready, 1)
                    for p in range(PAIRS):
                        act.wait_ge(gate_full, PAIRS * g + p + 1)
                        nc.scalar.activation(gate_all[:, p, g * GRP:(g + 1) * GRP], G_BANK[p],
                                             ACT.Copy).then_inc(gate_copied, 1)

            @block.tensor
            def _(pe):
                pe.wait_ge(w_loaded, 4 * 16)
                for g in range(NG):
                    pe.wait_ge(xn_ready, g + 1)
                    if g:
                        pe.wait_ge(xT_ready, KT * g)
                    for k in range(KT):
                        for t in range(TT):
                            ins = nc.tensor.transpose(T_BANK[k][:, t * P:(t + 1) * P],
                                                      xn[:, t, k * P:(k + 1) * P], id_sb[:, :])
                    ins.then_inc(xT_full, 1)
                    pe.wait_ge(gate_x_ready, g + 1)
                    for p in range(PAIRS):
                        if g:
                            pe.wait_ge(gate_copied, PAIRS * (g - 1) + p + 1)
                        for t in range(TT):
                            ins = nc.tensor.matmul(G_BANK[p][:, t * P:(t + 1) * P],
                                                   gate_x[:, t, 2 * p:2 * p + 2, :].rearrange("p e r -> p (e r)"),
                                                   id_sb[:, :], start=True, stop=True)
                        ins.then_inc(gate_full, 1)

        with ExitStack() as two:
            a_split = [sb(f"a_split{h}", [P, 2, GRP], F32R, stage=two) for h in range(2)]
            hid = [sb(f"hid{u}", [P, 2, GRP], stage=two) for u in range(UB)]
            c_sb = sb("c_sb", [P, PAIRS, GRP], stage=two)
            x_new = sb("x_new", [P, TT, D], stage=two)
            Y_BANK = [ps_y[:, 0:D], ps_c[:, 0:D]]
            block = two.enter_context(nc.Block())

            @block.sync
            def _(sp):
                with sp.Fori(0, NG) as g:
                    sp.wait_ge(y_ready, TT * g + TT + 2)
                    sp.dma_start(xf[bass.ds(g * GRP, GRP), :].rearrange("(t p) d -> p t d", p=P),
                                 x_new[:, :, :]).then_inc(stored, 16)
                sp.wait_ge(stored, 16 * NG + 16)

            @block.vector
            def _(dve):
                dve.sem_inc(gelu_done, UB)
                dve.sem_inc(down_done, UB)
                dve.sem_inc(c_ready, 1)
                dve.sem_inc(y_ready, 2)
                dve.sem_inc(a_ready, 1)
                dve.sem_inc(stored, 16)

                def low(g, n):
                    dve.wait_ge(a_high, E * g + n + 1)
                    half = a_split[n // 2 % 2][R:P, n % 2, :]
                    nc.vector.tensor_tensor(half, ps_y[R:P, :], half.bitcast(F32),
                                            ALU.subtract).then_inc(a_ready, 1)

                with dve.Fori(0, NG) as g:
                    low(g, 0)
                    low(g, 1)
                    for p in range(PAIRS):
                        if p < PAIRS - 1:
                            low(g, 2 * p + 2)
                            low(g, 2 * p + 3)
                        dve.wait_ge(down_done, UPS * g + FT * (p + 1) + UB)
                        if p == 0:
                            dve.wait_ge(y_full, TT * g + TT)
                        nc.vector.tensor_tensor(c_sb[:, p, :], ps_c[:, :], gate_all[:, p, bass.ds(g * GRP, GRP)],
                                                ALU.mult).then_inc(c_ready, 1)
                    dve.wait_ge(stored, 16 * g + 16)
                    for t in range(TT):
                        dve.wait_ge(y_full, TT * g + t + 1 + TT)
                        nc.vector.tensor_tensor(x_new[:, t, :], Y_BANK[t % 2],
                                                x_all[:, bass.ds(g * TT + t, 1), :].rearrange("p a d -> p (a d)"),
                                                ALU.add).then_inc(y_ready, 1)

            @block.scalar
            def _(act):
                def high(g, n):
                    act.wait_ge(a_full, E * g + n + 1)
                    act.wait_ge(up_done, UPS * g + FT * (n // 2 - 1) + UPS)
                    nc.scalar.activation(a_split[n // 2 % 2][:, n % 2, :], ps_y[:, :], ACT.Copy)\
                        .then_inc(a_high, 1)

                with act.Fori(0, NG) as g:
                    high(g, 0)
                    high(g, 1)
                    for k in range(UPS):
                        p, f, u = k // FT, k % FT, k % UB
                        act.wait_ge(up_done, UPS * g + k + 1 + UPS)
                        act.wait_ge(down_done, UPS * g + k + 1)
                        nc.scalar.activation(hid[u][:, :, :], ps_up[u][:, :, :], ACT.Gelu).then_inc(gelu_done, 1)
                        if p < PAIRS - 1 and f in (1, 4):
                            high(g, 2 * p + 2 + f // 4)

            @block.tensor
            def _(pe):
                pe.sem_inc(up_done, UPS)
                pe.sem_inc(y_full, TT)
                pe.wait_ge(w2_loaded, 6 * 16)

                def ranks(g, n):
                    pe.wait_ge(a_ready, E * g + n + 1)
                    if n == 0:
                        pe.wait_ge(y_ready, TT * g + 2)
                    for k in range(KT):
                        ins = nc.tensor.matmul(ps_y[:, :], w_1a[:, k, n, :, :].rearrange("p h r -> p (h r)"),
                                               xT_all[:, k, bass.ds(g * GRP, GRP)],
                                               start=(k == 0), stop=(k == KT - 1))
                    ins.then_inc(a_full, 1)

                def up(g, k):
                    p, f, u = k // FT, k % FT, k % UB
                    pe.wait_ge(gelu_done, UPS * g + k + 1)
                    if f == 0:
                        pe.wait_ge(a_ready, E * g + 2 * p + 3)
                    for e in range(2):
                        for part in (w_hi, w_lo):
                            ins = nc.tensor.matmul(ps_up[u][:, e, :], part[:, 2 * p + e, f * P:(f + 1) * P],
                                                   a_split[p % 2][:, e, :], start=(part is w_hi),
                                                   stop=(part is w_lo))
                    ins.then_inc(up_done, 1)

                def down(g, k):
                    p, f, u = k // FT, k % FT, k % UB
                    pe.wait_ge(gelu_done, UPS * g + k + 1 + UB)
                    if f == 0:
                        pe.wait_ge(c_ready, PAIRS * g + p + 1)
                        if p == 0:
                            pe.wait_ge(y_ready, TT * g + 2)
                    for e in range(2):
                        cols = slice(p * P + e * R, p * P + (e + 1) * R)
                        ins = nc.tensor.matmul(ps_c[e * R:(e + 1) * R, :], w_2a[:, f, cols], hid[u][:, e, :],
                                               start=(f == 0), stop=(f == FT - 1), skip_group_check=True)
                    ins.then_inc(down_done, 1)

                with pe.Fori(0, NG) as g:
                    ranks(g, 0)
                    ranks(g, 1)
                    up(g, 0)
                    up(g, 1)
                    for k in range(UPS):
                        if k + 2 < UPS:
                            up(g, k + 2)
                        down(g, k)
                        if k // FT < PAIRS - 1 and k % FT in (0, 3):
                            ranks(g, 2 * (k // FT) + 2 + k % FT // 3)
                    pe.wait_ge(c_ready, PAIRS * (g + 1) + 1)
                    for t in range(TT):
                        pe.wait_ge(y_ready, TT * g + t + 1)
                        for p in range(PAIRS):
                            ins = nc.tensor.matmul(Y_BANK[t % 2], c_sb[:, p, t * P:(t + 1) * P],
                                                   w_2b[:, p, :], start=(p == 0), stop=(p == PAIRS - 1))
                        ins.then_inc(y_full, 1)


def mamba(nc, x_in, out, w_in, conv_w, conv_b, norm_w, w_x, w_dt, b_dt, a_log, d_skip, w_out,
          pick_bc, sum_n, ident):
    NB, S, D = x_in.shape
    DI = w_out.shape[0]
    K = conv_w.shape[2]
    R = w_dt.shape[0]
    RX = w_x.shape[1]
    N = (RX - R) // 2
    TT, KT, CT = S // P, D // P, DI // P
    CH = 32
    Q = P // CH
    G = N // Q
    BLK = DI // CH
    BPT = BLK // CT
    PAD = K - 1
    RING = 4
    FB = 4
    F_T, F_U, F_Z = 0, KT, KT + CT
    F_X = F_Z + CT
    F_DT = F_X + 1
    F_BC = F_DT + CT
    F_ALL = F_BC + 2 * G
    F_PER = [len(range(r, F_ALL, FB)) for r in range(FB)]
    with ExitStack() as ctx:
        def sb(name, shape, dt=F32):
            return ctx.enter_context(nc.sbuf_tensor("m_" + name, shape, dt))

        def sem(name):
            return ctx.enter_context(nc.semaphore("m_" + name))

        def bank(name):
            return ctx.enter_context(nc.psum_tensor("m_" + name, [P, 512], F32))

        win = sb("win", [P, KT, 2 * DI])
        wx = sb("wx", [P, CT, RX])
        wdt = sb("wdt", [RX, DI])
        wout = sb("wout", [P, CT, D])
        cw = sb("cw", [P, CT, K])
        cb = sb("cb", [P, CT])
        nw = sb("nw", [P, KT])
        bdt = sb("bdt", [P, CT])
        dsk = sb("dsk", [P, CT])
        nega = sb("nega", [P, BLK, G])
        pick_s = sb("pick_s", [RX, 2 * G, P])
        sum_q = sb("sum_q", [P, CH])
        id_sb = sb("ident", [P, P])
        neg_half = sb("neg_half", [P, TT])
        xin = sb("xin", [P, TT, D])
        xl = sb("xl", [P, TT, D])
        x_new = sb("x_new", [P, TT, D])
        stats = sb("stats", [P, TT, 6])
        mv = sb("mv", [P, TT, 2])
        var_eps = sb("var_eps", [P, TT])
        rstd = sb("rstd", [P, TT])
        ms_eps = sb("ms_eps", [P, TT])
        rrms = sb("rrms", [P, TT])
        hT = sb("hT", [P, KT, S])
        fr1 = sb("fr1", [P, 2, PAD + S])
        fr2 = sb("fr2", [P, 2, S])
        fr3 = sb("fr3", [P, 2, S])
        xd = sb("xd", [RX, S])
        dt_sb = [sb(f"dt{h}", [P, CT, S]) for h in range(2)]
        du_sb = [sb(f"du{h}", [P, CT, S]) for h in range(2)]
        u_sb = [sb(f"u{h}", [P, CT, S]) for h in range(2)]
        z_sb = [sb(f"z{h}", [P, CT, S]) for h in range(2)]
        bc_sb = [sb(f"bc{h}", [P, 2 * G, S]) for h in range(2)]
        dt_rep = [sb(f"dt_rep{r}", [P, S]) for r in range(2)]
        du_rep = [sb(f"du_rep{r}", [P, S]) for r in range(2)]
        decay = [sb(f"decay{r}", [P, G, S]) for r in range(2)]
        state = [sb(f"state{r}", [P, G, S]) for r in range(RING)]
        ps_y = [bank(f"ps_y{r}") for r in range(2)]
        ps_o = [bank(f"ps_o{r}") for r in range(2)]
        ps_f = [bank(f"ps_f{r}") for r in range(FB)]

        w_loaded = sem("w_loaded")
        a_ready = sem("a_ready")
        scaled = sem("scaled")
        half_set = sem("half_set")
        xin_loaded = sem("xin_loaded")
        mv_done = sem("mv_done")
        var_done = sem("var_done")
        rstd_done = sem("rstd_done")
        ms_done = sem("ms_done")
        rrms_done = sem("rrms_done")
        xl_ready = sem("xl_ready")
        res_ready = sem("res_ready")
        res_stored = sem("res_stored")
        xh_ready = sem("xh_ready")
        f_full = [sem(f"f_full{r}") for r in range(FB)]
        f_free = [sem(f"f_free{r}") for r in range(FB)]
        hT_ready = sem("hT_ready")
        taps = sem("taps")
        conv_done = sem("conv_done")
        u_tanh = sem("u_tanh")
        u_ready = sem("u_ready")
        z_tanh = sem("z_tanh")
        z_ready = sem("z_ready")
        xd_ready = sem("xd_ready")
        sp_in = sem("sp_in")
        sp_exp = sem("sp_exp")
        sp_ln = sem("sp_ln")
        sp_w = sem("sp_w")
        sp_steps = sem("sp_steps")
        du_ready = sem("du_ready")
        dt_ready = sem("dt_ready")
        bc_ready = sem("bc_ready")
        dt_spread = [sem(f"dt_spread{r}") for r in range(2)]
        du_spread = [sem(f"du_spread{r}") for r in range(2)]
        decay_ready = sem("decay_ready")
        drive_ready = sem("drive_ready")
        scanned = sem("scanned")
        weighed = sem("weighed")
        summed = sem("summed")
        y_read = sem("y_read")
        y_skip = sem("y_skip")
        gated = sem("gated")
        o_full = sem("o_full")
        o_read = sem("o_read")
        res_back = sem("res_back")
        stored = sem("stored")
        NW = 15

        def rows(t, b):
            return t[bass.ds(b, 1), :, :].rearrange("a (t p) d -> p (a t) d", p=P)

        def f_count(b, use):
            return F_PER[use % FB] * b + use // FB + 1

        def f_read(b, use):
            return len(range(use % FB, F_BC, FB)) * b + use // FB + 1

        def spread(b, q):
            return 16 * (BLK // 2 * b + q // 2 + 1)

        block = ctx.enter_context(nc.Block())

        @block.sync
        def _(sp):
            for dst, src in ((id_sb[:, :], ident), (win[:, :, :], w_in.rearrange("(k p) e -> p k e", p=P)),
                             (wx[:, :, :], w_x.rearrange("(k p) e -> p k e", p=P)),
                             (wdt[0:R, :], w_dt), (wout[:, :, :], w_out.rearrange("(k p) e -> p k e", p=P)),
                             (cw[:, :, :], conv_w), (cb[:, :], conv_b), (nw[:, :], norm_w), (bdt[:, :], b_dt),
                             (dsk[:, :], d_skip), (nega[:, :, :], a_log), (pick_s[:, :, :], pick_bc), (sum_q[:, :], sum_n)):
                sp.dma_start(dst, src).then_inc(w_loaded, 16)

            def spread_block(st, o, q):
                h, b = st.half(o), st.item(o)
                c, r = BLK * b + q, q % 2
                rows_q = slice(CH * (q % BPT), CH * (q % BPT) + CH)
                again = q >= 2 or st.has(o - 1)
                if q % (BLK // 2) == 0:
                    sp.wait_ge(dt_ready, 2 * b + q // (BLK // 2) + 1)
                if again:
                    sp.wait_ge(decay_ready, G * (c - 1))
                sp.dma_start(dt_rep[r][:, :], dt_sb[h][rows_q, q // BPT, :].unsqueeze(1).to_broadcast([CH, Q, S]))\
                    .then_inc(dt_spread[r], 16)
                if q % (BLK // 2) == 0:
                    sp.wait_ge(du_ready, 2 * b + q // (BLK // 2) + 1)
                if again:
                    sp.wait_ge(drive_ready, c - 1)
                sp.dma_start(du_rep[r][:, :], du_sb[h][rows_q, q // BPT, :].unsqueeze(1).to_broadcast([CH, Q, S]))\
                    .then_inc(du_spread[r], 16)

            def emit(st):
                if st.has(0) and not st.has(-1):
                    spread_block(st, 0, 0)
                    spread_block(st, 0, 1)
                for q in range(BLK):
                    if q < BLK - 2 and st.has(0):
                        spread_block(st, 0, q + 2)
                    if q >= BLK - 2 and st.has(1) and st.has(0):
                        spread_block(st, 1, q + 2 - BLK)
                    if q == 0 and st.has(1):
                        sp.wait_ge(res_ready, st.item(1) + 1)
                        sp.dma_start(rows(out, st.item(1)), xin[:, :, :]).then_inc(res_stored, 16)
                    if q == 1 and st.has(-1):
                        b = st.item(-1)
                        sp.wait_ge(res_stored, 16 * (b + 1))
                        if st.has(-2):
                            sp.wait_ge(stored, 16 * b)
                        sp.dma_start(x_new[:, :, :], rows(out, b)).then_inc(res_back, 16)
                    if q == 2 and st.has(2):
                        if st.has(1):
                            sp.wait_ge(res_stored, 16 * st.item(2))
                        sp.dma_start(xin[:, :, :], rows(x_in, st.item(2))).then_inc(xin_loaded, 16)
                    if q == 9 and st.has(-1):
                        sp.wait_ge(o_read, 2 * (st.item(-1) + 1))
                        sp.dma_start(rows(out, st.item(-1)), x_new[:, :, :]).then_inc(stored, 16)

            run_steps(sp, emit, NB, 2, 1)
            sp.wait_ge(stored, 16 * NB)

        @block.gpsimd
        def _(pool):
            nc.gpsimd.memset(neg_half[:, :], -0.5).then_inc(half_set, 1)
            pool.wait_ge(half_set, 1)

            def emit(st):
                for q in range(BLK):
                    if st.has(0):
                        h, b = st.half(0), st.item(0)
                        c = BLK * b + q
                        pool.wait_ge(scanned, c + 1)
                        if q == 0:
                            pool.wait_ge(bc_ready, 2 * G * (b + 1))
                        s = state[q % RING]
                        nc.gpsimd.tensor_tensor(s[:, :, :], s[:, :, :], bc_sb[h][:, G:2 * G, :],
                                                ALU.mult).then_inc(weighed, 1)
                    if st.has(1) and 11 <= q < 13:
                        h, b, i = st.half(1), st.item(1), q - 11
                        pair = slice(2 * i, 2 * i + 2)
                        pool.wait_ge(dt_ready, 2 * b + i + 1)
                        nc.gpsimd.tensor_tensor(du_sb[h][:, pair, :], dt_sb[h][:, pair, :], u_sb[h][:, pair, :],
                                                ALU.mult).then_inc(du_ready, 1)
                    if st.has(0) and q in (7, 11, 15):
                        h, c = st.half(0), (q - 7) // 4
                        pool.wait_ge(y_read, CT * st.item(0) + c + 1)
                        nc.gpsimd.tensor_tensor(u_sb[h][:, c, :], u_sb[h][:, c, :], z_sb[h][:, c, :],
                                                ALU.mult).then_inc(gated, 1)
                    if st.has(2) and q == 14:
                        pool.wait_ge(xl_ready, st.item(2) + 1)
                        nc.gpsimd.tensor_tensor(xin[:, :, :], xin[:, :, :], xl[:, :, :],
                                                ALU.add).then_inc(res_ready, 1)
                    if st.has(2) and q == 12:
                        pool.wait_ge(var_done, st.item(2) + 1)
                        nc.gpsimd.tensor_tensor(rstd[:, :], var_eps[:, :], neg_half[:, :],
                                                ALU.pow).then_inc(rstd_done, 1)
                    if st.has(2) and q == 13:
                        pool.wait_ge(ms_done, 3 * (st.item(2) + 1))
                        nc.gpsimd.tensor_tensor(rrms[:, :], ms_eps[:, :], neg_half[:, :],
                                                ALU.pow).then_inc(rrms_done, 1)

            run_steps(pool, emit, NB, 2, 1)

        @block.vector
        def _(dve):
            dve.wait_ge(w_loaded, 16 * 13)
            nc.vector.memset(wdt[R:RX, :], 0.0).then_inc(scaled, 1)
            nc.vector.memset(fr1[:, :, 0:PAD], 0.0).then_inc(scaled, 1)
            for r in range(2):
                nc.vector.memset(decay[r][:, :, 0:1], 0.0).then_inc(scaled, 1)
            nc.vector.tensor_scalar(cw[:, :, :], cw[:, :, :], 0.5, None, ALU.mult).then_inc(scaled, 1)
            nc.vector.tensor_scalar(cb[:, :], cb[:, :], 0.5, None, ALU.mult).then_inc(scaled, 1)
            nc.vector.tensor_scalar(win[:, :, DI:2 * DI], win[:, :, DI:2 * DI], 0.5, None,
                                    ALU.mult).then_inc(scaled, 1)
            dve.wait_ge(a_ready, 1)
            nc.vector.tensor_scalar(nega[:, :, :], nega[:, :, :], -1.0, None, ALU.mult).then_inc(scaled, 1)

            def front(st, q):
                h, b = st.half(1), st.item(1)
                if 4 <= q < 4 + CT:
                    c = q - 4
                    r = c % 2
                    dve.wait_ge(taps, 2 * (CT * b + c + 1))
                    for k in range(PAD):
                        if k:
                            dve.wait_ge(conv_done, PAD * (CT * b + c) + k)
                        nc.vector.scalar_tensor_tensor(out=fr2[:, r, :], in0=fr1[:, r, k:k + S],
                                                       scalar=cw[:, c, k:k + 1], in1=fr2[:, r, :],
                                                       op0=ALU.mult, op1=ALU.add).then_inc(conv_done, 1)
                if 5 <= q < 5 + CT:
                    c = q - 5
                    r = c % 2
                    if c == 0 and st.reuses(1):
                        dve.wait_ge(o_full, 2 * (b - 1))
                    dve.wait_ge(u_tanh, CT * b + c + 1)
                    nc.vector.scalar_tensor_tensor(out=u_sb[h][:, c, :], in0=fr3[:, r, :], scalar=1.0,
                                                   in1=fr2[:, r, :], op0=ALU.add,
                                                   op1=ALU.mult).then_inc(u_ready, 1)
                if 8 <= q < 10:
                    for c in (2 * (q - 8), 2 * (q - 8) + 1):
                        use = F_Z + c
                        dve.wait_ge(z_tanh, CT * b + c + 1)
                        nc.vector.scalar_tensor_tensor(out=z_sb[h][:, c, :], in0=z_sb[h][:, c, :], scalar=1.0,
                                                       in1=ps_f[use % FB][:, :], op0=ALU.add,
                                                       op1=ALU.mult).then_inc(f_free[use % FB], 1)
                if 11 <= q < 13:
                    i = q - 11
                    n = 2 * b + i
                    w = fr1[:, :, PAD:PAD + S]
                    dve.wait_ge(sp_w, n + 1)
                    nc.vector.scalar_tensor_tensor(out=w, in0=w, scalar=1.0, in1=fr2[:, :, :],
                                                   op0=ALU.subtract, op1=ALU.subtract).then_inc(sp_steps, 1)
                    dve.wait_ge(sp_steps, 2 * n + 1)
                    dve.wait_ge(sp_ln, n + 1)
                    nc.vector.tensor_tensor(w, fr3[:, :, :], w, ALU.subtract).then_inc(sp_steps, 1)
                    dve.wait_ge(sp_steps, 2 * n + 2)
                    nc.vector.scalar_tensor_tensor(out=dt_sb[h][:, 2 * i:2 * i + 2, :], in0=hT[:, :, :], scalar=0.0,
                                                   in1=w, op0=ALU.max, op1=ALU.add).then_inc(dt_ready, 1)

            def norm(st, q):
                b = st.item(2)
                if q == 11:
                    dve.wait_ge(xin_loaded, 16 * (b + 1))
                    for t in range(TT):
                        nc.vector.bn_stats(stats[:, t, :], xin[:, t, :])
                    dve.drain()
                    for t in range(TT):
                        ins = nc.vector.bn_aggr(mv[:, t, :], stats[:, t, :])
                    ins.then_inc(mv_done, 1)
                    dve.wait_ge(mv_done, b + 1)
                    nc.vector.tensor_scalar(var_eps[:, :], mv[:, :, 1], EPS, None, ALU.add).then_inc(var_done, 1)
                if q == 13:
                    dve.wait_ge(rstd_done, b + 1)
                    nc.vector.tensor_tensor(ms_eps[:, :], rstd[:, :], rstd[:, :], ALU.mult).then_inc(ms_done, 1)
                    dve.wait_ge(ms_done, 3 * b + 1)
                    nc.vector.tensor_tensor(ms_eps[:, :], ms_eps[:, :], mv[:, :, 1], ALU.mult).then_inc(ms_done, 1)
                    dve.wait_ge(ms_done, 3 * b + 2)
                    nc.vector.tensor_scalar(ms_eps[:, :], ms_eps[:, :], EPS, None, ALU.add).then_inc(ms_done, 1)
                    if st.has(1):
                        dve.wait_ge(f_full[1], f_count(b - 1, F_T + 1))
                    for t in range(TT):
                        ins = nc.vector.tensor_scalar(xl[:, t, :], xin[:, t, :], mv[:, t, 0:1], rstd[:, t:t + 1],
                                                      ALU.subtract, ALU.mult)
                    ins.then_inc(xl_ready, 1)

            def read_y(st, o, c):
                h, b = st.half(o), st.item(o)
                n = CT * b + c
                dve.wait_ge(summed, BLK // 2 * b + BPT // 2 * (c + 1))
                nc.vector.scalar_tensor_tensor(out=u_sb[h][:, c, :], in0=u_sb[h][:, c, :], scalar=dsk[:, c:c + 1],
                                               in1=ps_y[c % 2][:, :], op0=ALU.mult, op1=ALU.add).then_inc(y_read, 1)
                if c < CT - 1:
                    return
                dve.wait_ge(y_read, n + 1)
                nc.vector.tensor_tensor(u_sb[h][:, c, :], u_sb[h][:, c, :], z_sb[h][:, c, :],
                                        ALU.mult).then_inc(gated, 1)

            def emit(st):
                for q in range(BLK):
                    if st.has(0):
                        h, b = st.half(0), st.item(0)
                        c = BLK * b + q
                        s = state[q % RING]
                        dve.wait_ge(du_spread[q % 2], spread(b, q))
                        if q == 0:
                            dve.wait_ge(bc_ready, 2 * G * b + G)
                        if q >= RING or st.has(-1):
                            dve.wait_ge(summed, BLK // 2 * b + (q - RING) // 2 + 1)
                        nc.vector.tensor_tensor(s[:, :, :], du_rep[q % 2][:, :].unsqueeze(1).to_broadcast([P, G, S]),
                                                bc_sb[h][:, 0:G, :], ALU.mult).then_inc(drive_ready, 1)
                        dve.wait_ge(drive_ready, c + 1)
                        dve.wait_ge(decay_ready, G * (c + 1))
                        flat = s[:, :, :].rearrange("p g t -> p (g t)")
                        nc.vector.tensor_tensor_scan(flat, decay[q % 2][:, :, :].rearrange("p g t -> p (g t)"),
                                                     flat, 0.0, ALU.mult, ALU.add).then_inc(scanned, 1)
                    if q in (7, 11, 15) and st.has(0):
                        read_y(st, 0, (q - 7) // 4)
                    if q == 3 and st.has(-1):
                        read_y(st, -1, CT - 1)
                    if st.has(-1) and q in (4, 5):
                        b = st.item(-1)
                        v = q - 4
                        dve.wait_ge(res_back, 16 * (b + 1))
                        dve.wait_ge(o_full, 2 * b + v + 1)
                        nc.vector.tensor_tensor(x_new[:, 2 * v:2 * v + 2, :], x_new[:, 2 * v:2 * v + 2, :],
                                                ps_o[v][:, :].rearrange("p (t d) -> p t d", d=D),
                                                ALU.add).then_inc(o_read, 1)
                    if st.has(1):
                        front(st, q)
                    if st.has(2):
                        norm(st, q)

            run_steps(dve, emit, NB, 2, 1)

        @block.scalar
        def _(act):
            act.wait_ge(w_loaded, 16 * 13)
            nc.scalar.activation(nega[:, :, :], nega[:, :, :], ACT.Exp).then_inc(a_ready, 1)
            act.wait_ge(scaled, 8)

            def front(st, q):
                h, b = st.half(1), st.item(1)
                if q == 1:
                    for k in range(KT):
                        use = F_T + k
                        act.wait_ge(f_full[use % FB], f_count(b, use))
                        if k == 0 and st.has(0):
                            act.wait_ge(dt_ready, 2 * b)
                        nc.scalar.activation(hT[:, k, :], ps_f[use % FB][:, :], ACT.Copy,
                                             scale=nw[:, k:k + 1]).then_inc(f_free[use % FB], 1)
                if 5 <= q < 5 + CT:
                    c = q - 5
                    r = c % 2
                    act.wait_ge(conv_done, PAD * (CT * b + c + 1))
                    nc.scalar.activation(fr3[:, r, :], fr2[:, r, :], ACT.Tanh).then_inc(u_tanh, 1)
                if 3 <= q < 3 + CT:
                    c = q - 3
                    r = c % 2
                    use = F_U + c
                    act.wait_ge(f_full[use % FB], f_count(b, use))
                    if c >= 2:
                        act.wait_ge(u_ready, CT * b + c - 1)
                    nc.scalar.activation(fr2[:, r, :], ps_f[use % FB][:, :], ACT.Identity, bias=cb[:, c:c + 1],
                                         scale=cw[:, c, PAD:K]).then_inc(taps, 1)
                    nc.scalar.activation(fr1[:, r, PAD:PAD + S], ps_f[use % FB][:, :], ACT.Copy).then_inc(taps, 1)
                    act.wait_ge(taps, 2 * (CT * b + c + 1))
                    act.sem_inc(f_free[use % FB], 1)
                if 7 <= q < 9:
                    for c in (2 * (q - 7), 2 * (q - 7) + 1):
                        use = F_Z + c
                        act.wait_ge(f_full[use % FB], f_count(b, use))
                        if c == 0 and st.reuses(1):
                            act.wait_ge(gated, CT * (b - 1))
                        nc.scalar.activation(z_sb[h][:, c, :], ps_f[use % FB][:, :], ACT.Tanh).then_inc(z_tanh, 1)
                if q == 9:
                    use = F_X
                    act.wait_ge(f_full[use % FB], f_count(b, use))
                    if st.has(0):
                        act.wait_ge(bc_ready, 2 * G * b)
                    nc.scalar.activation(xd[:, :], ps_f[use % FB][0:RX, :], ACT.Copy).then_inc(f_free[use % FB], 1)
                if 10 <= q < 12:
                    i = q - 10
                    n = 2 * b + i
                    for k in range(2):
                        c = 2 * i + k
                        use = F_DT + c
                        act.wait_ge(f_full[use % FB], f_count(b, use))
                        if i:
                            act.wait_ge(dt_ready, 2 * b + 1)
                        nc.scalar.activation(hT[:, k, :], ps_f[use % FB][:, :], ACT.Identity,
                                             bias=bdt[:, c:c + 1]).then_inc(f_free[use % FB], 1)
                    for k in range(2):
                        use = F_DT + 2 * i + k
                        act.wait_ge(f_free[use % FB], f_read(b, use))
                    nc.scalar.activation(fr2[:, :, :], hT[:, :, :], ACT.Abs).then_inc(sp_in, 1)
                    act.wait_ge(sp_in, n + 1)
                    nc.scalar.activation(fr2[:, :, :], fr2[:, :, :], ACT.Exp, scale=-1.0).then_inc(sp_exp, 1)
                    act.wait_ge(sp_exp, n + 1)
                    nc.scalar.activation(fr1[:, :, PAD:PAD + S], fr2[:, :, :], ACT.Identity,
                                         bias=1.0).then_inc(sp_w, 1)
                    nc.scalar.activation(fr3[:, :, :], fr2[:, :, :], ACT.Ln, bias=1.0).then_inc(sp_ln, 1)
                if 12 <= q < 16:
                    for k in range(2):
                        g = 2 * (q - 12) + k
                        use = F_BC + g
                        act.wait_ge(f_full[use % FB], f_count(b, use))
                        nc.scalar.activation(bc_sb[h][:, g, :], ps_f[use % FB][:, :], ACT.Copy).then_inc(bc_ready, 1)

            def decays(st, o, q):
                c = BLK * st.item(o) + q
                act.wait_ge(dt_spread[q % 2], spread(st.item(o), q))
                if q >= 2 or st.has(o - 1):
                    act.wait_ge(scanned, c - 1)
                for g in range(G):
                    nc.scalar.activation(decay[q % 2][:, g, 1:S], dt_rep[q % 2][:, 1:S], ACT.Exp,
                                         scale=nega[:, q, g:g + 1]).then_inc(decay_ready, 1)

            def emit(st):
                if st.has(0) and not st.has(-1):
                    decays(st, 0, 0)
                for q in range(BLK):
                    if q < BLK - 1 and st.has(0):
                        decays(st, 0, q + 1)
                    if q == BLK - 1 and st.has(1) and st.has(0):
                        decays(st, 1, 0)
                    if st.has(1):
                        front(st, q)
                    if st.has(2) and q == 15:
                        b = st.item(2)
                        act.wait_ge(rrms_done, b + 1)
                        act.wait_ge(res_ready, b + 1)
                        for t in range(TT):
                            nc.scalar.activation(xl[:, t, :], xl[:, t, :], ACT.Copy,
                                                 scale=rrms[:, t:t + 1]).then_inc(xh_ready, 1)

            run_steps(act, emit, NB, 2, 1)

        @block.tensor
        def _(pe):
            pe.wait_ge(w_loaded, 16 * 13)
            pe.wait_ge(scaled, 8)

            def take(st, use):
                b = st.item(1)
                if use >= FB:
                    if use - FB >= F_BC:
                        pe.wait_ge(bc_ready, 2 * G * b + use - FB - F_BC + 1)
                    else:
                        pe.wait_ge(f_free[use % FB], f_read(b, use - FB))
                elif st.has(0):
                    pe.wait_ge(bc_ready, 2 * G * b)
                return ps_f[use % FB]

            def front(st, q):
                h, b = st.half(1), st.item(1)
                if q == 1:
                    pe.wait_ge(xh_ready, TT * (b + 1))
                    for k in range(KT):
                        f = take(st, F_T + k)
                        for t in range(TT):
                            ins = nc.tensor.transpose(f[:, t * P:(t + 1) * P], xl[:, t, k * P:(k + 1) * P],
                                                      id_sb[:, :])
                        ins.then_inc(f_full[k % FB], 1)
                if 3 <= q < 3 + CT or 7 <= q < 9:
                    if q == 3:
                        for k in range(KT):
                            pe.wait_ge(f_free[k], f_read(b, F_T + k))
                    for e in (q - 3,) if q < 7 else (CT + 2 * (q - 7), CT + 2 * (q - 7) + 1):
                        use = F_U + e
                        f = take(st, use)
                        for k in range(KT):
                            ins = nc.tensor.matmul(f[:, :], win[:, k, e * P:(e + 1) * P], hT[:, k, :],
                                                   start=(k == 0), stop=(k == KT - 1))
                        ins.then_inc(f_full[use % FB], 1)
                if q == 9:
                    f = take(st, F_X)
                    pe.wait_ge(u_ready, CT * (b + 1))
                    for c in range(CT):
                        ins = nc.tensor.matmul(f[0:RX, :], wx[:, c, :], u_sb[h][:, c, :],
                                               start=(c == 0), stop=(c == CT - 1))
                    ins.then_inc(f_full[F_X % FB], 1)
                if 10 <= q < 12:
                    for c in (2 * (q - 10), 2 * (q - 10) + 1):
                        use = F_DT + c
                        f = take(st, use)
                        pe.wait_ge(f_free[F_X % FB], f_read(b, F_X))
                        nc.tensor.matmul(f[:, :], wdt[:, c * P:(c + 1) * P], xd[:, :], start=True,
                                         stop=True).then_inc(f_full[use % FB], 1)
                if 12 <= q < 16:
                    for k in range(2):
                        g = 2 * (q - 12) + k
                        use = F_BC + g
                        f = take(st, use)
                        nc.tensor.matmul(f[:, :], pick_s[:, g, :], xd[:, :], start=True,
                                         stop=True).then_inc(f_full[use % FB], 1)

            def sum_pair(st, o, q):
                b = st.item(o)
                tile = q // BPT
                if q % BPT == 0:
                    if tile >= 2:
                        pe.wait_ge(y_read, CT * b + tile - 1)
                    elif st.has(o - 1):
                        pe.wait_ge(y_read, CT * b + tile - 1)
                pe.wait_ge(weighed, BLK * b + q + 2)
                for g in range(G):
                    for k in range(2):
                        p0 = CH * ((q + k) % BPT)
                        ins = nc.tensor.matmul(ps_y[tile % 2][p0:p0 + CH, :], sum_q[:, :],
                                               state[(q + k) % RING][:, g, :], start=(g == 0), stop=(g == G - 1),
                                               skip_group_check=True)
                ins.then_inc(summed, 1)

            def project(st, v):
                h, b = st.half(-1), st.item(-1)
                pe.wait_ge(gated, CT * (b + 1))
                if st.has(-2):
                    pe.wait_ge(o_read, 2 * b + v - 1)
                for u in range(2):
                    t = 2 * v + u
                    for c in range(CT):
                        ins = nc.tensor.matmul(ps_o[v][:, u * D:(u + 1) * D], u_sb[h][:, c, t * P:(t + 1) * P],
                                               wout[:, c, :], start=(c == 0), stop=(c == CT - 1))
                ins.then_inc(o_full, 1)

            def emit(st):
                for q in range(BLK):
                    if q % 2 == 0 and q >= RING and st.has(0):
                        sum_pair(st, 0, q - RING)
                    if q % 2 == 0 and q < RING and st.has(-1):
                        sum_pair(st, -1, BLK + q - RING)
                    if q in (4, 5) and st.has(-1):
                        project(st, q - 4)
                    if st.has(1):
                        front(st, q)

            run_steps(pe, emit, NB, 2, 1)


def _transposed(a):
    return np.swapaxes(a, -1, -2)


def _columns(v):
    return v.reshape(-1, P).T


def kernel(**inputs):
    import concourse.bacc as _bacc
    from concourse.bass_utils import run_bass_kernel_spmd as _run

    x = inputs["L0_attn_a_x"]
    NB, S, D = x.shape
    a = {k[len("L0_attn_a_"):]: v for k, v in inputs.items() if k.startswith("L0_attn_a_")}
    m = {k[len("L0_attn_b_"):]: v for k, v in inputs.items() if k.startswith("L0_attn_b_")}
    f = {k[len("L0_ffn_"):]: v for k, v in inputs.items() if k.startswith("L0_ffn_")}
    wave = np.arange(1, D + 1, dtype=np.float32) * np.float32(2.0 * math.pi / D)
    inv = (np.float32(1.0) / (wave + np.float32(1e-8))).astype(np.float32)
    DI, N = m["A_log"].shape
    R, CH, E = m["dt_proj_w"].shape[0], 32, 8
    Q = P // CH
    G = N // Q
    part = np.arange(P)
    state_row = R + Q * np.arange(2 * G)[:, None] + (part % Q)[None, :]
    pick_bc = np.arange(R + 2 * N)[:, None, None] == state_row[None, :, :]
    sum_n = (part // Q)[:, None] == np.arange(CH)[None, :]
    lay = {
        "x": x,
        "wqkT": np.concatenate([_transposed(a["Wq"]), _transposed(a["Wk"])], axis=1),
        "wvT": _transposed(a["Wv"]),
        "bqk": np.concatenate([_columns(a["bq"]), _columns(a["bk"])], axis=1),
        "bv": a["bv"].reshape(1, D),
        "phase": np.concatenate([_columns(a["phase_bias"])] * 2, axis=1),
        "inv_wl": np.concatenate([_columns(inv)] * 2, axis=1),
        "ident": np.eye(P, dtype=np.float32),
        "experts": np.tile(np.arange(E, dtype=np.float32), (P, 1)),
        "weights": f["expert_weights"],
        "indices": f["expert_indices"],
        "w1aT": _transposed(f["w1_A"]),
        "w1b": f["w1_B"],
        "w2aT": _transposed(f["w2_A"]),
        "w2b": f["w2_B"],
        "w_in": m["in_proj_w"],
        "conv_w": m["conv_w"].reshape(-1, P, m["conv_w"].shape[1]).transpose(1, 0, 2),
        "conv_b": _columns(m["conv_b"]),
        "norm_w": _columns(m["norm_w"]),
        "w_x": m["x_proj_w"],
        "w_dt": m["dt_proj_w"],
        "b_dt": _columns(m["dt_proj_b"]),
        "a_log": m["A_log"].reshape(DI // CH, CH, G, Q).transpose(1, 3, 0, 2).reshape(P, DI // CH, G),
        "d_skip": _columns(m["D"]),
        "w_out": m["out_proj_w"],
        "pick_bc": pick_bc.astype(np.float32),
        "sum_n": sum_n.astype(np.float32),
    }
    nc = _bacc.Bacc("TRN2", target_bir_lowering=False, num_devices=1)
    arrays, ap = {}, {}
    for name, v in lay.items():
        arrays[name] = np.ascontiguousarray(v)
        ap[name] = nc.dram_tensor(name, v.shape, mybir.dt.from_np(v.dtype), kind="ExternalInput").ap()
    out = nc.dram_tensor("out", x.shape, F32, kind="ExternalOutput").ap()
    x1 = nc.dram_tensor("x1", x.shape, F32, kind="Internal").ap()
    ffn_args = [ap[n] for n in ("weights", "indices", "experts", "w1aT", "w1b", "w2aT", "w2b", "ident")]
    attention(nc, ap["x"], ap["wqkT"], ap["wvT"], ap["bqk"], ap["bv"], ap["phase"], ap["inv_wl"], ap["ident"], x1)
    expert_ffn(nc, "f1_", x1, *ffn_args)
    mamba(nc, x1, out, *(ap[n] for n in (
        "w_in", "conv_w", "conv_b", "norm_w", "w_x", "w_dt", "b_dt", "a_log", "d_skip", "w_out",
        "pick_bc", "sum_n", "ident")))
    expert_ffn(nc, "f2_", out, *ffn_args)
    r = _run(nc, [arrays], core_ids=[0])
    return r.results[0]["out"]
```

```python
import concourse.bass as bass
from concourse import mybir
from contextlib import ExitStack
import math
import numpy as np

F32 = mybir.dt.float32
I32 = mybir.dt.int32
F32R = mybir.dt.float32r
ALU = mybir.AluOpType
ACT = mybir.ActivationFunctionType
P = 128
EPS = 1e-5


class Step:

    def __init__(self, base, j, items):
        self.base, self.j, self.items = base, j, items

    def has(self, o):
        return not isinstance(self.base, int) or 0 <= 2 * self.base + self.j + o < self.items

    def reuses(self, o):
        return not isinstance(self.base, int) or 2 * self.base + self.j + o >= 2

    def item(self, o):
        return 2 * self.base + (self.j + o)

    def half(self, o):
        return (self.j + o) % 2

    def turn(self, o):
        return self.base + (self.j + o) // 2


def run_steps(eng, emit, items, ahead, after=0):
    for s in range(-ahead, 2):
        emit(Step(s // 2, s % 2, items))
    pairs = (items - ahead) // 2
    with eng.Fori(1, pairs) as i:
        emit(Step(i, 0, items))
        emit(Step(i, 1, items))
    for s in range(2 * pairs, items + after):
        emit(Step(s // 2, s % 2, items))


def attention(nc, x, wqkT, wvT, bqk, bv, phase, inv_wl, ident, x1):
    NB, S, D = x.shape
    TT, KT = S // P, D // P
    NF = 2 * KT
    MAGIC = 1.5 * 2.0 ** 23
    C1 = 6.28125
    C2 = 2.0 * math.pi - C1
    PI_IN = 3.1415925
    with ExitStack() as ctx:
        def sb(name, shape, dt=F32):
            return ctx.enter_context(nc.sbuf_tensor("a_" + name, shape, dt))

        def sem(name):
            return ctx.enter_context(nc.semaphore("a_" + name))

        w_hi = sb("w_hi", [P, KT, 3 * D], F32R)
        w_lo = sb("w_lo", [P, KT, 3 * D], F32R)
        b_v = sb("b_v", [P, D])
        id_sb = sb("ident", [P, P])
        bqk_c = sb("bqk_c", [P, NF])
        wl_c = sb("wl_c", [P, NF])
        ph_c = sb("ph_c", [P, NF])
        shift = sb("shift", [P, NF])
        half_pi = sb("half_pi", [P, 1])
        neg_half = sb("neg_half", [P, TT])
        xin = [sb(f"xin{h}", [P, TT, D]) for h in range(2)]
        xn = [sb(f"xn{h}", [P, TT, D]) for h in range(2)]
        xT_hi = [sb(f"xT_hi{h}", [P, KT, S], F32R) for h in range(2)]
        xT_lo = [sb(f"xT_lo{h}", [P, KT, S], F32R) for h in range(2)]
        xres = [sb(f"xres{h}", [P, TT, D]) for h in range(2)]
        xout = [sb(f"xout{h}", [P, TT, D]) for h in range(2)]
        stats = sb("stats", [P, TT, 6])
        mv = [sb(f"mv{h}", [P, TT, 2]) for h in range(2)]
        var_eps = [sb(f"var_eps{h}", [P, TT]) for h in range(2)]
        rstd = [sb(f"rstd{h}", [P, TT]) for h in range(2)]
        theta = sb("theta", [P, NF, S])
        turns = sb("turns", [P, NF, S])
        rest = sb("rest", [P, NF, S])
        sin_in = sb("sin_in", [P, NF, S])
        cos_in = sb("cos_in", [P, NF, S])
        trig = sb("trig", [P, 2 * NF, S])
        trig_hi = [sb(f"trig_hi{h}", [P, 2 * NF, S], F32R) for h in range(2)]
        trig_lo = [sb(f"trig_lo{h}", [P, 2 * NF, S], F32R) for h in range(2)]
        vals = [sb(f"vals{h}", [P, TT, D + 1]) for h in range(2)]
        probs = [sb(f"probs{h}", [P, TT, S]) for h in range(2)]
        w_raw = probs[0][:, 0:KT * 3 * D // S, :].rearrange("p a s -> p (a s)").rearrange("p (k e) -> p k e", k=KT)
        rden = sb("rden", [P, TT])
        ps_t = [ctx.enter_context(nc.psum_tensor(f"a_ps_t{r}", [P, 512], F32)) for r in range(2)]
        ring = [ctx.enter_context(nc.psum_tensor(f"a_ring{r}", [P, 512], F32)) for r in range(2)]
        ps_s = [ctx.enter_context(nc.psum_tensor(f"a_ps_s{r}", [P, 512], F32)) for r in range(2)]
        ps_o = [ctx.enter_context(nc.psum_tensor(f"a_ps_o{r}", [P, 512], F32)) for r in range(2)]

        w_loaded = sem("w_loaded")
        consts_set = sem("consts_set")
        shift_set = sem("shift_set")
        xin_loaded = [sem(f"xin_loaded{h}") for h in range(2)]
        xres_loaded = [sem(f"xres_loaded{h}") for h in range(2)]
        mv_done = sem("mv_done")
        var_done = sem("var_done")
        rstd_done = sem("rstd_done")
        xn_ready = sem("xn_ready")
        xT_full = sem("xT_full")
        xT_high = sem("xT_high")
        xT_copied = sem("xT_copied")
        w_high = sem("w_high")
        w_split = sem("w_split")
        ring_full = [sem(f"ring_full{r}") for r in range(2)]
        ring_free = [sem(f"ring_free{r}") for r in range(2)]
        reduced = sem("reduced")
        trig_in_used = sem("trig_in_used")
        trig_high = sem("trig_high")
        sin_low = sem("sin_low")
        cos_low = sem("cos_low")
        sim_full = sem("sim_full")
        probs_ready = sem("probs_ready")
        out_full = [sem(f"out_full{r}") for r in range(2)]
        rden_done = sem("rden_done")
        out_free = [sem(f"out_free{r}") for r in range(2)]
        stored = [sem(f"stored{h}") for h in range(2)]

        def rows(t, b):
            return t[bass.ds(b, 1), :, :].rearrange("a (t p) d -> p (a t) d", p=P)

        block = ctx.enter_context(nc.Block())

        @block.sync
        def _(sp):
            sp.dma_start(id_sb[:, :], ident).then_inc(w_loaded, 16)
            sp.dma_start(w_raw[:, :, 0:2 * D], wqkT.rearrange("(k p) e -> p k e", p=P)).then_inc(w_loaded, 16)
            sp.dma_start(w_raw[:, :, 2 * D:3 * D], wvT.rearrange("(k p) e -> p k e", p=P)).then_inc(w_loaded, 16)
            sp.dma_start(b_v[:, :], bv.to_broadcast([P, D])).then_inc(w_loaded, 16)
            sp.dma_start(bqk_c[:, :], bqk).then_inc(w_loaded, 16)
            sp.dma_start(wl_c[:, :], inv_wl).then_inc(w_loaded, 16)
            sp.dma_start(ph_c[:, :], phase).then_inc(w_loaded, 16)

            def emit(st):
                if st.has(3):
                    h, n = st.half(3), st.turn(3)
                    if st.reuses(3):
                        sp.wait_ge(xn_ready, TT * (st.item(3) - 1))
                    sp.dma_start(xin[h][:, :, :], rows(x, st.item(3))).then_inc(xin_loaded[h], 16)
                if st.has(0):
                    h, n = st.half(0), st.turn(0)
                    if st.reuses(0):
                        sp.wait_ge(out_free[1], 2 * (st.item(0) - 1))
                    sp.dma_start(xres[h][:, :, :], rows(x, st.item(0))).then_inc(xres_loaded[h], 16)
                    for r in range(2):
                        sp.wait_ge(out_free[r], 2 * st.item(0) + 2)
                    sp.dma_start(rows(x1, st.item(0)), xout[h][:, :, :]).then_inc(stored[h], 16)

            run_steps(sp, emit, NB, 3)
            for h in range(2):
                sp.wait_ge(stored[h], 16 * (NB // 2))

        @block.gpsimd
        def _(pool):
            nc.gpsimd.memset(neg_half[:, :], -0.5).then_inc(consts_set, 1)
            pool.wait_ge(consts_set, 1)

            def emit(st):
                if st.has(3):
                    h = st.half(3)
                    pool.wait_ge(var_done, st.item(3) + 1)
                    nc.gpsimd.tensor_tensor(rstd[h][:, :], var_eps[h][:, :], neg_half[:, :],
                                            ALU.pow).then_inc(rstd_done, 1)
                if st.has(1):
                    h, b = st.half(1), st.item(1)
                    pool.wait_ge(trig_high, 2 * b + 1)
                    nc.gpsimd.tensor_tensor(trig_lo[h][:, 0:NF, :], trig[:, 0:NF, :],
                                            trig_hi[h][:, 0:NF, :].bitcast(F32), ALU.subtract).then_inc(sin_low, 1)

            run_steps(pool, emit, NB, 3)

        @block.vector
        def _(dve):
            nc.vector.memset(half_pi[:, :], math.pi / 2).then_inc(shift_set, 1)
            for h in range(2):
                nc.vector.memset(vals[h][:, :, D:D + 1], 1.0).then_inc(shift_set, 1)
            dve.wait_ge(w_loaded, 7 * 16)
            nc.vector.tensor_copy(w_hi[:, :, :], w_raw).then_inc(w_high, 1)
            dve.wait_ge(w_high, 1)
            nc.vector.tensor_tensor(w_lo[:, :, :], w_raw, w_hi[:, :, :].bitcast(F32),
                                    ALU.subtract).then_inc(w_split, 1)
            nc.vector.tensor_tensor(shift[:, :], bqk_c[:, :], wl_c[:, :], ALU.mult).then_inc(shift_set, 1)
            dve.wait_ge(shift_set, 4)
            nc.vector.tensor_tensor(shift[:, :], shift[:, :], ph_c[:, :], ALU.add).then_inc(shift_set, 1)

            def emit(st):
                if st.has(0):
                    h, b = st.half(0), st.item(0)
                    dve.wait_ge(trig_high, 2 * b + 2)
                    nc.vector.tensor_tensor(trig_lo[h][:, NF:2 * NF, :], trig[:, NF:2 * NF, :],
                                            trig_hi[h][:, NF:2 * NF, :].bitcast(F32),
                                            ALU.subtract).then_inc(cos_low, 1)
                if st.has(1):
                    h, n, b = st.half(1), st.turn(1), st.item(1)
                    if st.reuses(1):
                        dve.wait_ge(out_full[1], 2 * (b - 1))
                    for v in range(2):
                        dve.wait_ge(ring_full[v], 3 * b + 3)
                        nc.vector.tensor_tensor(vals[h][:, 2 * v:2 * v + 2, 0:D],
                                                ring[v][:, :].rearrange("p (t d) -> p t d", d=D),
                                                b_v[:, :].unsqueeze(1).to_broadcast([P, 2, D]),
                                                ALU.add).then_inc(ring_free[v], 1)
                    for r in range(2):
                        dve.wait_ge(ring_free[r], 3 * b + 2)
                    nc.vector.tensor_scalar(turns[:, :, :], theta[:, :, :], 1.0 / (2.0 * math.pi), MAGIC,
                                            ALU.mult, ALU.add).then_inc(reduced, 1)
                    dve.wait_ge(reduced, 5 * b + 1)
                    nc.vector.tensor_scalar(turns[:, :, :], turns[:, :, :], MAGIC, None,
                                            ALU.subtract).then_inc(reduced, 1)
                    dve.wait_ge(reduced, 5 * b + 2)
                    nc.vector.scalar_tensor_tensor(out=rest[:, :, :], in0=turns[:, :, :], scalar=-C1,
                                                   in1=theta[:, :, :], op0=ALU.mult,
                                                   op1=ALU.add).then_inc(reduced, 1)
                    dve.wait_ge(reduced, 5 * b + 3)
                    nc.vector.scalar_tensor_tensor(out=rest[:, :, :], in0=turns[:, :, :], scalar=-C2,
                                                   in1=rest[:, :, :], op0=ALU.mult,
                                                   op1=ALU.add).then_inc(reduced, 1)
                    dve.wait_ge(reduced, 5 * b + 4)
                    dve.wait_ge(trig_in_used, 3 * b)
                    nc.vector.tensor_scalar(sin_in[:, :, :], rest[:, :, :], -PI_IN, PI_IN,
                                            ALU.max, ALU.min).then_inc(reduced, 1)
                if st.has(2):
                    h, n = st.half(2), st.turn(2)
                    b = st.item(2)
                    if st.reuses(2):
                        dve.wait_ge(ring_full[1], 3 * (b - 1))
                    for k in range(KT):
                        dve.wait_ge(xT_full, KT * b + k + 1)
                        nc.vector.tensor_copy(xT_hi[h][:, k, :], ps_t[k][:, :]).then_inc(xT_high, 1)
                    for k in range(KT):
                        dve.wait_ge(xT_high, KT * b + k + 1)
                        nc.vector.tensor_tensor(xT_lo[h][:, k, :], ps_t[k][:, :], xT_hi[h][:, k, :].bitcast(F32),
                                                ALU.subtract).then_inc(xT_copied, 1)
                if st.has(3):
                    h, n, b = st.half(3), st.turn(3), st.item(3)
                    dve.wait_ge(xin_loaded[h], 16 * (n + 1))
                    for t in range(TT):
                        nc.vector.bn_stats(stats[:, t, :], xin[h][:, t, :])
                    dve.drain()
                    for t in range(TT):
                        ins = nc.vector.bn_aggr(mv[h][:, t, :], stats[:, t, :])
                    ins.then_inc(mv_done, 1)
                    dve.wait_ge(mv_done, b + 1)
                    nc.vector.tensor_scalar(var_eps[h][:, :], mv[h][:, :, 1], EPS, None,
                                            ALU.add).then_inc(var_done, 1)
                if st.has(0):
                    h, n, b = st.half(0), st.turn(0), st.item(0)
                    dve.wait_ge(xres_loaded[h], 16 * (n + 1))
                    if st.reuses(0):
                        dve.wait_ge(stored[h], 16 * n)
                    for t in range(TT):
                        r = t % 2
                        dve.wait_ge(out_full[r], 2 * b + t // 2 + 1)
                        nc.vector.reciprocal(rden[:, t:t + 1], ps_o[r][:, D:D + 1]).then_inc(rden_done, 1)
                        dve.wait_ge(rden_done, TT * b + t + 1)
                        ins = nc.vector.scalar_tensor_tensor(out=xout[h][:, t, :], in0=ps_o[r][:, 0:D],
                                                             scalar=rden[:, t:t + 1], in1=xres[h][:, t, :],
                                                             op0=ALU.mult, op1=ALU.add)
                        ins.then_inc(out_free[r], 1)
                if st.has(3):
                    h, n, b = st.half(3), st.turn(3), st.item(3)
                    dve.wait_ge(rstd_done, b + 1)
                    if st.reuses(3):
                        dve.wait_ge(xT_full, KT * (b - 1))
                    for t in range(TT):
                        ins = nc.vector.tensor_scalar(xn[h][:, t, :], xin[h][:, t, :], mv[h][:, t, 0:1],
                                                      rstd[h][:, t:t + 1], ALU.subtract, ALU.mult)
                        ins.then_inc(xn_ready, 1)

            run_steps(dve, emit, NB, 3)

        @block.scalar
        def _(act):
            act.wait_ge(shift_set, 5)

            def emit(st):
                if st.has(1):
                    b = st.item(1)
                    act.wait_ge(reduced, 5 * b)
                    for f in range(NF):
                        r = f % 2
                        act.wait_ge(ring_full[r], 3 * b + f // 2 + 1)
                        nc.scalar.activation(theta[:, f, :], ring[r][:, :], ACT.Identity,
                                             bias=shift[:, f:f + 1], scale=wl_c[:, f:f + 1])\
                            .then_inc(ring_free[r], 1)
                if st.has(0):
                    h, n, b = st.half(0), st.turn(0), st.item(0)
                    if st.reuses(0):
                        act.wait_ge(out_full[1], 2 * (b - 1))
                    for t in range(TT):
                        act.wait_ge(sim_full, TT * b + t + 1)
                        nc.scalar.activation(probs[h][:, t, :], ps_s[t % 2][:, :], ACT.Exp,
                                             scale=1.0 / math.sqrt(D)).then_inc(probs_ready, 1)
                if st.has(1):
                    h, n, b = st.half(1), st.turn(1), st.item(1)
                    if st.reuses(1):
                        act.wait_ge(sim_full, TT * (b - 1))
                    act.wait_ge(reduced, 5 * b + 5)
                    if st.has(0):
                        act.wait_ge(sin_low, b)
                        act.wait_ge(cos_low, b)
                    nc.scalar.activation(trig[:, 0:NF, :], sin_in[:, :, :], ACT.Sin).then_inc(trig_in_used, 1)
                    nc.scalar.activation(cos_in[:, :, :], sin_in[:, :, :], ACT.Abs).then_inc(trig_in_used, 1)
                    act.wait_ge(trig_in_used, 3 * b + 2)
                    nc.scalar.activation(trig[:, NF:2 * NF, :], cos_in[:, :, :], ACT.Sin, bias=half_pi[:, 0:1],
                                         scale=-1.0).then_inc(trig_in_used, 1)
                    nc.scalar.activation(trig_hi[h][:, 0:NF, :], trig[:, 0:NF, :], ACT.Copy)\
                        .then_inc(trig_high, 1)
                    act.wait_ge(trig_in_used, 3 * b + 3)
                    nc.scalar.activation(trig_hi[h][:, NF:2 * NF, :], trig[:, NF:2 * NF, :], ACT.Copy)\
                        .then_inc(trig_high, 1)

            run_steps(act, emit, NB, 3)

        @block.tensor
        def _(pe):
            pe.wait_ge(w_loaded, 7 * 16)
            pe.wait_ge(w_split, 1)

            def take(st, use):
                r = use % 2
                pe.wait_ge(ring_free[r], 3 * st.item(1) + use // 2)
                return r

            def emit(st):
                if st.has(1):
                    h, b = st.half(1), st.item(1)
                    pe.wait_ge(xT_copied, KT * (b + 1))
                    parts = [(wp, xp, k) for wp, xp in ((w_hi, xT_hi[h]), (w_lo, xT_hi[h]), (w_hi, xT_lo[h]))
                             for k in range(KT)]
                    for f in range(NF):
                        r = take(st, f)
                        for i, (wp, xp, k) in enumerate(parts):
                            ins = nc.tensor.matmul(ring[r][:, :], wp[:, k, f * P:(f + 1) * P], xp[:, k, :],
                                                   start=(i == 0), stop=(i == len(parts) - 1))
                        ins.then_inc(ring_full[r], 1)
                    for v in range(2):
                        r = take(st, NF + v)
                        for u in range(2):
                            t = 2 * v + u
                            for i, (wp, xp, k) in enumerate(parts):
                                ins = nc.tensor.matmul(ring[r][:, u * D:(u + 1) * D],
                                                       xp[:, k, t * P:(t + 1) * P], wp[:, k, 2 * D:3 * D],
                                                       start=(i == 0), stop=(i == len(parts) - 1))
                        ins.then_inc(ring_full[r], 1)
                if st.has(0):
                    h, n, b = st.half(0), st.turn(0), st.item(0)
                    pe.wait_ge(sin_low, b + 1)
                    pe.wait_ge(cos_low, b + 1)
                    high, low = trig_hi[h], trig_lo[h]
                    steps = [(keys, queries, f) for keys, queries in ((high, high), (high, low), (low, high))
                             for f in (*range(KT), *range(NF, NF + KT))]
                    for t in range(TT):
                        if t >= 2:
                            pe.wait_ge(probs_ready, TT * b + t - 1)
                        for i, (keys, queries, f) in enumerate(steps):
                            ins = nc.tensor.matmul(ps_s[t % 2][:, :], keys[:, KT + f, t * P:(t + 1) * P],
                                                   queries[:, f, :], start=(i == 0), stop=(i == len(steps) - 1))
                        ins.then_inc(sim_full, 1)
                if st.has(2):
                    h, b = st.half(2), st.item(2)
                    pe.wait_ge(xn_ready, TT * (b + 1))
                    for k in range(KT):
                        if st.has(1):
                            pe.wait_ge(xT_copied, KT * (b - 1) + k + 1)
                        for t in range(TT):
                            ins = nc.tensor.transpose(ps_t[k][:, t * P:(t + 1) * P],
                                                      xn[h][:, t, k * P:(k + 1) * P], id_sb[:, :])
                        ins.then_inc(xT_full, 1)
                if st.has(0):
                    h, b = st.half(0), st.item(0)
                    pe.wait_ge(probs_ready, TT * (b + 1))
                    for r in range(2):
                        pe.wait_ge(ring_free[r], 3 * b + 3)
                    for s in range(TT):
                        r = s % 2
                        pe.wait_ge(out_free[r], 2 * b + s // 2)
                        for t in range(TT):
                            ins = nc.tensor.matmul(ps_o[r][:, 0:D + 1], probs[h][:, t, s * P:(s + 1) * P],
                                                   vals[h][:, t, :], start=(t == 0), stop=(t == TT - 1))
                        ins.then_inc(out_full[r], 1)

            run_steps(pe, emit, NB, 3)



def expert_ffn(nc, tag, x, weights, indices, experts, w1aT, w1b, w2aT, w2b, ident):
    D = x.shape[2]
    TOK, TOPK = weights.shape
    ER, FF = w1b.shape
    E = experts.shape[1]
    R = ER // E
    GRP = 512
    NG, TT, KT = TOK // GRP, GRP // P, D // P
    PAIRS, FT = ER // P, FF // P
    NT = TOK // P
    UPS = PAIRS * FT
    UB = 3
    xf = x.rearrange("b s d -> (b s) d")
    with ExitStack() as ctx:
        def sb(name, shape, dt=F32, stage=None):
            return (stage or ctx).enter_context(nc.sbuf_tensor(tag + name, shape, dt))

        def sem(name):
            return ctx.enter_context(nc.semaphore(tag + name))

        x_all = sb("x_all", [P, NT, D])
        xT_all = sb("xT_all", [P, KT, TOK])
        gate_all = sb("gate_all", [P, PAIRS, TOK])
        w_1a = sb("w_1a", [P, KT, E, 2, R])
        w_hi = sb("w_hi", [P, E, FF], F32R)
        w_lo = sb("w_lo", [P, E, FF], F32R)
        w_2a = sb("w_2a", [P, FT, ER])
        w_2b = sb("w_2b", [P, PAIRS, D])
        ps_up = [ctx.enter_context(nc.psum_tensor(f"{tag}ps_up{u}", [P, 2, 512], F32)) for u in range(UB)]
        ps_c = ctx.enter_context(nc.psum_tensor(tag + "ps_c", [P, 512], F32))
        ps_y = ctx.enter_context(nc.psum_tensor(tag + "ps_y", [P, 512], F32))
        T_BANK = [ps_up[0][:, k, :] for k in range(KT)]
        G_BANK = [ps_up[1 + p // 2][:, p % 2, :] for p in range(PAIRS)]

        x_loaded = [sem(f"x_loaded{g}") for g in range(NG)]
        w_loaded = sem("w_loaded")
        w2_loaded = sem("w2_loaded")
        raw_loaded = [sem(f"raw_loaded{r}") for r in range(2)]
        half_set = sem("half_set")
        mv_done = sem("mv_done")
        var_done = sem("var_done")
        rstd_done = sem("rstd_done")
        gate_steps = sem("gate_steps")
        xn_ready = sem("xn_ready")
        gate_x_ready = sem("gate_x_ready")
        xT_full = sem("xT_full")
        xT_ready = sem("xT_ready")
        gate_full = sem("gate_full")
        gate_copied = sem("gate_copied")
        w_high = sem("w_high")
        w_low = sem("w_low")
        a_full = sem("a_full")
        a_high = sem("a_high")
        a_ready = sem("a_ready")
        up_done = sem("up_done")
        gelu_done = sem("gelu_done")
        down_done = sem("down_done")
        c_ready = sem("c_ready")
        y_full = sem("y_full")
        y_ready = sem("y_ready")
        stored = sem("stored")

        with ExitStack() as one:
            id_sb = sb("ident", [P, P], stage=one)
            ex_sb = sb("experts", [P, E], stage=one)
            g_w = sb("g_w", [P, NT, TOPK], stage=one)
            g_i = sb("g_i", [P, NT, TOPK], I32, stage=one)
            g_f = sb("g_f", [P, NT, TOPK], stage=one)
            hit = [sb(f"hit{k}", [P, NT, E], stage=one) for k in range(TOPK)]
            gate = sb("gate", [P, NT, E], stage=one)
            gate_x = sb("gate_x", [P, TT, E, R], stage=one)
            stats = sb("stats", [P, NT, 6], stage=one)
            mv = sb("mv", [P, NT, 2], stage=one)
            var_eps = sb("var_eps", [P, NT], stage=one)
            neg_half = sb("neg_half", [P, NT], stage=one)
            rstd = sb("rstd", [P, NT], stage=one)
            xn = sb("xn", [P, TT, D], stage=one)
            raw = [sb(f"raw{r}", [P, 2, FF], stage=one) for r in range(2)]
            block = one.enter_context(nc.Block())

            @block.sync
            def _(sp):
                sp.dma_start(g_w[:, :, :], weights.rearrange("(t p) k -> p t k", p=P)).then_inc(w_loaded, 16)
                sp.dma_start(g_i[:, :, :], indices.rearrange("(t p) k -> p t k", p=P)).then_inc(w_loaded, 16)
                sp.dma_start(ex_sb[:, :], experts).then_inc(w_loaded, 16)
                sp.dma_start(id_sb[:, :], ident).then_inc(w_loaded, 16)
                for g in range(NG):
                    sp.dma_start(x_all[:, g * TT:(g + 1) * TT, :],
                                 xf[g * GRP:(g + 1) * GRP, :].rearrange("(t p) d -> p t d", p=P))\
                        .then_inc(x_loaded[g], 16)
                for p in range(PAIRS):
                    if p == 2:
                        for half in range(2):
                            for k in range(KT):
                                sp.dma_start(w_1a[:, k, :, half, :],
                                             w1aT[k * P:(k + 1) * P, :].rearrange("p (e r) -> p e r", r=R))\
                                    .then_inc(w2_loaded, 16)
                        sp.dma_start(w_2a[:, :, :], w2aT.rearrange("(q p) e -> p q e", p=P)).then_inc(w2_loaded, 16)
                        sp.dma_start(w_2b[:, :, :], w2b.rearrange("(q p) d -> p q d", p=P)).then_inc(w2_loaded, 16)
                    if p >= 2:
                        sp.wait_ge(w_low, p - 1)
                    for half in range(2):
                        sp.dma_start(raw[p % 2][half * R:(half + 1) * R, :, :],
                                     w1b[p * P:(p + 1) * P, :].rearrange("(e r) f -> r e f", r=R))\
                            .then_inc(raw_loaded[p % 2], 16)

            @block.gpsimd
            def _(pool):
                nc.gpsimd.memset(neg_half[:, :], -0.5).then_inc(half_set, 1)
                pool.wait_ge(half_set, 1)
                pool.wait_ge(var_done, 1)
                nc.gpsimd.tensor_tensor(rstd[:, :], var_eps[:, :], neg_half[:, :], ALU.pow).then_inc(rstd_done, 1)

            @block.vector
            def _(dve):
                dve.wait_ge(w_loaded, 4 * 16)
                nc.vector.tensor_copy(g_f[:, :, :], g_i[:, :, :]).then_inc(gate_steps, 1)
                dve.wait_ge(gate_steps, 1)
                for k in range(TOPK):
                    nc.vector.tensor_tensor(hit[k][:, :, :], ex_sb[:, :].unsqueeze(1).to_broadcast([P, NT, E]),
                                            g_f[:, :, k:k + 1].to_broadcast([P, NT, E]),
                                            ALU.is_equal).then_inc(gate_steps, 1)
                dve.wait_ge(gate_steps, 1 + TOPK)
                for k in range(TOPK):
                    nc.vector.tensor_tensor(hit[k][:, :, :], hit[k][:, :, :],
                                            g_w[:, :, k:k + 1].to_broadcast([P, NT, E]),
                                            ALU.mult).then_inc(gate_steps, 1)
                dve.wait_ge(gate_steps, 1 + 2 * TOPK)
                nc.vector.tensor_tensor(gate[:, :, :], hit[0][:, :, :], hit[1][:, :, :],
                                        ALU.add).then_inc(gate_steps, 1)
                dve.wait_ge(gate_steps, 2 + 2 * TOPK)

                def repeat_gates(g):
                    if g:
                        dve.wait_ge(gate_full, PAIRS * g)
                    nc.vector.tensor_copy(gate_x[:, :, :, :], gate[:, g * TT:(g + 1) * TT, :].unsqueeze(3)
                                          .to_broadcast([P, TT, E, R])).then_inc(gate_x_ready, 1)

                repeat_gates(0)
                for g in range(NG):
                    dve.wait_ge(x_loaded[g], 16)
                    for t in range(TT):
                        nc.vector.bn_stats(stats[:, g * TT + t, :], x_all[:, g * TT + t, :])
                dve.drain()
                for t in range(NT):
                    ins = nc.vector.bn_aggr(mv[:, t, :], stats[:, t, :])
                ins.then_inc(mv_done, 1)
                dve.wait_ge(mv_done, 1)
                nc.vector.tensor_scalar(var_eps[:, :], mv[:, :, 1], EPS, None, ALU.add).then_inc(var_done, 1)
                dve.wait_ge(rstd_done, 1)
                for g in range(NG):
                    if g:
                        dve.wait_ge(xT_full, g)
                    for t in range(TT):
                        n = g * TT + t
                        ins = nc.vector.tensor_scalar(xn[:, t, :], x_all[:, n, :], mv[:, n, 0:1],
                                                      rstd[:, n:n + 1], ALU.subtract, ALU.mult)
                    ins.then_inc(xn_ready, 1)
                    if g + 1 < NG:
                        repeat_gates(g + 1)
                    dve.wait_ge(w_high, g + 1)
                    pair = slice(2 * g, 2 * g + 2)
                    nc.vector.tensor_tensor(w_lo[:, pair, :], raw[g % 2][:, :, :], w_hi[:, pair, :].bitcast(F32),
                                            ALU.subtract).then_inc(w_low, 1)

            @block.scalar
            def _(act):
                def copy_gates(g):
                    for p in range(PAIRS):
                        act.wait_ge(gate_full, PAIRS * g + p + 1)
                        nc.scalar.activation(gate_all[:, p, g * GRP:(g + 1) * GRP], G_BANK[p],
                                             ACT.Copy).then_inc(gate_copied, 1)

                copy_gates(0)
                for g in range(NG):
                    act.wait_ge(raw_loaded[g % 2], 32 * (g // 2 + 1))
                    nc.scalar.activation(w_hi[:, 2 * g:2 * g + 2, :], raw[g % 2][:, :, :], ACT.Copy)\
                        .then_inc(w_high, 1)
                    act.wait_ge(xT_full, g + 1)
                    for k in range(KT):
                        nc.scalar.activation(xT_all[:, k, g * GRP:(g + 1) * GRP], T_BANK[k],
                                             ACT.Copy).then_inc(xT_ready, 1)
                    if g + 1 < NG:
                        copy_gates(g + 1)

            @block.tensor
            def _(pe):
                pe.wait_ge(w_loaded, 4 * 16)

                def spread_gates(g):
                    pe.wait_ge(gate_x_ready, g + 1)
                    for p in range(PAIRS):
                        if g:
                            pe.wait_ge(gate_copied, PAIRS * (g - 1) + p + 1)
                        for t in range(TT):
                            ins = nc.tensor.matmul(G_BANK[p][:, t * P:(t + 1) * P],
                                                   gate_x[:, t, 2 * p:2 * p + 2, :].rearrange("p e r -> p (e r)"),
                                                   id_sb[:, :], start=True, stop=True)
                        ins.then_inc(gate_full, 1)

                spread_gates(0)
                for g in range(NG):
                    pe.wait_ge(xn_ready, g + 1)
                    if g:
                        pe.wait_ge(xT_ready, KT * g)
                    for k in range(KT):
                        for t in range(TT):
                            ins = nc.tensor.transpose(T_BANK[k][:, t * P:(t + 1) * P],
                                                      xn[:, t, k * P:(k + 1) * P], id_sb[:, :])
                    ins.then_inc(xT_full, 1)
                    if g + 1 < NG:
                        spread_gates(g + 1)

        with ExitStack() as two:
            a_split = [sb(f"a_split{h}", [P, 2, GRP], F32R, stage=two) for h in range(2)]
            hid = [sb(f"hid{u}", [P, 2, GRP], stage=two) for u in range(UB)]
            c_sb = sb("c_sb", [P, PAIRS, GRP], stage=two)
            x_new = sb("x_new", [P, TT, D], stage=two)
            Y_BANK = [ps_y[:, 0:D], ps_c[:, 0:D]]
            block = two.enter_context(nc.Block())

            @block.sync
            def _(sp):
                with sp.Fori(0, NG) as g:
                    sp.wait_ge(y_ready, TT * g + TT + 2)
                    sp.dma_start(xf[bass.ds(g * GRP, GRP), :].rearrange("(t p) d -> p t d", p=P),
                                 x_new[:, :, :]).then_inc(stored, 16)
                sp.wait_ge(stored, 16 * NG + 16)

            @block.vector
            def _(dve):
                dve.sem_inc(gelu_done, UB)
                dve.sem_inc(down_done, UB)
                dve.sem_inc(c_ready, 1)
                dve.sem_inc(y_ready, 2)
                dve.sem_inc(a_ready, 1)
                dve.sem_inc(stored, 16)

                def low(g, n):
                    dve.wait_ge(a_high, E * g + n + 1)
                    half = a_split[n // 2 % 2][R:P, n % 2, :]
                    nc.vector.tensor_tensor(half, ps_y[R:P, :], half.bitcast(F32),
                                            ALU.subtract).then_inc(a_ready, 1)

                with dve.Fori(0, NG) as g:
                    low(g, 0)
                    low(g, 1)
                    for p in range(PAIRS):
                        if p < PAIRS - 1:
                            low(g, 2 * p + 2)
                            low(g, 2 * p + 3)
                        dve.wait_ge(down_done, UPS * g + FT * (p + 1) + UB)
                        if p == 0:
                            dve.wait_ge(y_full, TT * g + TT)
                        nc.vector.tensor_tensor(c_sb[:, p, :], ps_c[:, :], gate_all[:, p, bass.ds(g * GRP, GRP)],
                                                ALU.mult).then_inc(c_ready, 1)
                    dve.wait_ge(stored, 16 * g + 16)
                    for t in range(TT):
                        dve.wait_ge(y_full, TT * g + t + 1 + TT)
                        nc.vector.tensor_tensor(x_new[:, t, :], Y_BANK[t % 2],
                                                x_all[:, bass.ds(g * TT + t, 1), :].rearrange("p a d -> p (a d)"),
                                                ALU.add).then_inc(y_ready, 1)

            @block.scalar
            def _(act):
                def high(g, n):
                    act.wait_ge(a_full, E * g + n + 1)
                    act.wait_ge(up_done, UPS * g + FT * (n // 2 - 1) + UPS)
                    nc.scalar.activation(a_split[n // 2 % 2][:, n % 2, :], ps_y[:, :], ACT.Copy)\
                        .then_inc(a_high, 1)

                with act.Fori(0, NG) as g:
                    high(g, 0)
                    high(g, 1)
                    for k in range(UPS):
                        p, f, u = k // FT, k % FT, k % UB
                        act.wait_ge(up_done, UPS * g + k + 1 + UPS)
                        act.wait_ge(down_done, UPS * g + k + 1)
                        nc.scalar.activation(hid[u][:, :, :], ps_up[u][:, :, :], ACT.Gelu).then_inc(gelu_done, 1)
                        if p < PAIRS - 1 and f in (1, 4):
                            high(g, 2 * p + 2 + f // 4)

            @block.tensor
            def _(pe):
                pe.sem_inc(up_done, UPS)
                pe.sem_inc(y_full, TT)
                pe.wait_ge(w2_loaded, 6 * 16)

                def ranks(g, n):
                    pe.wait_ge(a_ready, E * g + n + 1)
                    if n == 0:
                        pe.wait_ge(y_ready, TT * g + 2)
                    for k in range(KT):
                        ins = nc.tensor.matmul(ps_y[:, :], w_1a[:, k, n, :, :].rearrange("p h r -> p (h r)"),
                                               xT_all[:, k, bass.ds(g * GRP, GRP)],
                                               start=(k == 0), stop=(k == KT - 1))
                    ins.then_inc(a_full, 1)

                def up(g, k):
                    p, f, u = k // FT, k % FT, k % UB
                    pe.wait_ge(gelu_done, UPS * g + k + 1)
                    if f == 0:
                        pe.wait_ge(a_ready, E * g + 2 * p + 3)
                    for e in range(2):
                        for part in (w_hi, w_lo):
                            ins = nc.tensor.matmul(ps_up[u][:, e, :], part[:, 2 * p + e, f * P:(f + 1) * P],
                                                   a_split[p % 2][:, e, :], start=(part is w_hi),
                                                   stop=(part is w_lo))
                    ins.then_inc(up_done, 1)

                def down(g, k):
                    p, f, u = k // FT, k % FT, k % UB
                    pe.wait_ge(gelu_done, UPS * g + k + 1 + UB)
                    if f == 0:
                        pe.wait_ge(c_ready, PAIRS * g + p + 1)
                        if p == 0:
                            pe.wait_ge(y_ready, TT * g + 2)
                    for e in range(2):
                        cols = slice(p * P + e * R, p * P + (e + 1) * R)
                        ins = nc.tensor.matmul(ps_c[e * R:(e + 1) * R, :], w_2a[:, f, cols], hid[u][:, e, :],
                                               start=(f == 0), stop=(f == FT - 1), skip_group_check=True)
                    ins.then_inc(down_done, 1)

                with pe.Fori(0, NG) as g:
                    ranks(g, 0)
                    ranks(g, 1)
                    up(g, 0)
                    up(g, 1)
                    for k in range(UPS):
                        if k + 2 < UPS:
                            up(g, k + 2)
                        down(g, k)
                        if k // FT < PAIRS - 1 and k % FT in (0, 3):
                            ranks(g, 2 * (k // FT) + 2 + k % FT // 3)
                    pe.wait_ge(c_ready, PAIRS * (g + 1) + 1)
                    for t in range(TT):
                        pe.wait_ge(y_ready, TT * g + t + 1)
                        for p in range(PAIRS):
                            ins = nc.tensor.matmul(Y_BANK[t % 2], c_sb[:, p, t * P:(t + 1) * P],
                                                   w_2b[:, p, :], start=(p == 0), stop=(p == PAIRS - 1))
                        ins.then_inc(y_full, 1)


def mamba(nc, x_in, out, w_in, conv_w, conv_b, norm_w, w_x, w_dt, b_dt, a_log, d_skip, w_out,
          pick_bc, sum_n, ident):
    NB, S, D = x_in.shape
    DI = w_out.shape[0]
    K = conv_w.shape[2]
    R = w_dt.shape[0]
    RX = w_x.shape[1]
    N = (RX - R) // 2
    TT, KT, CT = S // P, D // P, DI // P
    CH = 32
    Q = P // CH
    G = N // Q
    BLK = DI // CH
    BPT = BLK // CT
    PAD = K - 1
    RING = 4
    FB = 4
    U_AT, V_AT, Z_AT = [2, 3, 5, 7], [3, 6, 7, 8], [5, 7, 9, 9]
    X_AT, DT_AT, BC_AT = 10, 11, 12
    F_T = 0
    order = [(kind, c) for q in range(BLK) for kind, at in (("U", U_AT), ("V", V_AT), ("Z", Z_AT))
             for c in range(CT) if at[c] == q]
    F_U, F_V, F_Z = [[KT + order.index((kind, c)) for c in range(CT)] for kind in ("U", "V", "Z")]
    F_X = KT + len(order)
    F_DT = F_X + 1
    F_BC = F_DT + CT
    F_ALL = F_BC + 2 * G
    F_PER = [len(range(r, F_ALL, FB)) for r in range(FB)]
    with ExitStack() as ctx:
        def sb(name, shape, dt=F32):
            return ctx.enter_context(nc.sbuf_tensor("m_" + name, shape, dt))

        def sem(name):
            return ctx.enter_context(nc.semaphore("m_" + name))

        def bank(name):
            return ctx.enter_context(nc.psum_tensor("m_" + name, [P, 512], F32))

        win = sb("win", [P, KT, 2 * DI])
        wx = sb("wx", [P, CT, RX])
        wdt = sb("wdt", [RX, DI])
        wout = sb("wout", [P, CT, D])
        cw = sb("cw", [P, CT, K])
        cb = sb("cb", [P, CT])
        tap = sb("tap", [P, CT, K, P])
        nw = sb("nw", [P, KT])
        bdt = sb("bdt", [P, CT])
        dsk = sb("dsk", [P, CT])
        nega = sb("nega", [P, BLK, G])
        pick_s = sb("pick_s", [RX, 2 * G, P])
        sum_q = sb("sum_q", [P, CH])
        id_sb = sb("ident", [P, P])
        neg_half = sb("neg_half", [P, TT])
        xin = sb("xin", [P, TT, D])
        xl = sb("xl", [P, TT, D])
        x_new = sb("x_new", [P, TT, D])
        stats = sb("stats", [P, TT, 6])
        mv = sb("mv", [P, TT, 2])
        var_eps = sb("var_eps", [P, TT])
        rstd = sb("rstd", [P, TT])
        ms_eps = sb("ms_eps", [P, TT])
        rrms = sb("rrms", [P, TT])
        hT = sb("hT", [P, KT, S])
        fr1 = sb("fr1", [P, 2, PAD + S])
        fr2 = sb("fr2", [P, 2, S])
        fr3 = sb("fr3", [P, 2, S])
        xd = sb("xd", [RX, S])
        dt_sb = [sb(f"dt{h}", [P, CT, S]) for h in range(2)]
        du_sb = [sb(f"du{r}", [P, CT // 2, S]) for r in range(3)]
        u_sb = [sb(f"u{h}", [P, CT, S]) for h in range(2)]
        z_sb = [sb(f"z{h}", [P, CT, S]) for h in range(2)]
        bc_sb = [sb(f"bc{h}", [P, 2 * G, S]) for h in range(2)]
        dt_rep = [sb(f"dt_rep{r}", [P, S]) for r in range(2)]
        du_rep = [sb(f"du_rep{r}", [P, S]) for r in range(2)]
        decay = [sb(f"decay{r}", [P, G, S]) for r in range(2)]
        state = [sb(f"state{r}", [P, G, S]) for r in range(RING)]
        ps_y = [bank(f"ps_y{r}") for r in range(2)]
        ps_o = [bank(f"ps_o{r}") for r in range(2)]
        ps_f = [bank(f"ps_f{r}") for r in range(FB)]

        w_loaded = sem("w_loaded")
        a_ready = sem("a_ready")
        scaled = sem("scaled")
        half_set = sem("half_set")
        xin_loaded = sem("xin_loaded")
        mv_done = sem("mv_done")
        var_done = sem("var_done")
        rstd_done = sem("rstd_done")
        ms_done = sem("ms_done")
        rrms_done = sem("rrms_done")
        xl_ready = sem("xl_ready")
        res_ready = sem("res_ready")
        res_stored = sem("res_stored")
        xh_ready = sem("xh_ready")
        f_full = [sem(f"f_full{r}") for r in range(FB)]
        f_free = [sem(f"f_free{r}") for r in range(FB)]
        hT_ready = sem("hT_ready")
        u_tanh = sem("u_tanh")
        u_ready = sem("u_ready")
        z_tanh = sem("z_tanh")
        z_ready = sem("z_ready")
        xd_ready = sem("xd_ready")
        sp_in = sem("sp_in")
        sp_exp = sem("sp_exp")
        sp_ln = sem("sp_ln")
        sp_w = sem("sp_w")
        sp_steps = sem("sp_steps")
        du_ready = sem("du_ready")
        dt_ready = sem("dt_ready")
        bc_ready = sem("bc_ready")
        dt_spread = [sem(f"dt_spread{r}") for r in range(2)]
        du_spread = [sem(f"du_spread{r}") for r in range(2)]
        decay_ready = sem("decay_ready")
        drive_ready = sem("drive_ready")
        scanned = sem("scanned")
        weighed = sem("weighed")
        summed = sem("summed")
        y_read = sem("y_read")
        y_skip = sem("y_skip")
        gated = sem("gated")
        o_full = sem("o_full")
        o_read = sem("o_read")
        res_back = sem("res_back")
        stored = sem("stored")
        NW = 15

        def rows(t, b):
            return t[bass.ds(b, 1), :, :].rearrange("a (t p) d -> p (a t) d", p=P)

        def du_pair(h, i):
            return du_sb[1 + h if i else 0]

        def f_count(b, use):
            return F_PER[use % FB] * b + use // FB + 1

        def f_read(b, use):
            return len(range(use % FB, F_BC, FB)) * b + use // FB + 1

        def spread(b, q):
            return 16 * (BLK // 2 * b + q // 2 + 1)

        block = ctx.enter_context(nc.Block())

        @block.sync
        def _(sp):
            for dst, src in ((id_sb[:, :], ident), (win[:, :, :], w_in.rearrange("(k p) e -> p k e", p=P)),
                             (wx[:, :, :], w_x.rearrange("(k p) e -> p k e", p=P)),
                             (wdt[0:R, :], w_dt), (wout[:, :, :], w_out.rearrange("(k p) e -> p k e", p=P)),
                             (cw[:, :, :], conv_w), (cb[:, :], conv_b), (nw[:, :], norm_w), (bdt[:, :], b_dt),
                             (dsk[:, :], d_skip), (nega[:, :, :], a_log), (pick_s[:, :, :], pick_bc), (sum_q[:, :], sum_n)):
                sp.dma_start(dst, src).then_inc(w_loaded, 16)

            def spread_block(st, o, q):
                h, b = st.half(o), st.item(o)
                c, r = BLK * b + q, q % 2
                rows_q = slice(CH * (q % BPT), CH * (q % BPT) + CH)
                again = q >= 2 or st.has(o - 1)
                if q % (BLK // 2) == 0:
                    sp.wait_ge(dt_ready, 2 * b + q // (BLK // 2) + 1)
                if again:
                    sp.wait_ge(decay_ready, G * (c - 1))
                sp.dma_start(dt_rep[r][:, :], dt_sb[h][rows_q, q // BPT, :].unsqueeze(1).to_broadcast([CH, Q, S]))\
                    .then_inc(dt_spread[r], 16)
                if q % (BLK // 2) == 0:
                    sp.wait_ge(du_ready, 2 * b + q // (BLK // 2) + 1)
                if again:
                    sp.wait_ge(drive_ready, c - 1)
                sp.dma_start(du_rep[r][:, :],
                             du_pair(h, q // BPT // 2)[rows_q, q // BPT % 2, :].unsqueeze(1).to_broadcast([CH, Q, S]))\
                    .then_inc(du_spread[r], 16)

            def emit(st):
                if st.has(0) and not st.has(-1):
                    spread_block(st, 0, 0)
                    spread_block(st, 0, 1)
                for q in range(BLK):
                    if q < BLK - 2 and st.has(0):
                        spread_block(st, 0, q + 2)
                    if q >= BLK - 2 and st.has(1) and st.has(0):
                        spread_block(st, 1, q + 2 - BLK)
                    if q == 10 and st.has(2):
                        sp.wait_ge(res_ready, st.item(2) + 1)
                        sp.dma_start(rows(out, st.item(2)), xin[:, :, :]).then_inc(res_stored, 16)
                    if q == 1 and st.has(-1):
                        b = st.item(-1)
                        sp.wait_ge(res_stored, 16 * (b + 1))
                        if st.has(-2):
                            sp.wait_ge(stored, 16 * b)
                        sp.dma_start(x_new[:, :, :], rows(out, b)).then_inc(res_back, 16)
                    if q == 13 and st.has(3):
                        if st.has(2):
                            sp.wait_ge(res_stored, 16 * st.item(3))
                        sp.dma_start(xin[:, :, :], rows(x_in, st.item(3))).then_inc(xin_loaded, 16)
                    if q == 9 and st.has(-1):
                        sp.wait_ge(o_read, 2 * (st.item(-1) + 1))
                        sp.dma_start(rows(out, st.item(-1)), x_new[:, :, :]).then_inc(stored, 16)

            run_steps(sp, emit, NB, 3, 1)
            sp.wait_ge(stored, 16 * NB)

        @block.gpsimd
        def _(pool):
            nc.gpsimd.memset(neg_half[:, :], -0.5).then_inc(half_set, 1)
            pool.wait_ge(half_set, 1)

            def emit(st):
                for q in range(BLK):
                    if st.has(0):
                        h, b = st.half(0), st.item(0)
                        c = BLK * b + q
                        pool.wait_ge(scanned, c + 1)
                        if q == 0:
                            pool.wait_ge(bc_ready, 2 * G * (b + 1))
                        s = state[q % RING]
                        nc.gpsimd.tensor_tensor(s[:, :, :], s[:, :, :], bc_sb[h][:, G:2 * G, :],
                                                ALU.mult).then_inc(weighed, 1)
                    if st.has(1) and DT_AT + 1 <= q < DT_AT + 3:
                        h, b, i = st.half(1), st.item(1), q - DT_AT - 1
                        pair = slice(2 * i, 2 * i + 2)
                        pool.wait_ge(dt_ready, 2 * b + i + 1)
                        nc.gpsimd.tensor_tensor(du_pair(h, i)[:, :, :], dt_sb[h][:, pair, :], u_sb[h][:, pair, :],
                                                ALU.mult).then_inc(du_ready, 1)
                    if st.has(0) and q in (7, 11, 15):
                        h, c = st.half(0), (q - 7) // 4
                        pool.wait_ge(y_read, CT * st.item(0) + c + 1)
                        nc.gpsimd.tensor_tensor(u_sb[h][:, c, :], u_sb[h][:, c, :], z_sb[h][:, c, :],
                                                ALU.mult).then_inc(gated, 1)
                    if st.has(2) and q == 8:
                        pool.wait_ge(xl_ready, st.item(2) + 1)
                        nc.gpsimd.tensor_tensor(xin[:, :, :], xin[:, :, :], xl[:, :, :],
                                                ALU.add).then_inc(res_ready, 1)
                    if st.has(2) and q == 0:
                        pool.wait_ge(var_done, st.item(2) + 1)
                        nc.gpsimd.tensor_tensor(rstd[:, :], var_eps[:, :], neg_half[:, :],
                                                ALU.pow).then_inc(rstd_done, 1)
                    if st.has(2) and q == 2:
                        pool.wait_ge(ms_done, 3 * (st.item(2) + 1))
                        if st.has(1):
                            pool.wait_ge(xh_ready, TT * st.item(2))
                        nc.gpsimd.tensor_tensor(rrms[:, :], ms_eps[:, :], neg_half[:, :],
                                                ALU.pow).then_inc(rrms_done, 1)

            run_steps(pool, emit, NB, 2, 1)

        @block.vector
        def _(dve):
            dve.wait_ge(w_loaded, 16 * 13)
            nc.vector.memset(wdt[R:RX, :], 0.0).then_inc(scaled, 1)
            nc.vector.memset(fr1[:, :, 0:PAD], 0.0).then_inc(scaled, 1)
            for r in range(2):
                nc.vector.memset(decay[r][:, :, 0:1], 0.0).then_inc(scaled, 1)
            nc.vector.tensor_scalar(cw[:, :, :], cw[:, :, :], 0.5, None, ALU.mult).then_inc(scaled, 1)
            nc.vector.tensor_scalar(cb[:, :], cb[:, :], 0.5, None, ALU.mult).then_inc(scaled, 1)
            nc.vector.tensor_scalar(win[:, :, DI:2 * DI], win[:, :, DI:2 * DI], 0.5, None,
                                    ALU.mult).then_inc(scaled, 1)
            dve.wait_ge(scaled, 5)
            for c in range(CT):
                for k in range(K):
                    nc.vector.tensor_scalar(tap[:, c, k, :], id_sb[:, :], cw[:, c, k:k + 1], None,
                                            ALU.mult).then_inc(scaled, 1)
            dve.wait_ge(a_ready, 1)
            nc.vector.tensor_scalar(nega[:, :, :], nega[:, :, :], -1.0, None, ALU.mult).then_inc(scaled, 1)

            def front(st, q):
                h, b = st.half(1), st.item(1)
                if 6 <= q < 6 + CT:
                    c = q - 6
                    r = c % 2
                    if c == 0 and st.reuses(1):
                        dve.wait_ge(o_full, 2 * (b - 1))
                    dve.wait_ge(u_tanh, CT * b + c + 1)
                    nc.vector.scalar_tensor_tensor(out=u_sb[h][:, c, :], in0=fr3[:, r, :], scalar=1.0,
                                                   in1=fr2[:, r, :], op0=ALU.add,
                                                   op1=ALU.mult).then_inc(u_ready, 1)
                for c in range(CT):
                    if Z_AT[c] + 1 == q:
                        use = F_Z[c]
                        dve.wait_ge(z_tanh, CT * b + c + 1)
                        nc.vector.scalar_tensor_tensor(out=z_sb[h][:, c, :], in0=z_sb[h][:, c, :], scalar=1.0,
                                                       in1=ps_f[use % FB][:, :], op0=ALU.add,
                                                       op1=ALU.mult).then_inc(f_free[use % FB], 1)
                if DT_AT + 1 <= q < DT_AT + 3:
                    i = q - DT_AT - 1
                    n = 2 * b + i
                    w = fr1[:, :, PAD:PAD + S]
                    dve.wait_ge(sp_w, n + 1)
                    nc.vector.scalar_tensor_tensor(out=w, in0=w, scalar=1.0, in1=fr2[:, :, :],
                                                   op0=ALU.subtract, op1=ALU.subtract).then_inc(sp_steps, 1)
                    dve.wait_ge(sp_steps, 2 * n + 1)
                    dve.wait_ge(sp_ln, n + 1)
                    nc.vector.tensor_tensor(w, fr3[:, :, :], w, ALU.subtract).then_inc(sp_steps, 1)
                    dve.wait_ge(sp_steps, 2 * n + 2)
                    nc.vector.scalar_tensor_tensor(out=dt_sb[h][:, 2 * i:2 * i + 2, :], in0=hT[:, :, :], scalar=0.0,
                                                   in1=w, op0=ALU.max, op1=ALU.add).then_inc(dt_ready, 1)

            def norm(st, q):
                b = st.item(2)
                if q == 0:
                    dve.wait_ge(xin_loaded, 16 * (b + 1))
                    for t in range(TT):
                        nc.vector.bn_stats(stats[:, t, :], xin[:, t, :])
                    dve.drain()
                    for t in range(TT):
                        ins = nc.vector.bn_aggr(mv[:, t, :], stats[:, t, :])
                    ins.then_inc(mv_done, 1)
                    dve.wait_ge(mv_done, b + 1)
                    nc.vector.tensor_scalar(var_eps[:, :], mv[:, :, 1], EPS, None, ALU.add).then_inc(var_done, 1)
                if q == 2:
                    dve.wait_ge(rstd_done, b + 1)
                    nc.vector.tensor_tensor(ms_eps[:, :], rstd[:, :], rstd[:, :], ALU.mult).then_inc(ms_done, 1)
                    dve.wait_ge(ms_done, 3 * b + 1)
                    nc.vector.tensor_tensor(ms_eps[:, :], ms_eps[:, :], mv[:, :, 1], ALU.mult).then_inc(ms_done, 1)
                    dve.wait_ge(ms_done, 3 * b + 2)
                    nc.vector.tensor_scalar(ms_eps[:, :], ms_eps[:, :], EPS, None, ALU.add).then_inc(ms_done, 1)
                    if st.has(1):
                        dve.wait_ge(f_full[1], f_count(b - 1, F_T + 1))
                    for t in range(TT):
                        ins = nc.vector.tensor_scalar(xl[:, t, :], xin[:, t, :], mv[:, t, 0:1], rstd[:, t:t + 1],
                                                      ALU.subtract, ALU.mult)
                    ins.then_inc(xl_ready, 1)

            def read_y(st, o, c):
                h, b = st.half(o), st.item(o)
                n = CT * b + c
                dve.wait_ge(summed, BLK // 2 * b + BPT // 2 * (c + 1))
                nc.vector.scalar_tensor_tensor(out=u_sb[h][:, c, :], in0=u_sb[h][:, c, :], scalar=dsk[:, c:c + 1],
                                               in1=ps_y[c % 2][:, :], op0=ALU.mult, op1=ALU.add).then_inc(y_read, 1)
                if c < CT - 1:
                    return
                dve.wait_ge(y_read, n + 1)
                nc.vector.tensor_tensor(u_sb[h][:, c, :], u_sb[h][:, c, :], z_sb[h][:, c, :],
                                        ALU.mult).then_inc(gated, 1)

            def emit(st):
                for q in range(BLK):
                    if st.has(0):
                        h, b = st.half(0), st.item(0)
                        c = BLK * b + q
                        s = state[q % RING]
                        dve.wait_ge(du_spread[q % 2], spread(b, q))
                        if q == 0:
                            dve.wait_ge(bc_ready, 2 * G * b + G)
                        if q >= RING or st.has(-1):
                            dve.wait_ge(summed, BLK // 2 * b + (q - RING) // 2 + 1)
                        nc.vector.tensor_tensor(s[:, :, :], du_rep[q % 2][:, :].unsqueeze(1).to_broadcast([P, G, S]),
                                                bc_sb[h][:, 0:G, :], ALU.mult).then_inc(drive_ready, 1)
                        dve.wait_ge(drive_ready, c + 1)
                        dve.wait_ge(decay_ready, G * (c + 1))
                        flat = s[:, :, :].rearrange("p g t -> p (g t)")
                        nc.vector.tensor_tensor_scan(flat, decay[q % 2][:, :, :].rearrange("p g t -> p (g t)"),
                                                     flat, 0.0, ALU.mult, ALU.add).then_inc(scanned, 1)
                    if q in (7, 11, 15) and st.has(0):
                        read_y(st, 0, (q - 7) // 4)
                    if q == 3 and st.has(-1):
                        read_y(st, -1, CT - 1)
                    if st.has(-1) and q in (5, 6):
                        b = st.item(-1)
                        v = q - 5
                        dve.wait_ge(res_back, 16 * (b + 1))
                        dve.wait_ge(o_full, 2 * b + v + 1)
                        nc.vector.tensor_tensor(x_new[:, 2 * v:2 * v + 2, :], x_new[:, 2 * v:2 * v + 2, :],
                                                ps_o[v][:, :].rearrange("p (t d) -> p t d", d=D),
                                                ALU.add).then_inc(o_read, 1)
                    if st.has(1):
                        front(st, q)
                    if st.has(2):
                        norm(st, q)

            run_steps(dve, emit, NB, 2, 1)

        @block.scalar
        def _(act):
            act.wait_ge(w_loaded, 16 * 13)
            nc.scalar.activation(nega[:, :, :], nega[:, :, :], ACT.Exp).then_inc(a_ready, 1)
            act.wait_ge(scaled, 8 + CT * K)

            def front(st, q):
                h, b = st.half(1), st.item(1)
                if q == 1:
                    for k in range(KT):
                        use = F_T + k
                        act.wait_ge(f_full[use % FB], f_count(b, use))
                        if k == 0 and st.has(0):
                            act.wait_ge(dt_ready, 2 * b)
                        nc.scalar.activation(hT[:, k, :], ps_f[use % FB][:, :], ACT.Copy,
                                             scale=nw[:, k:k + 1]).then_inc(f_free[use % FB], 1)
                if q in U_AT:
                    c = U_AT.index(q)
                    use = F_U[c]
                    act.wait_ge(f_full[use % FB], f_count(b, use))
                    nc.scalar.activation(fr1[:, c % 2, PAD:PAD + S], ps_f[use % FB][:, :],
                                         ACT.Copy).then_inc(f_free[use % FB], 1)
                if q in V_AT:
                    c = V_AT.index(q)
                    r = c % 2
                    use = F_V[c]
                    act.wait_ge(f_full[use % FB], f_count(b, use))
                    if c >= 2:
                        act.wait_ge(u_ready, CT * b + c - 1)
                    nc.scalar.activation(fr2[:, r, :], ps_f[use % FB][:, :], ACT.Identity,
                                         bias=cb[:, c:c + 1]).then_inc(f_free[use % FB], 1)
                    act.wait_ge(f_free[use % FB], f_read(b, use))
                    nc.scalar.activation(fr3[:, r, :], fr2[:, r, :], ACT.Tanh).then_inc(u_tanh, 1)
                for c in range(CT):
                    if Z_AT[c] == q:
                        use = F_Z[c]
                        act.wait_ge(f_full[use % FB], f_count(b, use))
                        if c == 0 and st.reuses(1):
                            act.wait_ge(gated, CT * (b - 1))
                        nc.scalar.activation(z_sb[h][:, c, :], ps_f[use % FB][:, :], ACT.Tanh).then_inc(z_tanh, 1)
                if q == X_AT:
                    use = F_X
                    act.wait_ge(f_full[use % FB], f_count(b, use))
                    if st.has(0):
                        act.wait_ge(bc_ready, 2 * G * b)
                    nc.scalar.activation(xd[:, :], ps_f[use % FB][0:RX, :], ACT.Copy).then_inc(f_free[use % FB], 1)
                if DT_AT <= q < DT_AT + 2:
                    i = q - DT_AT
                    n = 2 * b + i
                    for k in range(2):
                        c = 2 * i + k
                        use = F_DT + c
                        act.wait_ge(f_full[use % FB], f_count(b, use))
                        if i:
                            act.wait_ge(dt_ready, 2 * b + 1)
                        nc.scalar.activation(hT[:, k, :], ps_f[use % FB][:, :], ACT.Identity,
                                             bias=bdt[:, c:c + 1]).then_inc(f_free[use % FB], 1)
                    for k in range(2):
                        use = F_DT + 2 * i + k
                        act.wait_ge(f_free[use % FB], f_read(b, use))
                    nc.scalar.activation(fr2[:, :, :], hT[:, :, :], ACT.Abs).then_inc(sp_in, 1)
                    act.wait_ge(sp_in, n + 1)
                    nc.scalar.activation(fr2[:, :, :], fr2[:, :, :], ACT.Exp, scale=-1.0).then_inc(sp_exp, 1)
                    act.wait_ge(sp_exp, n + 1)
                    nc.scalar.activation(fr1[:, :, PAD:PAD + S], fr2[:, :, :], ACT.Identity,
                                         bias=1.0).then_inc(sp_w, 1)
                    nc.scalar.activation(fr3[:, :, :], fr2[:, :, :], ACT.Ln, bias=1.0).then_inc(sp_ln, 1)
                if q >= BC_AT:
                    for k in range(2):
                        g = 2 * (q - BC_AT) + k
                        use = F_BC + g
                        act.wait_ge(f_full[use % FB], f_count(b, use))
                        nc.scalar.activation(bc_sb[h][:, g, :], ps_f[use % FB][:, :], ACT.Copy).then_inc(bc_ready, 1)

            def decays(st, o, q):
                c = BLK * st.item(o) + q
                act.wait_ge(dt_spread[q % 2], spread(st.item(o), q))
                if q >= 2 or st.has(o - 1):
                    act.wait_ge(scanned, c - 1)
                for g in range(G):
                    nc.scalar.activation(decay[q % 2][:, g, 1:S], dt_rep[q % 2][:, 1:S], ACT.Exp,
                                         scale=nega[:, q, g:g + 1]).then_inc(decay_ready, 1)

            def emit(st):
                if st.has(0) and not st.has(-1):
                    decays(st, 0, 0)
                for q in range(BLK):
                    if q < BLK - 1 and st.has(0):
                        decays(st, 0, q + 1)
                    if q == BLK - 1 and st.has(1) and st.has(0):
                        decays(st, 1, 0)
                    if st.has(1):
                        front(st, q)
                    if st.has(2) and q == 10:
                        b = st.item(2)
                        act.wait_ge(rrms_done, b + 1)
                        act.wait_ge(res_ready, b + 1)
                        for t in range(TT):
                            nc.scalar.activation(xl[:, t, :], xl[:, t, :], ACT.Copy,
                                                 scale=rrms[:, t:t + 1]).then_inc(xh_ready, 1)

            run_steps(act, emit, NB, 2, 1)

        @block.tensor
        def _(pe):
            pe.wait_ge(w_loaded, 16 * 13)
            pe.wait_ge(scaled, 8 + CT * K)

            def take(st, use):
                b = st.item(1)
                if use >= FB:
                    if use - FB >= F_BC:
                        pe.wait_ge(bc_ready, 2 * G * b + use - FB - F_BC + 1)
                    else:
                        pe.wait_ge(f_free[use % FB], f_read(b, use - FB))
                elif st.has(0):
                    pe.wait_ge(bc_ready, 2 * G * b)
                return ps_f[use % FB]

            def project_in(st, use, e):
                f = take(st, use)
                for k in range(KT):
                    ins = nc.tensor.matmul(f[:, :], win[:, k, e * P:(e + 1) * P], hT[:, k, :],
                                           start=(k == 0), stop=(k == KT - 1))
                ins.then_inc(f_full[use % FB], 1)

            def front(st, q):
                h, b = st.half(1), st.item(1)
                if q == 1:
                    pe.wait_ge(xh_ready, TT * (b + 1))
                    for k in range(KT):
                        f = take(st, F_T + k)
                        for t in range(TT):
                            ins = nc.tensor.transpose(f[:, t * P:(t + 1) * P], xl[:, t, k * P:(k + 1) * P],
                                                      id_sb[:, :])
                        ins.then_inc(f_full[k % FB], 1)
                if q == U_AT[0]:
                    for k in range(KT):
                        pe.wait_ge(f_free[k], f_read(b, F_T + k))
                if q in U_AT:
                    c = U_AT.index(q)
                    project_in(st, F_U[c], c)
                if q in V_AT:
                    c = V_AT.index(q)
                    use = F_V[c]
                    f = take(st, use)
                    pe.wait_ge(f_free[F_U[c] % FB], f_read(b, F_U[c]))
                    for k in range(K):
                        ins = nc.tensor.matmul(f[:, :], tap[:, c, k, :], fr1[:, c % 2, k:k + S],
                                               start=(k == 0), stop=(k == K - 1))
                    ins.then_inc(f_full[use % FB], 1)
                for c in range(CT):
                    if Z_AT[c] == q:
                        project_in(st, F_Z[c], CT + c)
                if q == X_AT:
                    f = take(st, F_X)
                    pe.wait_ge(u_ready, CT * (b + 1))
                    for c in range(CT):
                        ins = nc.tensor.matmul(f[0:RX, :], wx[:, c, :], u_sb[h][:, c, :],
                                               start=(c == 0), stop=(c == CT - 1))
                    ins.then_inc(f_full[F_X % FB], 1)
                if DT_AT <= q < DT_AT + 2:
                    for c in (2 * (q - DT_AT), 2 * (q - DT_AT) + 1):
                        use = F_DT + c
                        f = take(st, use)
                        pe.wait_ge(f_free[F_X % FB], f_read(b, F_X))
                        nc.tensor.matmul(f[:, :], wdt[:, c * P:(c + 1) * P], xd[:, :], start=True,
                                         stop=True).then_inc(f_full[use % FB], 1)
                if q >= BC_AT:
                    for k in range(2):
                        g = 2 * (q - BC_AT) + k
                        use = F_BC + g
                        f = take(st, use)
                        nc.tensor.matmul(f[:, :], pick_s[:, g, :], xd[:, :], start=True,
                                         stop=True).then_inc(f_full[use % FB], 1)

            def sum_pair(st, o, q):
                b = st.item(o)
                tile = q // BPT
                if q % BPT == 0:
                    if tile >= 2:
                        pe.wait_ge(y_read, CT * b + tile - 1)
                    elif st.has(o - 1):
                        pe.wait_ge(y_read, CT * b + tile - 1)
                pe.wait_ge(weighed, BLK * b + q + 2)
                for g in range(G):
                    for k in range(2):
                        p0 = CH * ((q + k) % BPT)
                        ins = nc.tensor.matmul(ps_y[tile % 2][p0:p0 + CH, :], sum_q[:, :],
                                               state[(q + k) % RING][:, g, :], start=(g == 0), stop=(g == G - 1),
                                               skip_group_check=True)
                ins.then_inc(summed, 1)

            def project(st, v):
                h, b = st.half(-1), st.item(-1)
                pe.wait_ge(gated, CT * (b + 1))
                if st.has(-2):
                    pe.wait_ge(o_read, 2 * b + v - 1)
                for u in range(2):
                    t = 2 * v + u
                    for c in range(CT):
                        ins = nc.tensor.matmul(ps_o[v][:, u * D:(u + 1) * D], u_sb[h][:, c, t * P:(t + 1) * P],
                                               wout[:, c, :], start=(c == 0), stop=(c == CT - 1))
                ins.then_inc(o_full, 1)

            def emit(st):
                for q in range(BLK):
                    if q % 2 and q >= RING - 1 and st.has(0):
                        sum_pair(st, 0, q - (RING - 1))
                    if q % 2 and q < RING - 1 and st.has(-1):
                        sum_pair(st, -1, BLK + q - (RING - 1))
                    if q in (4, 5) and st.has(-1):
                        project(st, q - 4)
                    if st.has(1):
                        front(st, q)

            run_steps(pe, emit, NB, 2, 1)


def _transposed(a):
    return np.swapaxes(a, -1, -2)


def _columns(v):
    return v.reshape(-1, P).T


def kernel(**inputs):
    import concourse.bacc as _bacc
    from concourse.bass_utils import run_bass_kernel_spmd as _run

    x = inputs["L0_attn_a_x"]
    NB, S, D = x.shape
    a = {k[len("L0_attn_a_"):]: v for k, v in inputs.items() if k.startswith("L0_attn_a_")}
    m = {k[len("L0_attn_b_"):]: v for k, v in inputs.items() if k.startswith("L0_attn_b_")}
    f = {k[len("L0_ffn_"):]: v for k, v in inputs.items() if k.startswith("L0_ffn_")}
    wave = np.arange(1, D + 1, dtype=np.float32) * np.float32(2.0 * math.pi / D)
    inv = (np.float32(1.0) / (wave + np.float32(1e-8))).astype(np.float32)
    DI, N = m["A_log"].shape
    R, CH, E = m["dt_proj_w"].shape[0], 32, 8
    Q = P // CH
    G = N // Q
    part = np.arange(P)
    state_row = R + Q * np.arange(2 * G)[:, None] + (part % Q)[None, :]
    pick_bc = np.arange(R + 2 * N)[:, None, None] == state_row[None, :, :]
    sum_n = (part // Q)[:, None] == np.arange(CH)[None, :]
    lay = {
        "x": x,
        "wqkT": np.concatenate([_transposed(a["Wq"]), _transposed(a["Wk"])], axis=1),
        "wvT": _transposed(a["Wv"]),
        "bqk": np.concatenate([_columns(a["bq"]), _columns(a["bk"])], axis=1),
        "bv": a["bv"].reshape(1, D),
        "phase": np.concatenate([_columns(a["phase_bias"])] * 2, axis=1),
        "inv_wl": np.concatenate([_columns(inv)] * 2, axis=1),
        "ident": np.eye(P, dtype=np.float32),
        "experts": np.tile(np.arange(E, dtype=np.float32), (P, 1)),
        "weights": f["expert_weights"],
        "indices": f["expert_indices"],
        "w1aT": _transposed(f["w1_A"]),
        "w1b": f["w1_B"],
        "w2aT": _transposed(f["w2_A"]),
        "w2b": f["w2_B"],
        "w_in": m["in_proj_w"],
        "conv_w": m["conv_w"].reshape(-1, P, m["conv_w"].shape[1]).transpose(1, 0, 2),
        "conv_b": _columns(m["conv_b"]),
        "norm_w": _columns(m["norm_w"]),
        "w_x": m["x_proj_w"],
        "w_dt": m["dt_proj_w"],
        "b_dt": _columns(m["dt_proj_b"]),
        "a_log": m["A_log"].reshape(DI // CH, CH, G, Q).transpose(1, 3, 0, 2).reshape(P, DI // CH, G),
        "d_skip": _columns(m["D"]),
        "w_out": m["out_proj_w"],
        "pick_bc": pick_bc.astype(np.float32),
        "sum_n": sum_n.astype(np.float32),
    }
    nc = _bacc.Bacc("TRN2", target_bir_lowering=False, num_devices=1)
    arrays, ap = {}, {}
    for name, v in lay.items():
        arrays[name] = np.ascontiguousarray(v)
        ap[name] = nc.dram_tensor(name, v.shape, mybir.dt.from_np(v.dtype), kind="ExternalInput").ap()
    out = nc.dram_tensor("out", x.shape, F32, kind="ExternalOutput").ap()
    x1 = nc.dram_tensor("x1", x.shape, F32, kind="Internal").ap()
    ffn_args = [ap[n] for n in ("weights", "indices", "experts", "w1aT", "w1b", "w2aT", "w2b", "ident")]
    attention(nc, ap["x"], ap["wqkT"], ap["wvT"], ap["bqk"], ap["bv"], ap["phase"], ap["inv_wl"], ap["ident"], x1)
    expert_ffn(nc, "f1_", x1, *ffn_args)
    mamba(nc, x1, out, *(ap[n] for n in (
        "w_in", "conv_w", "conv_b", "norm_w", "w_x", "w_dt", "b_dt", "a_log", "d_skip", "w_out",
        "pick_bc", "sum_n", "ident")))
    expert_ffn(nc, "f2_", out, *ffn_args)
    r = _run(nc, [arrays], core_ids=[0])
    return r.results[0]["out"]
```
